# Optimizing a Trainium2 kernel written in Bass

```python
import numpy as np
import jax
import jax.numpy as jnp

def _softmax(x, axis=-1):
    return jax.nn.softmax(x, axis=axis)

def _gelu(x):
    return jax.nn.gelu(x, approximate=True)

def _silu(x):
    return jax.nn.silu(x)

def _sigmoid(x):
    return jax.nn.sigmoid(x)

def _layernorm(x, axis=-1, eps=1e-05):
    m = jnp.mean(x, axis=axis, keepdims=True)
    v = jnp.var(x, axis=axis, keepdims=True)
    return (x - m) / jnp.sqrt(v + eps)

def _scatter_add(tgt, idx, src, axis=0):
    return tgt.at[idx].add(src)

def _segment_sum(src, seg, n):
    return jax.ops.segment_sum(src, seg, n)
kernel_name = 'mk_decoder_postln_d1_seqx_r4_8bd3c4'

def setup_inputs(seed: int=0):
    np.random.seed(seed)
    _w = jnp.asarray

    def _rec_inputs():
        import jax
        import jax.numpy as jnp
        _rk = jax.random.key(seed)
        x = -0.000125 + 0.9999 * jax.random.normal(jax.random.fold_in(_rk, 1), (4, 512, 512), jnp.float32)
        _lenS = 512 - jax.random.randint(jax.random.fold_in(_rk, 7), (4,), 0, max(1, 512 // 4) + 1, jnp.int32)
        _lenS2 = 512 - jax.random.randint(jax.random.fold_in(_rk, 8), (4,), 0, max(1, 512 // 4) + 1, jnp.int32)
        fside_BxS2xS2_0 = -3.05549e-07 + 0.0199987 * jax.random.normal(jax.random.fold_in(_rk, 11), (4, 512, 512), jnp.float32)
        _ctx_1024P = jax.random.normal(jax.random.fold_in(_rk, 12), (4, 16, 256), jnp.float32)
        _ctx_1024c = jax.random.dirichlet(jax.random.fold_in(_rk, 512), 0.3 * jnp.ones((16,), jnp.float32), (4, 512))
        _ctx_1024t = jnp.einsum('bsk,bkd->bsd', _ctx_1024c, _ctx_1024P)
        _ctx_1024t = _ctx_1024t * jax.lax.rsqrt(jnp.mean(jnp.square(_ctx_1024t)) + 1e-12) * 0.953939
        ctx_1024 = 6.82029e-06 + 0.0200006 * (_ctx_1024t + 0.3 * jax.random.normal(jax.random.fold_in(_rk, 612), (4, 512, 256), jnp.float32))
        return (x, fside_BxS2xS2_0, ctx_1024)
    x, fside_BxS2xS2_0, ctx_1024 = _rec_inputs()

    def _L0_attn_setup():
        import jax, jax.numpy as jnp
        import numpy as np
        EPS = 1e-06
        H, NOPE, ROPE, VD = (16, 128, 64, 128)
        QHD = NOPE + ROPE
        SCALE = QHD ** (-0.5)
        THETA = 10000.0

        def rmsnorm(x, w):
            x32 = x.astype(jnp.float32)
            var = jnp.mean(x32 * x32, axis=-1, keepdims=True)
            return (w * (x32 * jax.lax.rsqrt(var + EPS))).astype(x.dtype)

        def rope_cos_sin(seq_len):
            inv_freq = 1.0 / THETA ** (jnp.arange(0, ROPE, 2, dtype=jnp.float32) / ROPE)
            t = jnp.arange(seq_len, dtype=jnp.float32)
            freqs = jnp.outer(t, inv_freq)
            emb = jnp.concatenate([freqs, freqs], -1)
            return (jnp.cos(emb), jnp.sin(emb))

        def rotate_half(x):
            x1, x2 = (x[..., :x.shape[-1] // 2], x[..., x.shape[-1] // 2:])
            return jnp.concatenate([-x2, x1], axis=-1)
        key = jax.random.key(seed)
        ks = jax.random.split(key, 6)
        B, S, D = (2, 512, 512)
        return {'hidden_states': jax.random.normal(ks[0], (B, S, D), jnp.float32), 'q_a_w': jax.random.normal(ks[1], (384, D), jnp.float32) * 0.02, 'q_a_ln_w': jnp.ones((384,), jnp.float32), 'q_b_w': jax.random.normal(ks[2], (H * QHD, 384), jnp.float32) * 0.02, 'kv_a_w': jax.random.normal(ks[3], (128 + ROPE, D), jnp.float32) * 0.02, 'kv_a_ln_w': jnp.ones((128,), jnp.float32), 'kv_b_w': jax.random.normal(ks[4], (H * (NOPE + VD), 128), jnp.float32) * 0.02, 'o_w': jax.random.normal(ks[5], (D, H * VD), jnp.float32) * 0.02}
    _L0_attn_all = _L0_attn_setup()
    _L0_attn_in = {k: v for k, v in _L0_attn_all.items() if k in ('q_a_w', 'q_a_ln_w', 'q_b_w', 'kv_a_w', 'kv_a_ln_w', 'kv_b_w', 'o_w')}
    del _L0_attn_all

    def _L0_xattn_setup():
        import jax, jax.numpy as jnp
        import numpy as np
        EPS = 1e-06
        QMAX = 127.0

        def _smooth_quant_linear(x, w):
            amax_x = jnp.max(jnp.abs(x), axis=0)
            amax_w = jnp.max(jnp.abs(w), axis=0)
            s = jnp.sqrt(jnp.maximum(amax_x, EPS) / jnp.maximum(amax_w, EPS))
            s = jnp.maximum(s, EPS)
            xs = x / s
            ws = w * s
            x_scale = jnp.maximum(jnp.max(jnp.abs(xs), axis=-1, keepdims=True), EPS) / QMAX
            w_scale = jnp.maximum(jnp.max(jnp.abs(ws), axis=-1, keepdims=True), EPS) / QMAX
            x_q = jnp.clip(jnp.round(xs / x_scale), -QMAX, QMAX)
            w_q = jnp.clip(jnp.round(ws / w_scale), -QMAX, QMAX)
            return x_q @ w_q.T * x_scale * w_scale.T

        def _expert_forward(xe, guw, dw):
            h = _smooth_quant_linear(xe, guw)
            gate, up = jnp.split(h, 2, axis=-1)
            a = jax.nn.silu(gate) * up
            return _smooth_quant_linear(a, dw)
        key = jax.random.key(seed)
        k1, k2, k3 = jax.random.split(key, 3)
        E, T, D, I = (8, 512, 512, 256)
        x = jax.random.normal(k1, (E, T, D), dtype=jnp.float32)
        gate_up_weight = jax.random.normal(k2, (E, 2 * I, D), dtype=jnp.float32) * 0.02
        down_weight = jax.random.normal(k3, (E, D, I), dtype=jnp.float32) * 0.02
        return {'x': x, 'gate_up_weight': gate_up_weight, 'down_weight': down_weight}
    _L0_xattn_all = _L0_xattn_setup()
    _L0_xattn_in = {k: v for k, v in _L0_xattn_all.items() if k in ()}
    del _L0_xattn_all

    def _L0_ffn_setup():
        import jax, jax.numpy as jnp
        import numpy as np
        GOLDEN_CENTER = 1.0 / np.e
        GOLDEN_LOWER = 0.5 - np.log(4.0 / 3.0)
        GOLDEN_UPPER = 0.5

        def _golden_weights(x, Wr, temperature):
            inh = jax.nn.sigmoid(x @ Wr / temperature)
            in_zone = (inh >= GOLDEN_LOWER) & (inh <= GOLDEN_UPPER)
            distance = jnp.abs(inh - GOLDEN_CENTER)
            weights = jnp.exp(-distance / 0.1) * in_zone.astype(x.dtype)
            wsum = jnp.sum(weights, axis=-1, keepdims=True)
            no_expert = wsum < 1e-08
            fb = jnp.exp(-distance / 0.3)
            _, top2 = jax.lax.top_k(fb, 2)
            fb_mask = jnp.sum(jax.nn.one_hot(top2, weights.shape[-1], dtype=x.dtype), axis=-2)
            fb_w = fb * fb_mask
            fb_w = fb_w / jnp.maximum(jnp.sum(fb_w, axis=-1, keepdims=True), 1e-08)
            weights = jnp.where(no_expert, fb_w, weights)
            weights = weights / jnp.maximum(jnp.sum(weights, axis=-1, keepdims=True), 1e-08)
            return weights
        key = jax.random.key(seed)
        ks = jax.random.split(key, 5)
        B, T, D, E, F = (2, 512, 512, 8, 512)
        s_in = 1.0 / np.sqrt(D)
        s_f = 1.0 / np.sqrt(F)
        return {'x': jax.random.normal(ks[0], (B, T, D), dtype=jnp.float32), 'Wg': jax.random.normal(ks[1], (E, D, F), dtype=jnp.float32) * s_in, 'Wu': jax.random.normal(ks[2], (E, D, F), dtype=jnp.float32) * s_in, 'Wd': jax.random.normal(ks[3], (E, F, D), dtype=jnp.float32) * s_f, 'Wr': jax.random.normal(ks[4], (D, E), dtype=jnp.float32) * s_in, 'temperature': jnp.ones((1,), dtype=jnp.float32)}
    _L0_ffn_all = _L0_ffn_setup()
    _L0_ffn_in = {k: v for k, v in _L0_ffn_all.items() if k in ('Wg', 'Wu', 'Wd', 'Wr', 'temperature')}
    del _L0_ffn_all
    return {'x': x, 'fside_BxS2xS2_0': fside_BxS2xS2_0, 'ctx_1024': ctx_1024, 'L0_attn_q_a_w': _L0_attn_in['q_a_w'], 'L0_attn_q_a_ln_w': _L0_attn_in['q_a_ln_w'], 'L0_attn_q_b_w': _L0_attn_in['q_b_w'], 'L0_attn_kv_a_w': _L0_attn_in['kv_a_w'], 'L0_attn_kv_a_ln_w': _L0_attn_in['kv_a_ln_w'], 'L0_attn_kv_b_w': _L0_attn_in['kv_b_w'], 'L0_attn_o_w': _L0_attn_in['o_w'], 'L0_ffn_Wg': _L0_ffn_in['Wg'], 'L0_ffn_Wu': _L0_ffn_in['Wu'], 'L0_ffn_Wd': _L0_ffn_in['Wd'], 'L0_ffn_Wr': _L0_ffn_in['Wr'], 'L0_ffn_temperature': _L0_ffn_in['temperature']}

def reference(x, fside_BxS2xS2_0, ctx_1024, L0_attn_q_a_w, L0_attn_q_a_ln_w, L0_attn_q_b_w, L0_attn_kv_a_w, L0_attn_kv_a_ln_w, L0_attn_kv_b_w, L0_attn_o_w, L0_ffn_Wg, L0_ffn_Wu, L0_ffn_Wd, L0_ffn_Wr, L0_ffn_temperature):
    import jax
    import jax.numpy as jnp

    def _L0_attn_ref(hidden_states, q_a_w, q_a_ln_w, q_b_w, kv_a_w, kv_a_ln_w, kv_b_w, o_w):
        import jax, jax.numpy as jnp
        import numpy as np
        EPS = 1e-06
        H, NOPE, ROPE, VD = (16, 128, 64, 128)
        QHD = NOPE + ROPE
        SCALE = QHD ** (-0.5)
        THETA = 10000.0

        def rmsnorm(x, w):
            x32 = x.astype(jnp.float32)
            var = jnp.mean(x32 * x32, axis=-1, keepdims=True)
            return (w * (x32 * jax.lax.rsqrt(var + EPS))).astype(x.dtype)

        def rope_cos_sin(seq_len):
            inv_freq = 1.0 / THETA ** (jnp.arange(0, ROPE, 2, dtype=jnp.float32) / ROPE)
            t = jnp.arange(seq_len, dtype=jnp.float32)
            freqs = jnp.outer(t, inv_freq)
            emb = jnp.concatenate([freqs, freqs], -1)
            return (jnp.cos(emb), jnp.sin(emb))

        def rotate_half(x):
            x1, x2 = (x[..., :x.shape[-1] // 2], x[..., x.shape[-1] // 2:])
            return jnp.concatenate([-x2, x1], axis=-1)
        B, S, D = hidden_states.shape
        q_a = hidden_states @ q_a_w.T
        q = rmsnorm(q_a, q_a_ln_w) @ q_b_w.T
        q = q.reshape(B, S, H, QHD).transpose(0, 2, 1, 3)
        q_nope, q_pe = (q[..., :NOPE], q[..., NOPE:])
        ckv_full = hidden_states @ kv_a_w.T
        ckv, k_pe_raw = (ckv_full[..., :128], ckv_full[..., 128:])
        kv = rmsnorm(ckv, kv_a_ln_w) @ kv_b_w.T
        kv = kv.reshape(B, S, H, NOPE + VD).transpose(0, 2, 1, 3)
        k_nope, v = (kv[..., :NOPE], kv[..., NOPE:])
        k_pe = k_pe_raw.reshape(B, 1, S, ROPE)
        cos, sin = rope_cos_sin(S)
        cos, sin = (cos[None, None], sin[None, None])
        q_pe = q_pe * cos + rotate_half(q_pe) * sin
        k_pe = k_pe * cos + rotate_half(k_pe) * sin
        query = jnp.concatenate([q_nope, q_pe], -1)
        key_s = jnp.concatenate([k_nope, jnp.broadcast_to(k_pe, (B, H, S, ROPE))], -1)
        scores = jnp.einsum('bhqd,bhkd->bhqk', query, key_s) * SCALE
        causal = jnp.tril(jnp.ones((S, S), bool))
        scores = jnp.where(causal[None, None], scores, -jnp.inf)
        probs = jax.nn.softmax(scores.astype(jnp.float32), axis=-1).astype(query.dtype)
        attn = jnp.einsum('bhqk,bhkd->bhqd', probs, v)
        attn = attn.transpose(0, 2, 1, 3).reshape(B, S, H * VD)
        return attn @ o_w.T

    def _L0_xattn_ref(x, gate_up_weight, down_weight):
        import jax, jax.numpy as jnp
        import numpy as np
        EPS = 1e-06
        QMAX = 127.0

        def _smooth_quant_linear(x, w):
            amax_x = jnp.max(jnp.abs(x), axis=0)
            amax_w = jnp.max(jnp.abs(w), axis=0)
            s = jnp.sqrt(jnp.maximum(amax_x, EPS) / jnp.maximum(amax_w, EPS))
            s = jnp.maximum(s, EPS)
            xs = x / s
            ws = w * s
            x_scale = jnp.maximum(jnp.max(jnp.abs(xs), axis=-1, keepdims=True), EPS) / QMAX
            w_scale = jnp.maximum(jnp.max(jnp.abs(ws), axis=-1, keepdims=True), EPS) / QMAX
            x_q = jnp.clip(jnp.round(xs / x_scale), -QMAX, QMAX)
            w_q = jnp.clip(jnp.round(ws / w_scale), -QMAX, QMAX)
            return x_q @ w_q.T * x_scale * w_scale.T

        def _expert_forward(xe, guw, dw):
            h = _smooth_quant_linear(xe, guw)
            gate, up = jnp.split(h, 2, axis=-1)
            a = jax.nn.silu(gate) * up
            return _smooth_quant_linear(a, dw)
        return jax.vmap(_expert_forward)(x, gate_up_weight, down_weight)

    def _L0_ffn_ref(x, Wg, Wu, Wd, Wr, temperature):
        import jax, jax.numpy as jnp
        import numpy as np
        GOLDEN_CENTER = 1.0 / np.e
        GOLDEN_LOWER = 0.5 - np.log(4.0 / 3.0)
        GOLDEN_UPPER = 0.5

        def _golden_weights(x, Wr, temperature):
            inh = jax.nn.sigmoid(x @ Wr / temperature)
            in_zone = (inh >= GOLDEN_LOWER) & (inh <= GOLDEN_UPPER)
            distance = jnp.abs(inh - GOLDEN_CENTER)
            weights = jnp.exp(-distance / 0.1) * in_zone.astype(x.dtype)
            wsum = jnp.sum(weights, axis=-1, keepdims=True)
            no_expert = wsum < 1e-08
            fb = jnp.exp(-distance / 0.3)
            _, top2 = jax.lax.top_k(fb, 2)
            fb_mask = jnp.sum(jax.nn.one_hot(top2, weights.shape[-1], dtype=x.dtype), axis=-2)
            fb_w = fb * fb_mask
            fb_w = fb_w / jnp.maximum(jnp.sum(fb_w, axis=-1, keepdims=True), 1e-08)
            weights = jnp.where(no_expert, fb_w, weights)
            weights = weights / jnp.maximum(jnp.sum(weights, axis=-1, keepdims=True), 1e-08)
            return weights
        weights = _golden_weights(x, Wr, temperature)
        gate = jnp.einsum('btd,edf->betf', x, Wg)
        up = jnp.einsum('btd,edf->betf', x, Wu)
        h = jax.nn.silu(gate) * up
        e_out = jnp.einsum('betf,efd->betd', h, Wd)
        out = jnp.einsum('bte,betd->btd', weights, e_out)
        return out
    x = _layernorm(x + _L0_attn_ref(x, L0_attn_q_a_w, L0_attn_q_a_ln_w, L0_attn_q_b_w, L0_attn_kv_a_w, L0_attn_kv_a_ln_w, L0_attn_kv_b_w, L0_attn_o_w), axis=-1)
    x = _layernorm(x + _L0_xattn_ref(x, fside_BxS2xS2_0, ctx_1024), axis=-1)
    x = _layernorm(x + _L0_ffn_ref(x, L0_ffn_Wg, L0_ffn_Wu, L0_ffn_Wd, L0_ffn_Wr, L0_ffn_temperature), axis=-1)
    return x

_drawn_inputs = setup_inputs


def setup_inputs(seed=0):
    import zlib

    import numpy as np

    out = dict(_drawn_inputs(seed))
    spreads = {'L0_attn_q_a_ln_w': (1.0, 0.6), 'L0_attn_kv_a_ln_w': (1.0, 0.6)}
    factors = {'L0_attn_q_a_w': 4.052, 'L0_attn_q_b_w': 3.88}
    for name, (base, spread) in spreads.items():
        noise = np.random.default_rng([zlib.crc32(name.encode()), seed]).standard_normal(out[name].shape)
        drawn = base * np.exp(spread * noise) if base else spread * noise
        out[name] = jnp.asarray(drawn.astype(out[name].dtype))
    for name, factor in factors.items():
        out[name] = (out[name] * factor).astype(out[name].dtype)
    return out
```

```python
from contextlib import ExitStack

import numpy as np

import concourse.bass as bass
from concourse import mybir

F32 = mybir.dt.float32
F32R = mybir.dt.float32r
BF16 = mybir.dt.bfloat16
ALU = mybir.AluOpType
ACT = mybir.ActivationFunctionType
AX_X = mybir.AxisListType.X

P = 128
B, S, D = 4, 512, 512
H, NOPE, ROPE, VD = 16, 128, 64, 128
QL, KL = 384, 128
QB = S // P
NT = B * QB
KD = D // P
KQ = QL // P
NP = H // 2
E, FF = 8, 512
KF = FF // P
INNER = 256
RMS_EPS, LN_EPS, Q_EPS, QMAX = 1e-6, 1e-5, 1e-6, 127.0
SCALE = float(NOPE + ROPE) ** -0.5
MASKED = -1e30
ROUND = 1.5 * 2.0 ** 23
SWAP = [(i + 16) % 32 for i in range(32)]
SEEN = [(q + 1) * P for q in range(QB)]


def past(engine, semaphore, count):
    if not (isinstance(count, int) and count == 0):
        engine.wait_ge(semaphore, count)


class Chain:

    def __init__(self, engine, semaphore, base=0):
        self.engine, self.semaphore, self.base, self.n = engine, semaphore, base, 0

    def link(self, instruction):
        self.n += 1
        instruction.then_inc(self.semaphore, 1)
        self.engine.wait_ge(self.semaphore, self.base + self.n)


class Space:

    def __init__(self, nc, stack):
        self.nc, self.stack = nc, stack

    def sb(self, name, shape, dtype=F32):
        return self.stack.enter_context(self.nc.sbuf_tensor(name, shape, dtype))

    def psum(self, name, shape, dtype=F32):
        return self.stack.enter_context(self.nc.psum_tensor(name, shape, dtype))

    def sem(self, name):
        return self.stack.enter_context(self.nc.semaphore(name))

    def banks(self, name, n):
        return [self.psum(f"{name}{i}", [P, 512]) for i in range(n)]


def split_matmul(nc, out, w_hi, w_lo, x_hi, x_lo, start, stop):
    nc.tensor.matmul(out, w_hi, x_hi, start=start, stop=False)
    nc.tensor.matmul(out, w_hi, x_lo, start=False, stop=False)
    return nc.tensor.matmul(out, w_lo, x_hi, start=False, stop=stop)


def latent_phase(nc, g, io):
    with ExitStack() as stack:
        m = Space(nc, stack)
        mask_in = m.sb("mask_in", [P, P])
        x_t = m.sb("x_t", [P, KD, S])
        x_hi = m.sb("x_hi", [P, KD, S], F32R)
        x_lo = m.sb("x_lo", [P, KD, S], F32R)
        wa = m.sb("wa", [P, KD, QL + KL])
        wa_hi = m.sb("wa_hi", [P, KD, QL + KL], F32R)
        wa_lo = m.sb("wa_lo", [P, KD, QL + KL], F32R)
        wr = m.sb("wkr", [P, KD, P])
        wr_hi = m.sb("wkr_hi", [P, KD, P], F32R)
        wr_lo = m.sb("wkr_lo", [P, KD, P], F32R)
        junk = m.sb("square_junk", [P, QB, QL + KL], BF16)
        latent = m.sb("latent", [P, QB, QL + KL])
        ssq = m.sb("ssq", [P, QB, 2])
        ms = m.sb("ms", [P, QB, 2])
        rms = m.sb("rms", [P, QB, 2])
        rstd = m.sb("rstd", [P, QB, 2])
        nt = m.sb("newton", [P, QB, 2])
        kv_gain = m.sb("kv_gain", [P, KL])
        rot = m.sb("krot", [P, S])
        rot_swapped = m.sb("krot_swapped", [P, S])
        product = m.banks("latent_bank", QB)
        rotary = m.psum("rotary_bank", [P, 512])
        turned = m.banks("turned_bank", 3)

        weights_in = m.sem("weights_in")
        consts_in = m.sem("consts_in")
        x_in = m.sem("x_in")
        w_split = m.sem("w_split")
        x_split_hi = m.sem("x_split_hi")
        x_split = m.sem("x_split")
        lat_mm = m.sem("lat_mm")
        rot_mm = m.sem("rot_mm")
        squared = m.sem("squared")
        mean_ready = m.sem("mean_ready")
        root_ready = m.sem("root_ready")
        normed = m.sem("normed")
        turn_mm = m.sem("turn_mm")
        turn_hi = m.sem("turn_hi")
        turn_lo = m.sem("turn_lo")
        values_done = m.sem("values_done")
        rot_read = m.sem("rot_read")
        rot_ready = m.sem("rot_ready")
        rot_hi_ready = m.sem("rot_hi_ready")
        rot_split = m.sem("rot_split")
        pool_step = m.sem("lat_pool_step")
        dve_step = m.sem("lat_dve_step")
        block = stack.enter_context(nc.Block())

        @block.sync
        def _(sp):
            sp.dma_start(wa[:], io["w_a"].rearrange("(k p) n -> p k n", p=P)).then_inc(weights_in, 16)
            sp.dma_start(wr[:], io["w_kr"].rearrange("(k p) n -> p k n", p=P)).then_inc(weights_in, 16)
            xt_view = io["x_t"].rearrange("b (k p) n -> b p k n", p=P)
            sp.dma_start(x_t[:], xt_view[0]).then_inc(x_in, 16)
            for dst, name in ((g.ident, "ident"), (mask_in, "mask"), (g.cos, "cos"), (g.sin, "sin"), (g.ones, "ones")):
                sp.dma_start(dst[:], io[name]).then_inc(consts_in, 16)
            sp.dma_start(kv_gain[:], io["kv_ln"].partition_broadcast(P)).then_inc(consts_in, 16)
            sp.dma_start(g.q_gain[:], io["q_ln"]).then_inc(consts_in, 16)
            sp.dma_start(g.res[:], io["x"].rearrange("b (t p) n -> p (b t) n", p=P)).then_inc(consts_in, 16)
            with sp.Fori(1, B) as b:
                sp.wait_ge(x_split, b)
                sp.dma_start(x_t[:], xt_view[bass.ts(b, 1)].rearrange("b p k n -> (b p) k n")).then_inc(x_in, 16)
            sp.wait_ge(consts_in, 8 * 16)

        @block.scalar
        def _(act):
            act.wait_ge(weights_in, 32)
            nc.scalar.activation(wa_hi[:], wa[:], ACT.Copy).then_inc(w_split, 1)
            nc.scalar.activation(wr_hi[:], wr[:], ACT.Copy).then_inc(w_split, 1)
            with act.Fori(0, B) as b:
                act.wait_ge(x_in, (b + 1) * 16)
                nc.scalar.activation(x_hi[:], x_t[:], ACT.Copy).then_inc(x_split_hi, 1)
                for t in range(QB):
                    act.wait_ge(lat_mm, QB * b + t + 1)
                    nc.scalar.activation(junk[:, t, 0:QL], product[t][:, 0:QL], ACT.Square,
                                         accum_out=ssq[:, t, 0:1])
                    nc.scalar.activation(junk[:, t, QL:], product[t][:, QL:QL + KL], ACT.Square,
                                         accum_out=ssq[:, t, 1:2]).then_inc(squared, 1)
                act.wait_ge(mean_ready, b + 1)
                nc.scalar.activation(rms[:], ms[:], ACT.Sqrt).then_inc(root_ready, 1)
                for c in range(KQ + 1):
                    act.wait_ge(turn_mm, (KQ + 1) * b + c + 1)
                    bank = turned[c % 3]
                    dst = g.qn_hi[:, c, bass.ts(b, S)] if c < KQ else g.key_hi[:, bass.ts(b, S)]
                    nc.scalar.activation(dst, bank[:], ACT.Copy).then_inc(turn_hi, 1)
                act.wait_ge(rot_ready, b + 1)
                nc.scalar.activation(g.kr_hi[:, bass.ts(b, S)], rot[:], ACT.Copy).then_inc(rot_hi_ready, 1)

        @block.vector
        def _(dve):
            start = Chain(dve, dve_step)
            dve.wait_ge(w_split, 2)
            nc.vector.tensor_tensor(wa_lo[:], wa[:], wa_hi[:].bitcast(F32), ALU.subtract).then_inc(w_split, 1)
            nc.vector.tensor_tensor(wr_lo[:], wr[:], wr_hi[:].bitcast(F32), ALU.subtract).then_inc(w_split, 1)
            dve.wait_ge(consts_in, 8 * 16)
            nc.vector.tensor_copy(g.ident_b[:], g.ident[:])
            nc.vector.tensor_copy(g.mask[:], mask_in[:])
            start.link(nc.vector.tensor_scalar(g.q_gain[:], g.q_gain[:], SCALE, None, ALU.mult))
            STEPS = 7
            with dve.Fori(0, B) as b:
                chain = Chain(dve, dve_step, b * STEPS + 1)
                dve.wait_ge(x_split_hi, b + 1)
                nc.vector.tensor_tensor(x_lo[:], x_t[:], x_hi[:].bitcast(F32), ALU.subtract).then_inc(x_split, 1)
                dve.wait_ge(squared, QB * (b + 1))
                nc.vector.tensor_scalar(ms[:, :, 0], ssq[:, :, 0], 1.0 / QL, RMS_EPS, ALU.mult, ALU.add)
                chain.link(nc.vector.tensor_scalar(ms[:, :, 1], ssq[:, :, 1], 1.0 / KL, RMS_EPS, ALU.mult, ALU.add))
                chain.link(nc.vector.tensor_copy(nt[:], ms[:]))
                dve.sem_inc(mean_ready, 1)
                dve.wait_ge(root_ready, b + 1)
                chain.link(nc.vector.reciprocal(rstd[:], rms[:]))
                chain.link(nc.vector.tensor_tensor(nt[:], nt[:], rstd[:], ALU.mult))
                chain.link(nc.vector.tensor_tensor(nt[:], nt[:], rstd[:], ALU.mult))
                chain.link(nc.vector.tensor_scalar(nt[:], nt[:], -0.5, 1.5, ALU.mult, ALU.add))
                chain.link(nc.vector.tensor_tensor(rstd[:], rstd[:], nt[:], ALU.mult))
                assert chain.n == STEPS
                for t in range(QB):
                    nc.vector.tensor_scalar(latent[:, t, 0:QL], product[t][:, 0:QL], rstd[:, t, 0:1],
                                            None, ALU.mult)
                    nc.vector.scalar_tensor_tensor(latent[:, t, QL:], product[t][:, QL:], rstd[:, t, 1:2],
                                                   kv_gain[:], ALU.mult, ALU.mult).then_inc(normed, 1)
                dve.wait_ge(normed, QB * (b + 1))
                value = latent[:, :, QL:]
                nc.vector.tensor_copy(g.val_hi[:, bass.ts(b, QB), :], value).then_inc(values_done, 1)
                dve.wait_ge(values_done, 2 * b + 1)
                nc.vector.tensor_tensor(g.val_lo[:, bass.ts(b, QB), :], value,
                                        g.val_hi[:, bass.ts(b, QB), :].bitcast(F32),
                                        ALU.subtract).then_inc(values_done, 1)
                dve.wait_ge(rot_mm, b + 1)
                nc.vector.tensor_tensor(rot[:], rotary[:], g.cos[:], ALU.mult)
                nc.vector.stream_shuffle(rot_swapped[:], rotary[:], SWAP).then_inc(rot_read, 1)
                for c in range(KQ + 1):
                    dve.wait_ge(turn_hi, (KQ + 1) * b + c + 1)
                    bank = turned[c % 3]
                    hi, lo = ((x[:, c, bass.ts(b, S)] for x in (g.qn_hi, g.qn_lo)) if c < KQ
                              else (x[:, bass.ts(b, S)] for x in (g.key_hi, g.key_lo)))
                    nc.vector.tensor_tensor(lo, bank[:], hi.bitcast(F32), ALU.subtract).then_inc(turn_lo, 1)
                dve.wait_ge(rot_hi_ready, b + 1)
                nc.vector.tensor_tensor(g.kr_lo[:, bass.ts(b, S)], rot[:], g.kr_hi[:, bass.ts(b, S)].bitcast(F32),
                                        ALU.subtract).then_inc(rot_split, 1)
                dve.wait_ge(rot_split, b + 1)

        @block.gpsimd
        def _(pool):
            pool.wait_ge(consts_in, 8 * 16)
            with pool.Fori(0, B) as b:
                pool.wait_ge(rot_read, b + 1)
                nc.gpsimd.tensor_tensor(rot_swapped[:], rot_swapped[:], g.sin[:], ALU.mult).then_inc(pool_step, 1)
                pool.wait_ge(pool_step, b + 1)
                nc.gpsimd.tensor_tensor(rot[:], rot[:], rot_swapped[:], ALU.add).then_inc(rot_ready, 1)

        @block.tensor
        def _(pe):
            pe.wait_ge(w_split, 4)
            pe.wait_ge(consts_in, 8 * 16)
            with pe.Fori(0, B) as b:
                pe.wait_ge(x_split, b + 1)
                for t in range(QB):
                    for k in range(KD):
                        last = split_matmul(nc, product[t][:], x_hi[:, k, t * P:(t + 1) * P],
                                            x_lo[:, k, t * P:(t + 1) * P], wa_hi[:, k, :], wa_lo[:, k, :],
                                            k == 0, k == KD - 1)
                    last.then_inc(lat_mm, 1)
                for k in range(KD):
                    last = split_matmul(nc, rotary[:], wr_hi[:, k, :], wr_lo[:, k, :], x_hi[:, k, :],
                                        x_lo[:, k, :], k == 0, k == KD - 1)
                last.then_inc(rot_mm, 1)
                pe.wait_ge(normed, QB * (b + 1))
                for c in range(KQ + 1):
                    if c == 3:
                        pe.wait_ge(turn_lo, (KQ + 1) * b + 1)
                    for t in range(QB):
                        last = nc.tensor.transpose(turned[c % 3][:, t * P:(t + 1) * P],
                                                   latent[:, t, c * P:(c + 1) * P], g.ident[:])
                    last.then_inc(turn_mm, 1)


def attention_phase(nc, g, io):
    NS = 2 * B
    with ExitStack() as stack:
        m = Space(nc, stack)
        raw_q = m.sb("raw_q", [P, 2, QL])
        raw_k = m.sb("raw_k", [P, 2, KL])
        raw_r = m.sb("raw_r", [P, KQ, P])
        raw_v = m.sb("raw_v", [P, 2, KL])
        raw_o = m.sb("raw_o", [P, 2, D])
        wq_hi = m.sb("wq_hi", [P, 2, KQ, KL], F32R)
        wq_lo = m.sb("wq_lo", [P, 2, KQ, KL], F32R)
        wr_hi = m.sb("wr_hi", [P, KQ, P], F32R)
        wr_lo = m.sb("wr_lo", [P, KQ, P], F32R)
        wo_hi = m.sb("wo_hi", [P, 2, D], F32R)
        wo_lo = m.sb("wo_lo", [P, 2, D], F32R)
        q_hi = m.sb("q_hi", [P, S], F32R)
        q_lo = m.sb("q_lo", [P, S], F32R)
        rot = m.sb("qrot", [P, S])
        rot_swapped = m.sb("qrot_swapped", [P, S])
        qr = m.sb("qr_stacked", [P, 2, S], F32R)
        probs = m.sb("probs", [P, 2, sum(SEEN)])
        neg_max = m.sb("neg_max", [P, 2, QB])
        row_sum = m.sb("row_sum", [P, 2, QB])
        row_inv = m.sb("row_inv", [P, 2, QB])
        pt_hi = m.sb("pt_hi", [P, sum(SEEN)], F32R)
        pt_lo = m.sb("pt_lo", [P, sum(SEEN)], F32R)
        mix_hi = m.sb("mix_hi", [P, 2, S], F32R)
        mix_lo = m.sb("mix_lo", [P, 2, S], F32R)
        score = m.banks("score_bank", 3)
        turned = m.banks("prob_bank", 2)
        front = m.psum("front_bank", [P, 512])
        mixed = m.psum("mixed_bank", [P, 512])
        outp = m.psum("out_bank", [P, 512])

        GROUPS = ((3,), (2, 0), (1,))
        NG = len(GROUPS)

        def score_at(q):
            bank, at = {3: (0, 0), 2: (1, 0), 0: (1, 3 * P), 1: (2, 0)}[q]
            return score[bank][:, at:at + SEEN[q]]

        def probs_at(h, q, start, size):
            at = sum(SEEN[:q]) + start
            return probs[:, h, at:at + size]

        def pt_at(x, k):
            at = sum(S - i * P for i in range(k))
            return x[:, at:at + S - k * P]

        def turned_at(k):
            bank, at = {0: (turned[0], 0), 1: (turned[1], 0), 3: (turned[1], 3 * P), 2: (score[2], 2 * P)}[k]
            return bank[:, at:at + S - k * P]

        fold_in = m.sem("fold_in")
        rope_in = m.sem("rope_in")
        outw_in = m.sem("outw_in")
        front_mm = m.sem("front_mm")
        outw_hi = m.sem("outw_hi")
        q_hi_ready = m.sem("q_hi_ready")
        q_ready = m.sem("q_ready")
        wq_ready = m.sem("wq_ready")
        wr_ready = m.sem("wr_ready")
        wo_ready = m.sem("wo_ready")
        rope_read = m.sem("rope_read")
        rope_swapped = m.sem("rope_swapped")
        rope_turned = m.sem("rope_turned")
        rope_hi = m.sem("rope_hi")
        rope_ready = m.sem("rope_ready")
        score_mm = m.sem("score_mm")
        max_ready = m.sem("max_ready")
        exp_done = m.sem("exp_done")
        inv_ready = m.sem("inv_ready")
        probs_ready = m.sem("probs_ready")
        turn_mm = m.sem("pturn_mm")
        turn_hi = m.sem("pturn_hi")
        turn_lo = m.sem("pturn_lo")
        mix_mm = m.sem("mix_mm")
        mix_hi_ready = m.sem("mix_hi_ready")
        mix_ready = m.sem("mix_ready")
        out_mm = m.sem("out_mm")
        out_added = m.sem("out_added")
        split_step = m.sem("split_step")
        block = stack.enter_context(nc.Block())

        FRONT = 16

        def front_uses(s, last):
            uses = [("rope", s // 2 + 1)] if s % 2 and not (last and s == NS - 1) else []
            if not (last and s == NS - 1):
                uses.append(("query", s + 1))
            if s in (1, 2):
                uses.append(("outw", s - 1))
            if s in (6, 7) and not last:
                uses.append(("wq", s - 6))
            return uses

        def front_index(s, last):
            return 4 + sum(len(front_uses(i, False)) for i in range(s))

        PROLOGUE = [("wq", 0), ("rope", 0), ("query", 0), ("wq", 1)]

        @block.sync
        def _(sp):
            wq_n = io["wq_nope"].rearrange("h d c -> d h c")
            wk_n = io["w_kv"][:, 0:NOPE, :].rearrange("h d c -> d h c")
            wv_n = io["w_kv"][:, NOPE:, :].rearrange("h d c -> d h c")
            wo_n = io["w_o_t"].rearrange("(h p) n -> p h n", p=P)
            wr_n = io["wq_rope_t"].rearrange("(k p) n -> p k n", p=P)

            def load_queries(p):
                sp.dma_start(raw_q[:], wq_n[:, bass.ts(p, 2), :]).then_inc(fold_in, 16)
                sp.dma_start(raw_k[:], wk_n[:, bass.ts(p, 2), :]).then_inc(fold_in, 16)
                sp.dma_start(raw_r[:], wr_n[:, :, bass.ts(p, P)]).then_inc(rope_in, 16)

            def load_outputs(p):
                sp.dma_start(raw_v[:], wv_n[:, bass.ts(p, 2), :]).then_inc(outw_in, 16)
                sp.dma_start(raw_o[:], wo_n[:, bass.ts(p, 2), :]).then_inc(outw_in, 16)

            load_queries(0)
            load_outputs(0)
            with sp.Fori(1, NP) as p:
                sp.wait_ge(wq_ready, 2 * p)
                sp.wait_ge(wr_ready, p)
                load_queries(p)
                sp.wait_ge(wo_ready, 2 * p)
                load_outputs(p)

        def over_pairs(engine, pair):
            pair(0, True, False)
            with engine.Fori(1, NP - 1) as p:
                pair(p, False, False)
            pair(NP - 1, False, True)

        @block.tensor
        def _(pe):
            before = [None]

            def front_one(p, kind, a):
                if before[0]:
                    p0, kind0, a0 = before[0]
                    read, count = {"wq": (wq_ready, 2), "outw": (wo_ready, 2), "rope": (rope_read, B),
                                   "query": (q_ready, NS)}[kind0]
                    pe.wait_ge(read, count * p0 + a0 + 1)
                before[0] = (p, kind, a)
                if kind == "wq":
                    pe.wait_ge(fold_in, (p + 1) * 32)
                    for c in range(KQ):
                        last = nc.tensor.matmul(front[:, c * KL:(c + 1) * KL], raw_q[:, a, c * P:(c + 1) * P],
                                                raw_k[:, a, :], start=True, stop=True)
                elif kind == "outw":
                    pe.wait_ge(outw_in, (p + 1) * 32)
                    last = nc.tensor.matmul(front[:], raw_v[:, a, :], raw_o[:, a, :], start=True, stop=True)
                elif kind == "rope":
                    if a % B == 0:
                        pe.wait_ge(wr_ready, p + 1)
                    b = a % B
                    for c in range(KQ):
                        last = split_matmul(nc, front[:], wr_hi[:, c, :], wr_lo[:, c, :],
                                            g.qn_hi[:, c, b * S:(b + 1) * S], g.qn_lo[:, c, b * S:(b + 1) * S],
                                            c == 0, c == KQ - 1)
                else:
                    h, b = a % 2, a // 2
                    if b == 0:
                        pe.wait_ge(wq_ready, 2 * p + h + 1)
                    for c in range(KQ):
                        last = split_matmul(nc, front[:], wq_hi[:, h, c, :], wq_lo[:, h, c, :],
                                            g.qn_hi[:, c, b * S:(b + 1) * S], g.qn_lo[:, c, b * S:(b + 1) * S],
                                            c == 0, c == KQ - 1)
                last.then_inc(front_mm, 1)

            def place(p, kind, a):
                if kind == "wq":
                    return p + 1, kind, a
                if (kind == "rope" and a == B) or (kind == "query" and a == NS):
                    return p + 1, kind, 0
                return p, kind, a

            def scores(p, s):
                b, h = s // 2, s % 2
                pe.wait_ge(q_ready, NS * p + s + 1)
                pe.wait_ge(rope_ready, B * p + b + 1)
                past(pe, exp_done, NG * (NS * p + s))
                for q in [q for group in GROUPS for q in group]:
                    n, tile = SEEN[q], slice(q * P, (q + 1) * P)
                    out = score_at(q)
                    keys = slice(b * S, b * S + n)
                    split_matmul(nc, out, q_hi[:, tile], q_lo[:, tile], g.key_hi[:, keys], g.key_lo[:, keys],
                                 True, False)
                    nc.tensor.matmul(out, qr[:, h, tile], g.kr_hi[:, keys], start=False, stop=False)
                    nc.tensor.matmul(out, qr[:, h, tile], g.kr_lo[:, keys], start=False, stop=False)
                    last = nc.tensor.matmul(out[:, q * P:n], g.ident_b[:], g.mask[:], start=False, stop=True)
                    if q != 2:
                        last.then_inc(score_mm, 1)

            def turn(j, s, parts, scored=0):
                h = s % 2
                if 0 in parts:
                    pe.wait_ge(probs_ready, j + 1)
                    past(pe, turn_lo, 3 * j)
                if 2 in parts:
                    pe.wait_ge(exp_done, scored)
                for k in parts:
                    for q in range(k, QB):
                        last = nc.tensor.transpose(turned_at(k)[:, (q - k) * P:(q - k + 1) * P],
                                                   probs_at(h, q, k * P, P), g.ident[:])
                    if k != 1:
                        last.then_inc(turn_mm, 1)

            def mix(j, s, n_out):
                b = s // 2
                past(pe, mix_ready, j)
                if n_out is not None:
                    pe.wait_ge(out_added, n_out)
                for i, (k, ready) in enumerate(((0, 1), (1, 2), (3, 2), (2, 3))):
                    pe.wait_ge(turn_lo, 3 * j + ready)
                    t = b * QB + k
                    last = split_matmul(nc, mixed[:, k * P:S], g.val_hi[:, t, :], g.val_lo[:, t, :],
                                        pt_at(pt_hi, k), pt_at(pt_lo, k), i == 0, i == QB - 1)
                last.then_inc(mix_mm, 1)

            def project(n, tiles):
                for t in tiles:
                    if t == 0:
                        pe.wait_ge(mix_ready, 2 * n + 2)
                        past(pe, out_added, QB * n)
                    bank = outp if t % 2 == 0 else mixed
                    if t >= 2:
                        pe.wait_ge(out_added, QB * n + t - 1)
                    for h in range(2):
                        last = split_matmul(nc, bank[:], mix_hi[:, h, t * P:(t + 1) * P],
                                            mix_lo[:, h, t * P:(t + 1) * P], wo_hi[:, h, :], wo_lo[:, h, :],
                                            h == 0, h == 1)
                    last.then_inc(out_mm, 1)

            def pair(p, first, last):
                for s in range(NS):
                    j = NS * p + s
                    back = not (first and s == 0)
                    uses = [place(p, *u) for u in front_uses(s, last)]
                    if s == 0:
                        before[0] = (p, "wq", 1)
                    scores(p, s)
                    if s % 2 == 0:
                        if back:
                            turn(j - 1, (s - 1) % NS, (0, 1, 3))
                        front_one(*uses[0])
                        if back:
                            turn(j - 1, (s - 1) % NS, (2,), NG * (j + 1))
                            mix(j - 1, (s - 1) % NS, None)
                        rest = 1
                    else:
                        n = B * p + s // 2 - 1
                        out = not (first and s == 1)
                        rest = 0
                        if uses and uses[0][1] == "rope":
                            front_one(*uses[0])
                            rest = 1
                        turn(j - 1, s - 1, (0, 1, 3))
                        if out:
                            if s == 3:
                                pe.wait_ge(wo_ready, 2 * p + 2)
                            project(n, (0, 1))
                        turn(j - 1, s - 1, (2,), NG * (j + 1))
                        if out:
                            project(n, (2, 3))
                        if len(uses) > rest and uses[rest][1] == "query":
                            front_one(*uses[rest])
                            rest += 1
                        mix(j - 1, s - 1, QB * (n + 1) if out else None)
                    for i in range(rest, len(uses)):
                        front_one(*uses[i])

            for i, (kind, a) in enumerate(PROLOGUE):
                front_one(0, kind, a)
            over_pairs(pe, pair)
            j = NS * NP - 1
            turn(j, NS - 1, (0, 1, 3, 2), NG * (j + 1))
            mix(j, NS - 1, QB * (B * NP - 1))
            project(B * NP - 1, range(QB))

        @block.scalar
        def _(act):
            def front_one(kind, p, a, index):
                if kind == "outw":
                    act.wait_ge(front_mm, index + 1)
                    nc.scalar.activation(wo_hi[:, a, :], front[:], ACT.Copy).then_inc(outw_hi, 1)
                elif kind == "query":
                    act.wait_ge(front_mm, index + 1)
                    nc.scalar.activation(q_hi[:], front[:], ACT.Copy).then_inc(q_hi_ready, 1)
                elif kind == "rope":
                    act.wait_ge(rope_turned, B * p + a + 1)
                    nc.scalar.activation(qr[0:64, 0, :], rot[0:64, :], ACT.Copy)
                    nc.scalar.activation(qr[64:P, 1, :], rot[64:P, :], ACT.Copy).then_inc(rope_hi, 1)

            def softmax(j, h, first_two):
                if not first_two:
                    act.wait_ge(turn_mm, 3 * (j - 1))
                for i, group in enumerate(GROUPS):
                    act.wait_ge(max_ready, NG * j + i + 1)
                    for q in group:
                        last = nc.scalar.activation(probs_at(h, q, 0, SEEN[q]), score_at(q), ACT.Exp,
                                                    bias=neg_max[:, h, q:q + 1], accum_out=row_sum[:, h, q:q + 1])
                    last.then_inc(exp_done, 1)

            def turn(j, parts):
                for i in parts:
                    act.wait_ge(turn_mm, 3 * j + i + 1)
                    for k in ((0,), (1, 3), (2,))[i]:
                        last = nc.scalar.activation(pt_at(pt_hi, k), turned_at(k), ACT.Copy)
                    last.then_inc(turn_hi, 1)

            def mix(j, h):
                act.wait_ge(mix_mm, j + 1)
                nc.scalar.activation(mix_hi[:, h, :], mixed[:], ACT.Copy).then_inc(mix_hi_ready, 1)

            def pair(p, first, last):
                for s in range(NS):
                    j = NS * p + s
                    back = not (first and s == 0)
                    uses = front_uses(s, last)
                    index = FRONT * p + front_index(s, last)
                    softmax(j, s % 2, first and s < 2)
                    if back:
                        turn(j - 1, (0, 1))
                        if s % 2:
                            turn(j - 1, (2,))
                    for i, (kind, a) in enumerate(uses):
                        if kind in ("rope", "query"):
                            front_one(kind, p, a, index + i)
                    if back:
                        if s % 2 == 0:
                            turn(j - 1, (2,))
                        mix(j - 1, (s - 1) % 2)
                    for i, (kind, a) in enumerate(uses):
                        if kind == "outw":
                            front_one(kind, p, a, index + i)

            for i, (kind, a) in enumerate(PROLOGUE):
                front_one(kind, 0, a, i)
            over_pairs(act, pair)
            turn(NS * NP - 1, (0, 1, 2))
            mix(NS * NP - 1, 1)

        @block.vector
        def _(dve):
            def split_columns(hi, lo, src, chain_at, ready):
                for c in range(KQ):
                    last = nc.vector.tensor_scalar(hi[:, c, :], src[:, c, :], g.q_gain[:, c:c + 1], None, ALU.mult)
                last.then_inc(split_step, 1)
                dve.wait_ge(split_step, chain_at)
                for c in range(KQ):
                    last = nc.vector.scalar_tensor_tensor(lo[:, c, :], src[:, c, :], g.q_gain[:, c:c + 1],
                                                          hi[:, c, :].bitcast(F32), ALU.mult, ALU.subtract)
                return last.then_inc(ready, 1)

            def front_one(kind, p, a, index):
                if kind == "wq":
                    dve.wait_ge(front_mm, index + 1)
                    src = front[:, 0:KQ * KL].rearrange("p (c n) -> p c n", c=KQ)
                    split_columns(wq_hi[:, a], wq_lo[:, a], src, 3 * p + (1 if a == 0 else 3), wq_ready)
                    if a == 0:
                        dve.wait_ge(rope_in, 16 * (p + 1))
                        split_columns(wr_hi, wr_lo, raw_r, 3 * p + 2, wr_ready)
                elif kind == "outw":
                    dve.wait_ge(outw_hi, 2 * p + a + 1)
                    nc.vector.tensor_tensor(wo_lo[:, a, :], front[:], wo_hi[:, a, :].bitcast(F32),
                                            ALU.subtract).then_inc(wo_ready, 1)
                elif kind == "rope":
                    dve.wait_ge(front_mm, index + 1)
                    past(dve, rope_ready, B * p + a)
                    nc.vector.tensor_tensor(rot[:], front[:], g.cos[:], ALU.mult)
                    nc.vector.stream_shuffle(rot_swapped[:], front[:], SWAP).then_inc(rope_read, 1)
                else:
                    dve.wait_ge(q_hi_ready, NS * p + a + 1)
                    nc.vector.tensor_tensor(q_lo[:], front[:], q_hi[:].bitcast(F32),
                                            ALU.subtract).then_inc(q_ready, 1)

            def maxima(j, h):
                for i, group in enumerate(GROUPS):
                    dve.wait_ge(score_mm, NG * j + i + 1)
                    for q in group:
                        last = nc.vector.tensor_reduce(neg_max[:, h, q:q + 1], score_at(q), AX_X, ALU.max, negate=True)
                    last.then_inc(max_ready, 1)

            def normalise(j, h):
                dve.wait_ge(exp_done, NG * (j + 1))
                nc.vector.reciprocal(row_inv[:, h, :], row_sum[:, h, :]).then_inc(inv_ready, 1)
                dve.wait_ge(inv_ready, j + 1)
                for q in range(QB):
                    row = probs_at(h, q, 0, SEEN[q])
                    last = nc.vector.tensor_scalar(row, row, row_inv[:, h, q:q + 1], None, ALU.mult)
                last.then_inc(probs_ready, 1)

            def turn(j, parts):
                for i in parts:
                    dve.wait_ge(turn_hi, 3 * j + i + 1)
                    for k in ((0,), (1, 3), (2,))[i]:
                        last = nc.vector.tensor_tensor(pt_at(pt_lo, k), turned_at(k),
                                                       pt_at(pt_hi, k).bitcast(F32), ALU.subtract)
                    last.then_inc(turn_lo, 1)

            def mix(j, h):
                dve.wait_ge(mix_hi_ready, j + 1)
                nc.vector.tensor_tensor(mix_lo[:, h, :], mixed[:], mix_hi[:, h, :].bitcast(F32),
                                        ALU.subtract).then_inc(mix_ready, 1)

            def add(n, b, tiles):
                for t in tiles:
                    bank = outp if t % 2 == 0 else mixed
                    row = g.res[:, b * QB + t, :]
                    dve.wait_ge(out_mm, QB * n + t + 1)
                    nc.vector.tensor_tensor(row, bank[:], row, ALU.add).then_inc(out_added, 1)

            def pair(p, first, last):
                for s in range(NS):
                    j = NS * p + s
                    back = not (first and s == 0)
                    uses = front_uses(s, last)
                    index = FRONT * p + front_index(s, last)

                    def use(kinds):
                        for i, (kind, a) in enumerate(uses):
                            if kind in kinds:
                                if kind == "wq":
                                    front_one(kind, p + 1, a, index + i)
                                else:
                                    front_one(kind, p, a, index + i)

                    maxima(j, s % 2)
                    if s % 2 == 0:
                        if back:
                            turn(j - 1, (0, 1))
                        use(("query",))
                        if back:
                            turn(j - 1, (2,))
                        normalise(j, 0)
                        if back:
                            mix(j - 1, 1)
                    else:
                        n, b = B * p + s // 2 - 1, (s // 2 - 1) % B
                        out = not (first and s == 1)
                        use(("rope",))
                        turn(j - 1, (0, 1))
                        if out:
                            add(n, b, (0, 1))
                        turn(j - 1, (2,))
                        if out:
                            add(n, b, (2, 3))
                        normalise(j, 1)
                        use(("query",))
                        mix(j - 1, 0)
                    use(("outw", "wq"))

            for i, (kind, a) in enumerate(PROLOGUE):
                front_one(kind, 0, a, i)
            over_pairs(dve, pair)
            turn(NS * NP - 1, (0, 1, 2))
            mix(NS * NP - 1, 1)
            add(B * NP - 1, B - 1, range(QB))

        @block.gpsimd
        def _(pool):
            def rope(n):
                pool.wait_ge(rope_read, n + 1)
                nc.gpsimd.tensor_tensor(rot_swapped[:], rot_swapped[:], g.sin[:], ALU.mult).then_inc(rope_swapped, 1)
                pool.wait_ge(rope_swapped, n + 1)
                nc.gpsimd.tensor_tensor(rot[:], rot[:], rot_swapped[:], ALU.add).then_inc(rope_turned, 1)
                pool.wait_ge(rope_hi, n + 1)
                nc.gpsimd.tensor_tensor(qr[64:P, 0, :], rot[0:64, :], qr[0:64, 0, :].bitcast(F32), ALU.subtract)
                nc.gpsimd.tensor_tensor(qr[0:64, 1, :], rot[64:P, :], qr[64:P, 1, :].bitcast(F32),
                                        ALU.subtract).then_inc(rope_ready, 1)

            with pool.Fori(0, B * NP) as n:
                rope(n)


def norm_rows(nc, dve, chain, carry, rows, n, stats, mean_var, inv, newton, variance_ready, root_ready, count):
    nc.vector.memset(carry[:, 0:1], 0.0)
    for t in range(n):
        last = nc.vector.bn_stats(stats[:, t, :], rows(t))
    chain.link(last)
    nc.vector.memset(carry[:, 1:2], 0.0)
    for t in range(n):
        last = nc.vector.bn_aggr(mean_var[:, t, :], stats[:, t, :])
    chain.link(last)
    chain.link(nc.vector.tensor_scalar(newton[:, 0:n], mean_var[:, 0:n, 1], LN_EPS, None, ALU.add))
    dve.sem_inc(variance_ready, 1)
    dve.wait_ge(root_ready, count)
    chain.link(nc.vector.reciprocal(inv[:, 0:n], inv[:, 0:n]))
    chain.link(nc.vector.tensor_tensor(newton[:, 0:n], newton[:, 0:n], inv[:, 0:n], ALU.mult))
    chain.link(nc.vector.tensor_tensor(newton[:, 0:n], newton[:, 0:n], inv[:, 0:n], ALU.mult))
    chain.link(nc.vector.tensor_scalar(newton[:, 0:n], newton[:, 0:n], -0.5, 1.5, ALU.mult, ALU.add))
    chain.link(nc.vector.tensor_tensor(inv[:, 0:n], inv[:, 0:n], newton[:, 0:n], ALU.mult))
    for t in range(n):
        last = nc.vector.tensor_scalar(rows(t), rows(t), mean_var[:, t, 0:1], inv[:, t:t + 1],
                                       ALU.subtract, ALU.mult)
    return last


NORM_STEPS = 8


def quant_phase(nc, g, io):
    with ExitStack() as stack:
        m = Space(nc, stack)
        w1 = m.sb("w1_rows", [P, KD, D])
        w2 = m.sb("w2_rows", [P, KD, INNER])
        xs = m.sb("xs", [P, QB, D])
        ws = m.sb("ws", [P, KD, D])
        hidden = m.sb("hidden", [P, QB, D])
        gated = m.sb("gated", [P, QB, INNER])
        amax = m.sb("amax", [P, 2, D])
        top = m.sb("top", [P, 2, KD])
        ratio = m.sb("ratio", [P, KD])
        root = m.sb("root", [P, KD])
        tiny = m.sb("tiny", [P, KD])
        factor = m.sb("factor", [P, 2, KD])
        diag = m.sb("diag", [P, 2, KD, P])
        rowmax = m.sb("rowmax", [P, 2, KD])
        step = m.sb("step", [P, 2, KD])
        per = m.sb("per", [P, 2, KD])
        xq = m.sb("xq", [P, QB, D], BF16)
        wq = m.sb("wq", [P, KD, D], BF16)
        xq_t = m.sb("xq_t", [P, KD, S], BF16)
        wq_t = m.sb("wq_t", [P, KD, D], BF16)
        wstep = m.sb("wstep", [P, D])
        stats = m.sb("stats", [P, NT, 6])
        mean_var = m.sb("mean_var", [P, NT, 2])
        inv = m.sb("inv", [P, NT])
        newton = m.sb("norm_newton", [P, NT])
        round_bias = m.sb("round_bias", [P, 1])
        top_bank = m.banks("top_bank", 2)
        spread = m.banks("spread_bank", 2)
        turned = [m.psum(f"qturn_bank{i}", [P, 1024], BF16) for i in range(2)]
        out = m.psum("qout_bank", [P, 512])
        step_bank = m.psum("step_bank", [P, 512])

        w_in = m.sem("w_in")
        amax_ready = m.sem("amax_ready")
        top_mm = m.sem("top_mm")
        ratio_ready = m.sem("ratio_ready")
        qroot_ready = m.sem("qroot_ready")
        diag_ready = m.sem("diag_ready")
        spread_mm = m.sem("spread_mm")
        scaled = m.sem("scaled")
        rounded = m.sem("rounded")
        quantised = m.sem("quantised")
        qturn_mm = m.sem("qturn_mm")
        qturn_read = m.sem("qturn_read")
        step_mm = m.sem("step_mm")
        step_read = m.sem("step_read")
        qout_mm = m.sem("qout_mm")
        qout_read = m.sem("qout_read")
        silu_done = m.sem("silu_done")
        batch_done = m.sem("batch_done")
        variance_ready = m.sem("variance_ready")
        nroot_ready = m.sem("nroot_ready")
        dve_step = m.sem("quant_dve_step")
        block = stack.enter_context(nc.Block())

        LINEARS = ((0, w1, KD), (1, w2, INNER // P))
        TURNS = 2 * sum(n for _, _, n in LINEARS)

        @block.sync
        def _(sp):
            def load(b):
                for w, name in ((w1, "w_gate_up"), (w2, "w_down")):
                    view = io[name].rearrange("b (t p) n -> b p t n", p=P)[bass.ts(b, 1)]
                    sp.dma_start(w[:], view.rearrange("b p t n -> (b p) t n")).then_inc(w_in, 16)

            load(0)
            with sp.Fori(1, B) as b:
                sp.wait_ge(batch_done, b)
                load(b)

        @block.scalar
        def _(act):
            act.wait_ge(variance_ready, 1)
            nc.scalar.activation(inv[:], newton[:], ACT.Sqrt).then_inc(nroot_ready, 1)
            with act.Fori(0, B) as b:
                for i, w, n in LINEARS:
                    act.wait_ge(ratio_ready, 2 * b + i + 1)
                    nc.scalar.activation(root[:, 0:n], ratio[:, 0:n], ACT.Sqrt).then_inc(qroot_ready, 1)
                    for side, data in ((0, xs), (1, ws)):
                        act.wait_ge(scaled, 4 * b + 2 * i + side + 1)
                        for t in range(QB):
                            row = data[:, t, 0:n * P]
                            last = nc.scalar.activation(row, row, ACT.Identity, bias=round_bias[:],
                                                        scale=per[:, side, t:t + 1])
                        last.then_inc(rounded, 1)
                    act.wait_ge(step_mm, 2 * b + i + 1)
                    nc.scalar.activation(wstep[:], step_bank[:], ACT.Copy).then_inc(step_read, 1)
                    for c in range(n):
                        act.wait_ge(qturn_mm, TURNS * b + (0, 2 * KD)[i] + c + 1)
                        nc.scalar.activation(xq_t[:, c, :], turned[0][:, 0:S], ACT.Copy).then_inc(qturn_read, 1)
                    if i == 0:
                        for t in range(QB):
                            act.wait_ge(qout_read, 2 * QB * b + t + 1)
                            nc.scalar.activation(gated[:, t, :], hidden[:, t, 0:INNER], ACT.Silu).then_inc(silu_done, 1)
                act.wait_ge(variance_ready, b + 2)
                nc.scalar.activation(inv[:, 0:QB], newton[:, 0:QB], ACT.Sqrt).then_inc(nroot_ready, 1)

        @block.vector
        def _(dve):
            start = Chain(dve, dve_step)
            start.link(nc.vector.memset(round_bias[:], ROUND))
            last = norm_rows(nc, dve, start, g.carry, lambda t: g.res[:, t, :], NT, stats, mean_var, inv, newton,
                             variance_ready, nroot_ready, 1)
            start.link(last)
            BATCH = 46
            with dve.Fori(0, B) as b:
                chain = Chain(dve, dve_step, start.n + b * BATCH)
                res = g.res[:, bass.ts(b, QB), :]
                for i, w, n in LINEARS:
                    x = res if i == 0 else gated[:]
                    width = n * P
                    dve.wait_ge(w_in, 32 * (b + 1))
                    for side, data in ((0, x), (1, w[:])):
                        nc.vector.tensor_reduce(amax[:, side, 0:width], data.rearrange("p t k -> p k t"), AX_X,
                                                ALU.max, apply_absolute_value=True).then_inc(amax_ready, 1)
                    dve.wait_ge(top_mm, 2 * (2 * b + i) + 2)
                    for side in range(2):
                        last = nc.vector.tensor_reduce(
                            top[:, side, 0:n], top_bank[side][:, 0:width].rearrange("p (k q) -> p k q", k=n),
                            AX_X, ALU.max)
                    chain.link(last)
                    chain.link(nc.vector.tensor_scalar(top[:, :, 0:n], top[:, :, 0:n], Q_EPS, None, ALU.max))
                    chain.link(nc.vector.reciprocal(tiny[:, 0:n], top[:, 1, 0:n]))
                    nc.vector.tensor_tensor(ratio[:, 0:n], top[:, 0, 0:n], tiny[:, 0:n],
                                            ALU.mult).then_inc(ratio_ready, 1)
                    dve.wait_ge(qroot_ready, 2 * b + i + 1)
                    chain.link(nc.vector.reciprocal(tiny[:, 0:n], root[:, 0:n]))
                    chain.link(nc.vector.tensor_tensor(tiny[:, 0:n], tiny[:, 0:n], ratio[:, 0:n], ALU.mult))
                    chain.link(nc.vector.tensor_tensor(tiny[:, 0:n], tiny[:, 0:n], root[:, 0:n], ALU.add))
                    chain.link(nc.vector.tensor_scalar(factor[:, 1, 0:n], tiny[:, 0:n], 0.5, Q_EPS, ALU.mult, ALU.max))
                    chain.link(nc.vector.reciprocal(factor[:, 0, 0:n], factor[:, 1, 0:n]))
                    for side in range(2):
                        for k in range(n):
                            last = nc.vector.tensor_scalar(diag[:, side, k, :], g.ident[:],
                                                           factor[:, side, k:k + 1], None, ALU.mult)
                        last.then_inc(diag_ready, 1)
                    for side, data, dst in ((0, x, xs), (1, w[:], ws)):
                        dve.wait_ge(spread_mm, 2 * (2 * b + i) + side + 1)
                        for t in range(QB):
                            last = nc.vector.tensor_tensor(dst[:, t, 0:width], data[:, t, :],
                                                           spread[side][:, 0:width], ALU.mult)
                        chain.link(last)
                        chain.link(nc.vector.tensor_reduce(rowmax[:, side, :], dst[:, :, 0:width], AX_X, ALU.max,
                                                           apply_absolute_value=True))
                        chain.link(nc.vector.tensor_scalar(rowmax[:, side, :], rowmax[:, side, :], Q_EPS, None, ALU.max))
                        chain.link(nc.vector.tensor_scalar(step[:, side, :], rowmax[:, side, :], 1.0 / QMAX, None,
                                                           ALU.mult))
                        nc.vector.reciprocal(per[:, side, :], step[:, side, :]).then_inc(scaled, 1)
                    dve.wait_ge(spread_mm, 2 * (2 * b + i) + 2)
                    for t in range(KD):
                        last = nc.vector.tensor_scalar(diag[:, 0, t, :], g.ident[:], step[:, 1, t:t + 1], None, ALU.mult)
                    last.then_inc(diag_ready, 1)
                    for side, data, dst in ((0, xs, xq), (1, ws, wq)):
                        dve.wait_ge(rounded, 4 * b + 2 * i + side + 1)
                        v = data[:, :, 0:width]
                        chain.link(nc.vector.tensor_scalar(v, v, ROUND - QMAX, ROUND + QMAX, ALU.max, ALU.min))
                        nc.vector.tensor_scalar(dst[:, :, 0:width], v, -ROUND, None, ALU.add).then_inc(quantised, 1)
                    for c in range(n):
                        dve.wait_ge(qturn_mm, TURNS * b + (0, 2 * KD)[i] + n + c + 1)
                        nc.vector.tensor_copy(wq_t[:, c, :], turned[1][:, 0:D]).then_inc(qturn_read, 1)
                    dve.wait_ge(step_read, 2 * b + i + 1)
                    for t in range(QB):
                        dve.wait_ge(qout_mm, 2 * QB * b + QB * i + t + 1)
                        nc.vector.scalar_tensor_tensor(hidden[:, t, :], out[:], step[:, 0, t:t + 1], wstep[:],
                                                       ALU.mult, ALU.mult).then_inc(qout_read, 1)
                    dve.wait_ge(qout_read, 2 * QB * b + QB * (i + 1))
                    if i == 0:
                        dve.wait_ge(silu_done, QB * (b + 1))
                        chain.link(nc.vector.tensor_tensor(gated[:], gated[:], hidden[:, :, INNER:], ALU.mult))
                    else:
                        chain.link(nc.vector.tensor_tensor(res, res, hidden[:], ALU.add))
                last = norm_rows(nc, dve, chain, g.carry, lambda t: g.res[:, bass.ds(b * QB + t, 1), :], QB, stats, mean_var,
                                 inv, newton, variance_ready, nroot_ready, b + 2)
                last.then_inc(batch_done, 1)
                assert chain.n == BATCH, chain.n

        @block.tensor
        def _(pe):
            with pe.Fori(0, B) as b:
                for i, w, n in LINEARS:
                    width = n * P
                    for side in range(2):
                        pe.wait_ge(amax_ready, 2 * (2 * b + i) + side + 1)
                        for k in range(n):
                            last = nc.tensor.transpose(top_bank[side][:, k * P:(k + 1) * P],
                                                       amax[:, side, k * P:(k + 1) * P], g.ident[:])
                        last.then_inc(top_mm, 1)
                    for side in range(2):
                        pe.wait_ge(diag_ready, 3 * (2 * b + i) + side + 1)
                        nc.tensor.matmul(spread[side][:, 0:width], g.ones[:], diag[:, side, 0:n, :],
                                         start=True, stop=True).then_inc(spread_mm, 1)
                    pe.wait_ge(diag_ready, 3 * (2 * b + i) + 3)
                    nc.tensor.matmul(step_bank[:], g.ones[:], diag[:, 0, :, :], start=True, stop=True).then_inc(step_mm, 1)
                    for side, data in ((0, xq), (1, wq)):
                        pe.wait_ge(quantised, 2 * (2 * b + i) + side + 1)
                        for c in range(n):
                            if (i, side, c) != (0, 0, 0):
                                pe.wait_ge(qturn_read, TURNS * b + (0, 2 * KD)[i] + side * n + c)
                            for t in range(QB):
                                last = nc.tensor.transpose(turned[side][:, t * P:(t + 1) * P],
                                                           data[:, t, c * P:(c + 1) * P], g.ident_b[:])
                            last.then_inc(qturn_mm, 1)
                    pe.wait_ge(qturn_read, TURNS * b + (0, 2 * KD)[i] + 2 * n)
                    for t in range(QB):
                        if (i, t) != (0, 0):
                            pe.wait_ge(qout_read, 2 * QB * b + QB * i + t)
                        for c in range(n):
                            last = nc.tensor.matmul(out[:], xq_t[:, c, t * P:(t + 1) * P], wq_t[:, c, :],
                                                    start=c == 0, stop=c == n - 1)
                        last.then_inc(qout_mm, 1)


def expert_phase(nc, g, io):
    lower, upper, centre = 0.5 - float(np.log(4.0 / 3.0)), 0.5, 1.0 / float(np.e)
    with ExitStack() as stack:
        m = Space(nc, stack)
        x_hi = m.sb("xt_hi", [P, KD, NT * P], F32R)
        x_lo = m.sb("xt_lo", [P, KD, NT * P], F32R)
        raw = [m.sb(f"raw_{k}", [P, KD, FF]) for k in ("gate", "up", "down")]
        w_hi = [m.sb(f"hi_{k}", [P, KD, FF], F32R) for k in ("gate", "up", "down")]
        w_lo = [m.sb(f"lo_{k}", [P, KD, FF], F32R) for k in ("gate", "up", "down")]
        h_hi = m.sb("h_hi", [P, KF, S], F32R)
        h_lo = m.sb("h_lo", [P, KF, S], F32R)
        silu = m.sb("silu", [P, S])
        h = m.sb("h", [P, S])
        wr = m.sb("router", [P, KD, E])
        wr_hi = m.sb("router_hi", [P, KD, E], F32R)
        wr_lo = m.sb("router_lo", [P, KD, E], F32R)
        temp = m.sb("temperature", [P, 1])
        weight = m.sb("weight", [P, NT, E])
        r = [m.sb(f"route{i}", [P, NT, E]) for i in range(5)]
        rs = [m.sb(f"route_sum{i}", [P, NT]) for i in range(3)]
        stats = m.sb("stats2", [P, NT, 6])
        mean_var = m.sb("mean_var2", [P, NT, 2])
        inv = m.sb("inv2", [P, NT])
        newton = m.sb("norm_newton2", [P, NT])
        gate = m.banks("gate_bank", 2)
        up = m.banks("up_bank", 2)
        down = m.banks("down_bank", QB)

        w_in = [m.sem(f"{k}_in") for k in ("gate", "up", "down")]
        router_in = m.sem("router_in")
        w_hi_ready = m.sem("w_hi_ready")
        w_ready = m.sem("w_ready")
        xturn_mm = m.sem("xturn_mm")
        xturn_hi = m.sem("xturn_hi")
        xturn_lo = m.sem("xturn_lo")
        logit_mm = m.sem("logit_mm")
        logit_scaled = m.sem("logit_scaled")
        exp_ready = m.sem("exp_ready")
        near_ready = m.sem("near_ready")
        gate_up_mm = m.sem("gate_up_mm")
        silu_ready = m.sem("silu_ready")
        h_ready = m.sem("h_ready")
        h_hi_ready = m.sem("h_hi_ready")
        h_split = m.sem("h_split")
        down_mm = m.sem("down_mm")
        down_added = m.sem("down_added")
        variance_ready = m.sem("variance2_ready")
        root_ready = m.sem("root2_ready")
        normed = m.sem("normed2")
        out_done = m.sem("out_done")
        dve_step = m.sem("expert_dve_step")
        block = stack.enter_context(nc.Block())
        SPLITS = 2 * KF + 1

        def split_slices():
            for f in range(KF):
                for which in (0, 1):
                    yield which, slice(f * P, (f + 1) * P)
            yield 2, slice(0, D)

        @block.sync
        def _(sp):
            views = [io[k].rearrange("e (k p) n -> e p k n", p=P) for k in ("w_g", "w_u", "w_d")]
            sp.dma_start(wr[:], io["w_router"].rearrange("(k p) e -> p k e", p=P)).then_inc(router_in, 16)
            sp.dma_start(temp[:], io["temperature"].partition_broadcast(P)).then_inc(router_in, 16)
            for i in range(3):
                sp.dma_start(raw[i][:], views[i][0]).then_inc(w_in[i], 16)
            with sp.Fori(1, E) as e:
                sp.wait_ge(w_ready, SPLITS * e - 1)
                for i in range(2):
                    sp.dma_start(raw[i][:], views[i][bass.ts(e, 1)].rearrange("e p k n -> (e p) k n")).then_inc(w_in[i], 16)
                sp.wait_ge(w_ready, SPLITS * e)
                sp.dma_start(raw[2][:], views[2][bass.ts(e, 1)].rearrange("e p k n -> (e p) k n")).then_inc(w_in[2], 16)
            out = io["out"].rearrange("b (t p) n -> p (b t) n", p=P)
            for b in range(B):
                sp.wait_ge(normed, b + 1)
                sp.dma_start(out[:, b * QB:(b + 1) * QB, :], g.res[:, b * QB:(b + 1) * QB, :]).then_inc(out_done, 16)
            sp.wait_ge(out_done, 16 * B)

        @block.tensor
        def _(pe):
            for t in range(NT):
                bank = down[t % QB]
                if t >= QB:
                    pe.wait_ge(xturn_lo, t - QB + 1)
                for k in range(KD):
                    last = nc.tensor.transpose(bank[:, k * P:(k + 1) * P], g.res[:, t, k * P:(k + 1) * P], g.ident[:])
                last.then_inc(xturn_mm, 1)
            pe.wait_ge(router_in, 32)
            pe.wait_ge(h_ready, 2)
            for t in range(NT):
                pe.wait_ge(xturn_lo, t + 1)
                for k in range(KD):
                    tile = slice(t * P, (t + 1) * P)
                    last = split_matmul(nc, gate[0][:, t * E:(t + 1) * E], x_hi[:, k, tile], x_lo[:, k, tile],
                                        wr_hi[:, k, :], wr_lo[:, k, :], k == 0, k == KD - 1)
            last.then_inc(logit_mm, 1)
            pe.wait_ge(logit_scaled, 1)
            with pe.Fori(0, E) as e:
                for b in range(B):
                    turn = B * e + b
                    tokens = slice(b * S, (b + 1) * S)
                    for f in range(KF):
                        n = KF * turn + f
                        if b == 0:
                            pe.wait_ge(w_ready, SPLITS * e + 2 * f + 2)
                        pe.wait_ge(h_ready, n - 1 + 2)
                        for which, bank in ((0, gate[f % 2]), (1, up[f % 2])):
                            for k in range(KD):
                                cols = slice(f * P, (f + 1) * P)
                                last = split_matmul(nc, bank[:], w_hi[which][:, k, cols], w_lo[which][:, k, cols],
                                                    x_hi[:, k, tokens], x_lo[:, k, tokens], k == 0, k == KD - 1)
                        last.then_inc(gate_up_mm, 1)
                    if b == 0:
                        pe.wait_ge(w_ready, SPLITS * (e + 1))
                    for part in (range(KF - 1), range(KF - 1, KF)):
                        pe.wait_ge(h_split, KF * turn + part[-1] + 1)
                        for t in range(QB):
                            for f in part:
                                last = split_matmul(nc, down[t][:], h_hi[:, f, t * P:(t + 1) * P],
                                                    h_lo[:, f, t * P:(t + 1) * P], w_hi[2][:, f, :], w_lo[2][:, f, :],
                                                    f == 0, f == KF - 1)
                            if part[-1] == KF - 1:
                                last.then_inc(down_mm, 1)

        @block.scalar
        def _(act):
            for t in range(NT):
                act.wait_ge(xturn_mm, t + 1)
                nc.scalar.activation(x_hi[:, :, t * P:(t + 1) * P],
                                     down[t % QB][:].rearrange("p (k n) -> p k n", k=KD), ACT.Copy).then_inc(xturn_hi, 1)
            def split(e, after):
                for i, (which, cols) in enumerate(split_slices()):
                    if i < 2:
                        act.wait_ge(w_in[which], 16 * (e + 1))
                    elif which == 2:
                        act.wait_ge(w_in[2], 16 * (e + 1))
                    if after is not None:
                        if which == 2:
                            act.wait_ge(down_mm, B * QB * e)
                        elif which == 0:
                            act.wait_ge(gate_up_mm, B * KF * e - KF + i // 2 + 1)
                    nc.scalar.activation(w_hi[which][:, :, cols], raw[which][:, :, cols],
                                         ACT.Copy).then_inc(w_hi_ready, 1)

            def silus(e, b):
                for f in range(KF):
                    n = KF * (B * e + b) + f
                    act.wait_ge(gate_up_mm, n + 1)
                    act.wait_ge(h_ready, n + 2)
                    nc.scalar.activation(silu[:], gate[f % 2][:], ACT.Silu).then_inc(silu_ready, 1)
                    act.wait_ge(h_ready, n + 3)
                    nc.scalar.activation(h_hi[:, f, :], h[:], ACT.Copy).then_inc(h_hi_ready, 1)

            split(0, None)
            act.wait_ge(logit_scaled, 1)
            nc.scalar.activation(r[1][:], r[0][:], ACT.Exp, scale=-1.0).then_inc(exp_ready, 1)
            act.wait_ge(near_ready, 1)
            nc.scalar.activation(r[1][:], r[0][:], ACT.Exp, scale=-1.0 / 0.1)
            nc.scalar.activation(r[2][:], r[0][:], ACT.Exp, scale=-1.0 / 0.3).then_inc(exp_ready, 1)

            with act.Fori(0, E - 1) as e:
                for b in range(B):
                    silus(e, b)
                split(e + 1, True)
            for b in range(B):
                silus(E - 1, b)
            for b in range(B):
                act.wait_ge(variance_ready, b + 1)
                nc.scalar.activation(inv[:, 0:QB], newton[:, 0:QB], ACT.Sqrt).then_inc(root_ready, 1)

        @block.vector
        def _(dve):
            chain = Chain(dve, dve_step)
            dve.wait_ge(router_in, 32)
            nc.vector.tensor_copy(wr_hi[:], wr[:]).then_inc(h_ready, 1)
            dve.wait_ge(h_ready, 1)
            nc.vector.tensor_tensor(wr_lo[:], wr[:], wr_hi[:].bitcast(F32), ALU.subtract).then_inc(h_ready, 1)
            chain.link(nc.vector.reciprocal(temp[:], temp[:]))
            for t in range(NT):
                dve.wait_ge(xturn_hi, t + 1)
                tile = slice(t * P, (t + 1) * P)
                nc.vector.tensor_tensor(x_lo[:, :, tile], down[t % QB][:].rearrange("p (k n) -> p k n", k=KD),
                                        x_hi[:, :, tile].bitcast(F32), ALU.subtract).then_inc(xturn_lo, 1)

            def split(e):
                for i, (which, cols) in enumerate(split_slices()):
                    dve.wait_ge(w_hi_ready, SPLITS * e + i + 1)
                    nc.vector.tensor_tensor(w_lo[which][:, :, cols], raw[which][:, :, cols],
                                            w_hi[which][:, :, cols].bitcast(F32), ALU.subtract).then_inc(w_ready, 1)

            split(0)
            dve.wait_ge(logit_mm, 1)
            nc.vector.tensor_scalar(r[0][:], gate[0][:, 0:NT * E].rearrange("p (t e) -> p t e", e=E), temp[:, 0:1],
                                    None, ALU.mult).then_inc(logit_scaled, 1)
            dve.wait_ge(exp_ready, 1)
            chain.link(nc.vector.tensor_scalar(r[1][:], r[1][:], 1.0, None, ALU.add))
            chain.link(nc.vector.reciprocal(r[2][:], r[1][:]))
            inside, zone, near = r[2], r[3], r[0]
            chain.link(nc.vector.tensor_scalar(zone[:], inside[:], lower, None, ALU.is_ge))
            chain.link(nc.vector.scalar_tensor_tensor(zone[:], inside[:], upper, zone[:], ALU.is_le, ALU.mult))
            chain.link(nc.vector.tensor_scalar(r[4][:], inside[:], centre, None, ALU.subtract))
            nc.vector.scalar_tensor_tensor(near[:], r[4][:], -1.0, r[4][:], ALU.mult, ALU.max).then_inc(near_ready, 1)
            dve.wait_ge(exp_ready, 2)
            wide, fallback = r[1], r[2]
            chain.link(nc.vector.tensor_tensor(weight[:], wide[:], zone[:], ALU.mult))
            rank, ahead = r[3], r[4]
            chain.link(nc.vector.memset(rank[:], 0.0))
            for i in range(E):
                one = fallback[:, :, i:i + 1]
                if i:
                    nc.vector.tensor_tensor(ahead[:, :, 0:i], one.to_broadcast([P, NT, i]), fallback[:, :, 0:i], ALU.is_gt)
                chain.link(nc.vector.tensor_tensor(ahead[:, :, i:E], one.to_broadcast([P, NT, E - i]),
                                                   fallback[:, :, i:E], ALU.is_ge))
                chain.link(nc.vector.tensor_tensor(rank[:], rank[:], ahead[:], ALU.add))
            chain.link(nc.vector.tensor_scalar(rank[:], rank[:], 2.5, None, ALU.is_le))
            chain.link(nc.vector.tensor_tensor(fallback[:], fallback[:], rank[:], ALU.mult))

            def row_scale(values, total):
                chain.link(nc.vector.tensor_scalar(rs[1][:], total[:], 1e-8, None, ALU.max))
                chain.link(nc.vector.reciprocal(rs[1][:], rs[1][:]))
                chain.link(nc.vector.tensor_tensor(values[:], values[:],
                                                   rs[1][:].unsqueeze(2).to_broadcast([P, NT, E]), ALU.mult))

            chain.link(nc.vector.tensor_reduce(rs[0][:], fallback[:], AX_X, ALU.add))
            row_scale(fallback, rs[0])
            chain.link(nc.vector.tensor_reduce(rs[0][:], weight[:], AX_X, ALU.add))
            none = rs[2]
            chain.link(nc.vector.tensor_scalar(none[:], rs[0][:], 1e-8, None, ALU.is_lt))
            chain.link(nc.vector.tensor_tensor(fallback[:], fallback[:], none[:].unsqueeze(2).to_broadcast([P, NT, E]),
                                               ALU.mult))
            chain.link(nc.vector.tensor_scalar(none[:], none[:], -1.0, 1.0, ALU.mult, ALU.add))
            chain.link(nc.vector.tensor_tensor(weight[:], weight[:], none[:].unsqueeze(2).to_broadcast([P, NT, E]),
                                               ALU.mult))
            chain.link(nc.vector.tensor_tensor(weight[:], weight[:], fallback[:], ALU.add))
            chain.link(nc.vector.tensor_reduce(rs[0][:], weight[:], AX_X, ALU.add))
            row_scale(weight, rs[0])

            def batches(e):
                for b in range(B):
                    turn = B * e + b
                    for f in range(KF):
                        n = KF * turn + f
                        dve.wait_ge(silu_ready, n + 1)
                        nc.vector.tensor_tensor(h[:], up[f % 2][:], silu[:], ALU.mult).then_inc(h_ready, 1)
                        dve.wait_ge(h_hi_ready, n + 1)
                        nc.vector.tensor_tensor(h_lo[:, f, :], h[:], h_hi[:, f, :].bitcast(F32),
                                                ALU.subtract).then_inc(h_split, 1)
                        dve.wait_ge(h_split, n + 1)
                    for t in range(QB):
                        tile = b * QB + t
                        dve.wait_ge(down_mm, QB * turn + t + 1)
                        row = g.res[:, tile, :]
                        nc.vector.scalar_tensor_tensor(row, down[t][:], weight[:, tile, bass.ds(e, 1)], row,
                                                       ALU.mult, ALU.add).then_inc(down_added, 1)

            with dve.Fori(0, E - 1) as e:
                batches(e)
                split(e + 1)
            batches(E - 1)
            dve.wait_ge(down_added, QB * B * E)
            for b in range(B):
                last = norm_rows(nc, dve, chain, g.carry, lambda t: g.res[:, b * QB + t, :], QB, stats, mean_var, inv, newton,
                                 variance_ready, root_ready, b + 1)
                chain.link(last)
                dve.sem_inc(normed, 1)


def build(nc, io):
    with ExitStack() as stack:
        m = Space(nc, stack)

        class g:
            res = m.sb("res", [P, NT, D])
            ident = m.sb("ident", [P, P])
            ident_b = m.sb("ident_b", [P, P], BF16)
            mask = m.sb("mask", [P, P], BF16)
            ones = m.sb("ones", [P, P])
            carry = m.sb("carry", [P, 2])

        with ExitStack() as inner:
            a = Space(nc, inner)
            g.cos = a.sb("cos", [P, S])
            g.sin = a.sb("sin", [P, S])
            g.q_gain = a.sb("q_gain", [P, KQ])
            g.qn_hi = a.sb("qn_hi", [P, KQ, B * S], F32R)
            g.qn_lo = a.sb("qn_lo", [P, KQ, B * S], F32R)
            g.key_hi = a.sb("key_hi", [P, B * S], F32R)
            g.key_lo = a.sb("key_lo", [P, B * S], F32R)
            g.kr_hi = a.sb("kr_hi", [P, B * S], F32R)
            g.kr_lo = a.sb("kr_lo", [P, B * S], F32R)
            g.val_hi = a.sb("val_hi", [P, NT, KL], F32R)
            g.val_lo = a.sb("val_lo", [P, NT, KL], F32R)
            latent_phase(nc, g, io)
            attention_phase(nc, g, io)
        quant_phase(nc, g, io)
        expert_phase(nc, g, io)


def rotary_order():
    half = ROPE // 2
    return np.concatenate([np.r_[q * 16:q * 16 + 16, half + q * 16:half + q * 16 + 16] for q in range(2)])


def shape_constants():
    order = rotary_order()
    inv_freq = (1.0 / np.float32(10000.0) ** (np.arange(0, ROPE, 2, dtype=np.float32) / np.float32(ROPE)))
    angle = np.outer(np.arange(S, dtype=np.float32), inv_freq.astype(np.float32)).astype(np.float32)
    angle = np.concatenate([angle, angle], -1)[:, order].T
    sign = np.where(order < ROPE // 2, -1.0, 1.0).astype(np.float32)[:, None]
    cos, sin = np.cos(angle), np.sin(angle) * sign
    mask = np.where(np.tril(np.ones((P, P), bool)), 0.0, MASKED)
    return {
        "cos": np.concatenate([cos, cos], 0).astype(np.float32),
        "sin": np.concatenate([sin, sin], 0).astype(np.float32),
        "mask": mask.astype(np.float32),
        "ident": np.eye(P, dtype=np.float32),
        "ones": np.ones((P, P), np.float32),
    }


def lay_out(inputs):
    a = {k: np.asarray(v) for k, v in inputs.items()}
    order = rotary_order()
    x = a["x"]
    wq = a["L0_attn_q_b_w"].reshape(H, NOPE + ROPE, QL)
    wkva = a["L0_attn_kv_a_w"]
    w_kr = wkva[KL:][order].T
    arrays = {
        "x": x,
        "x_t": x.transpose(0, 2, 1),
        "w_a": np.concatenate([a["L0_attn_q_a_w"], wkva[:KL]], 0).T,
        "w_kr": np.concatenate([w_kr, w_kr], 1),
        "q_ln": a["L0_attn_q_a_ln_w"].reshape(KQ, P).T,
        "kv_ln": a["L0_attn_kv_a_ln_w"],
        "wq_nope": wq[:, :NOPE],
        "wq_rope_t": wq[:, NOPE:][:, order].reshape(H * ROPE, QL).T,
        "w_kv": a["L0_attn_kv_b_w"].reshape(H, NOPE + VD, KL),
        "w_o_t": a["L0_attn_o_w"].T,
        "w_gate_up": a["fside_BxS2xS2_0"],
        "w_down": a["ctx_1024"],
        "w_g": a["L0_ffn_Wg"],
        "w_u": a["L0_ffn_Wu"],
        "w_d": a["L0_ffn_Wd"],
        "w_router": a["L0_ffn_Wr"],
        "temperature": a["L0_ffn_temperature"],
    }
    return {k: np.ascontiguousarray(v) for k, v in {**arrays, **shape_constants()}.items()}


def kernel(**inputs):
    import concourse.bacc as bacc
    from concourse.bass_utils import run_bass_kernel_spmd

    nc = bacc.Bacc("TRN2", target_bir_lowering=False, num_devices=1)
    arrays = lay_out(inputs)
    io = {k: nc.dram_tensor(f"in_{k}", v.shape, mybir.dt.from_np(v.dtype), kind="ExternalInput").ap()
          for k, v in arrays.items()}
    io["out"] = nc.dram_tensor("out_y", (B, S, D), F32, kind="ExternalOutput").ap()
    build(nc, io)
    result = run_bass_kernel_spmd(nc, [{f"in_{k}": v for k, v in arrays.items()}], core_ids=[0])
    return result.results[0]["out_y"]
```

```python
from contextlib import ExitStack

import numpy as np

import concourse.bass as bass
from concourse import mybir

F32 = mybir.dt.float32
F32R = mybir.dt.float32r
BF16 = mybir.dt.bfloat16
I32 = mybir.dt.int32
ALU = mybir.AluOpType
ACT = mybir.ActivationFunctionType
AX_X = mybir.AxisListType.X

P = 128
B, S, D = 4, 512, 512
H, NOPE, ROPE, VD = 16, 128, 64, 128
QL, KL = 384, 128
QB = S // P
NT = B * QB
KD = D // P
KQ = QL // P
NP = H // 2
E, FF = 8, 512
KF = FF // P
INNER = 256
RMS_EPS, LN_EPS, Q_EPS, QMAX = 1e-6, 1e-5, 1e-6, 127.0
SCALE = float(NOPE + ROPE) ** -0.5
MASKED = -1e30
ROUND = 1.5 * 2.0 ** 23
SWAP = [(i + 16) % 32 for i in range(32)]
SEEN = [(q + 1) * P for q in range(QB)]


def past(engine, semaphore, count):
    if not (isinstance(count, int) and count == 0):
        engine.wait_ge(semaphore, count)


class Chain:

    def __init__(self, engine, semaphore, base=0):
        self.engine, self.semaphore, self.base, self.n = engine, semaphore, base, 0

    def link(self, instruction):
        self.n += 1
        instruction.then_inc(self.semaphore, 1)
        self.engine.wait_ge(self.semaphore, self.base + self.n)


class Space:

    def __init__(self, nc, stack):
        self.nc, self.stack = nc, stack

    def sb(self, name, shape, dtype=F32):
        return self.stack.enter_context(self.nc.sbuf_tensor(name, shape, dtype))

    def psum(self, name, shape, dtype=F32):
        return self.stack.enter_context(self.nc.psum_tensor(name, shape, dtype))

    def sem(self, name):
        return self.stack.enter_context(self.nc.semaphore(name))

    def banks(self, name, n):
        return [self.psum(f"{name}{i}", [P, 512]) for i in range(n)]


def split_matmul(nc, out, w_hi, w_lo, x_hi, x_lo, start, stop):
    nc.tensor.matmul(out, w_hi, x_hi, start=start, stop=False)
    nc.tensor.matmul(out, w_hi, x_lo, start=False, stop=False)
    return nc.tensor.matmul(out, w_lo, x_hi, start=False, stop=stop)


def latent_phase(nc, g, io):
    with ExitStack() as stack:
        m = Space(nc, stack)
        mask_in = m.sb("mask_in", [P, P])
        x_t = m.sb("x_t", [P, KD, S])
        x_hi = m.sb("x_hi", [P, KD, S], F32R)
        x_lo = m.sb("x_lo", [P, KD, S], F32R)
        wa = m.sb("wa", [P, KD, QL + KL])
        wa_hi = m.sb("wa_hi", [P, KD, QL + KL], F32R)
        wa_lo = m.sb("wa_lo", [P, KD, QL + KL], F32R)
        wr = m.sb("wkr", [P, KD, P])
        wr_hi = m.sb("wkr_hi", [P, KD, P], F32R)
        wr_lo = m.sb("wkr_lo", [P, KD, P], F32R)
        junk = m.sb("square_junk", [P, QB, QL + KL], BF16)
        latent = m.sb("latent", [P, QB, QL + KL])
        ssq = m.sb("ssq", [P, QB, 2])
        ms = m.sb("ms", [P, QB, 2])
        rms = m.sb("rms", [P, QB, 2])
        rstd = m.sb("rstd", [P, QB, 2])
        nt = m.sb("newton", [P, QB, 2])
        kv_gain = m.sb("kv_gain", [P, KL])
        rot = m.sb("krot", [P, S])
        rot_swapped = m.sb("krot_swapped", [P, S])
        product = m.banks("latent_bank", QB)
        rotary = m.psum("rotary_bank", [P, 512])
        turned = m.banks("turned_bank", 3)

        weights_in = m.sem("weights_in")
        consts_in = m.sem("consts_in")
        x_in = m.sem("x_in")
        w_split = m.sem("w_split")
        x_split_hi = m.sem("x_split_hi")
        x_split = m.sem("x_split")
        lat_mm = m.sem("lat_mm")
        rot_mm = m.sem("rot_mm")
        squared = m.sem("squared")
        mean_ready = m.sem("mean_ready")
        root_ready = m.sem("root_ready")
        normed = m.sem("normed")
        turn_mm = m.sem("turn_mm")
        turn_hi = m.sem("turn_hi")
        turn_lo = m.sem("turn_lo")
        values_done = m.sem("values_done")
        rot_read = m.sem("rot_read")
        rot_ready = m.sem("rot_ready")
        rot_hi_ready = m.sem("rot_hi_ready")
        rot_split = m.sem("rot_split")
        pool_step = m.sem("lat_pool_step")
        dve_step = m.sem("lat_dve_step")
        block = stack.enter_context(nc.Block())

        @block.sync
        def _(sp):
            sp.dma_start(wa[:], io["w_a"].rearrange("(k p) n -> p k n", p=P)).then_inc(weights_in, 16)
            sp.dma_start(wr[:], io["w_kr"].rearrange("(k p) n -> p k n", p=P)).then_inc(weights_in, 16)
            xt_view = io["x_t"].rearrange("b (k p) n -> b p k n", p=P)
            sp.dma_start(x_t[:], xt_view[0]).then_inc(x_in, 16)
            for dst, name in ((g.ident, "ident"), (mask_in, "mask"), (g.cos, "cos"), (g.sin, "sin"), (g.ones, "ones")):
                sp.dma_start(dst[:], io[name]).then_inc(consts_in, 16)
            sp.dma_start(kv_gain[:], io["kv_ln"].partition_broadcast(P)).then_inc(consts_in, 16)
            sp.dma_start(g.q_gain[:], io["q_ln"]).then_inc(consts_in, 16)
            sp.dma_start(g.res[:], io["x"].rearrange("b (t p) n -> p (b t) n", p=P)).then_inc(consts_in, 16)
            with sp.Fori(1, B) as b:
                sp.wait_ge(x_split, b)
                sp.dma_start(x_t[:], xt_view[bass.ts(b, 1)].rearrange("b p k n -> (b p) k n")).then_inc(x_in, 16)
            sp.wait_ge(consts_in, 8 * 16)

        @block.scalar
        def _(act):
            act.wait_ge(weights_in, 32)
            nc.scalar.activation(wa_hi[:], wa[:], ACT.Copy).then_inc(w_split, 1)
            nc.scalar.activation(wr_hi[:], wr[:], ACT.Copy).then_inc(w_split, 1)
            with act.Fori(0, B) as b:
                act.wait_ge(x_in, (b + 1) * 16)
                nc.scalar.activation(x_hi[:], x_t[:], ACT.Copy).then_inc(x_split_hi, 1)
                for t in range(QB):
                    act.wait_ge(lat_mm, QB * b + t + 1)
                    nc.scalar.activation(junk[:, t, 0:QL], product[t][:, 0:QL], ACT.Square,
                                         accum_out=ssq[:, t, 0:1])
                    nc.scalar.activation(junk[:, t, QL:], product[t][:, QL:QL + KL], ACT.Square,
                                         accum_out=ssq[:, t, 1:2]).then_inc(squared, 1)
                act.wait_ge(mean_ready, b + 1)
                nc.scalar.activation(rms[:], ms[:], ACT.Sqrt).then_inc(root_ready, 1)
                for c in range(KQ + 1):
                    act.wait_ge(turn_mm, (KQ + 1) * b + c + 1)
                    bank = turned[c % 3]
                    dst = g.qn_hi[:, c, bass.ts(b, S)] if c < KQ else g.key_hi[:, bass.ts(b, S)]
                    nc.scalar.activation(dst, bank[:], ACT.Copy).then_inc(turn_hi, 1)
                act.wait_ge(rot_ready, b + 1)
                nc.scalar.activation(g.kr_hi[:, bass.ts(b, S)], rot[:], ACT.Copy).then_inc(rot_hi_ready, 1)

        @block.vector
        def _(dve):
            start = Chain(dve, dve_step)
            dve.wait_ge(w_split, 2)
            nc.vector.tensor_tensor(wa_lo[:], wa[:], wa_hi[:].bitcast(F32), ALU.subtract).then_inc(w_split, 1)
            nc.vector.tensor_tensor(wr_lo[:], wr[:], wr_hi[:].bitcast(F32), ALU.subtract).then_inc(w_split, 1)
            dve.wait_ge(consts_in, 8 * 16)
            nc.vector.tensor_copy(g.ident_b[:], g.ident[:])
            nc.vector.tensor_copy(g.mask[:], mask_in[:])
            start.link(nc.vector.tensor_scalar(g.q_gain[:], g.q_gain[:], SCALE, None, ALU.mult))
            STEPS = 7
            with dve.Fori(0, B) as b:
                chain = Chain(dve, dve_step, b * STEPS + 1)
                dve.wait_ge(x_split_hi, b + 1)
                nc.vector.tensor_tensor(x_lo[:], x_t[:], x_hi[:].bitcast(F32), ALU.subtract).then_inc(x_split, 1)
                dve.wait_ge(squared, QB * (b + 1))
                nc.vector.tensor_scalar(ms[:, :, 0], ssq[:, :, 0], 1.0 / QL, RMS_EPS, ALU.mult, ALU.add)
                chain.link(nc.vector.tensor_scalar(ms[:, :, 1], ssq[:, :, 1], 1.0 / KL, RMS_EPS, ALU.mult, ALU.add))
                chain.link(nc.vector.tensor_copy(nt[:], ms[:]))
                dve.sem_inc(mean_ready, 1)
                dve.wait_ge(root_ready, b + 1)
                chain.link(nc.vector.reciprocal(rstd[:], rms[:]))
                chain.link(nc.vector.tensor_tensor(nt[:], nt[:], rstd[:], ALU.mult))
                chain.link(nc.vector.tensor_tensor(nt[:], nt[:], rstd[:], ALU.mult))
                chain.link(nc.vector.tensor_scalar(nt[:], nt[:], -0.5, 1.5, ALU.mult, ALU.add))
                chain.link(nc.vector.tensor_tensor(rstd[:], rstd[:], nt[:], ALU.mult))
                assert chain.n == STEPS
                for t in range(QB):
                    nc.vector.tensor_scalar(latent[:, t, 0:QL], product[t][:, 0:QL], rstd[:, t, 0:1],
                                            None, ALU.mult)
                    nc.vector.scalar_tensor_tensor(latent[:, t, QL:], product[t][:, QL:], rstd[:, t, 1:2],
                                                   kv_gain[:], ALU.mult, ALU.mult).then_inc(normed, 1)
                dve.wait_ge(normed, QB * (b + 1))
                value = latent[:, :, QL:]
                nc.vector.tensor_copy(g.val_hi[:, bass.ts(b, QB), :], value).then_inc(values_done, 1)
                dve.wait_ge(values_done, 2 * b + 1)
                nc.vector.tensor_tensor(g.val_lo[:, bass.ts(b, QB), :], value,
                                        g.val_hi[:, bass.ts(b, QB), :].bitcast(F32),
                                        ALU.subtract).then_inc(values_done, 1)
                dve.wait_ge(rot_mm, b + 1)
                nc.vector.tensor_tensor(rot[:], rotary[:], g.cos[:], ALU.mult)
                nc.vector.stream_shuffle(rot_swapped[:], rotary[:], SWAP).then_inc(rot_read, 1)
                for c in range(KQ + 1):
                    dve.wait_ge(turn_hi, (KQ + 1) * b + c + 1)
                    bank = turned[c % 3]
                    hi, lo = ((x[:, c, bass.ts(b, S)] for x in (g.qn_hi, g.qn_lo)) if c < KQ
                              else (x[:, bass.ts(b, S)] for x in (g.key_hi, g.key_lo)))
                    nc.vector.tensor_tensor(lo, bank[:], hi.bitcast(F32), ALU.subtract).then_inc(turn_lo, 1)
                dve.wait_ge(rot_hi_ready, b + 1)
                nc.vector.tensor_tensor(g.kr_lo[:, bass.ts(b, S)], rot[:], g.kr_hi[:, bass.ts(b, S)].bitcast(F32),
                                        ALU.subtract).then_inc(rot_split, 1)
                dve.wait_ge(rot_split, b + 1)

        @block.gpsimd
        def _(pool):
            pool.wait_ge(consts_in, 8 * 16)
            with pool.Fori(0, B) as b:
                pool.wait_ge(rot_read, b + 1)
                nc.gpsimd.tensor_tensor(rot_swapped[:], rot_swapped[:], g.sin[:], ALU.mult).then_inc(pool_step, 1)
                pool.wait_ge(pool_step, b + 1)
                nc.gpsimd.tensor_tensor(rot[:], rot[:], rot_swapped[:], ALU.add).then_inc(rot_ready, 1)

        @block.tensor
        def _(pe):
            pe.wait_ge(w_split, 4)
            pe.wait_ge(consts_in, 8 * 16)
            with pe.Fori(0, B) as b:
                pe.wait_ge(x_split, b + 1)
                for t in range(QB):
                    for k in range(KD):
                        last = split_matmul(nc, product[t][:], x_hi[:, k, t * P:(t + 1) * P],
                                            x_lo[:, k, t * P:(t + 1) * P], wa_hi[:, k, :], wa_lo[:, k, :],
                                            k == 0, k == KD - 1)
                    last.then_inc(lat_mm, 1)
                for k in range(KD):
                    last = split_matmul(nc, rotary[:], wr_hi[:, k, :], wr_lo[:, k, :], x_hi[:, k, :],
                                        x_lo[:, k, :], k == 0, k == KD - 1)
                last.then_inc(rot_mm, 1)
                pe.wait_ge(normed, QB * (b + 1))
                for c in range(KQ + 1):
                    if c == 3:
                        pe.wait_ge(turn_lo, (KQ + 1) * b + 1)
                    for t in range(QB):
                        last = nc.tensor.transpose(turned[c % 3][:, t * P:(t + 1) * P],
                                                   latent[:, t, c * P:(c + 1) * P], g.ident[:])
                    last.then_inc(turn_mm, 1)


def attention_phase(nc, g, io):
    NS = 2 * B
    with ExitStack() as stack:
        m = Space(nc, stack)
        raw_q = m.sb("raw_q", [P, 2, QL])
        raw_k = m.sb("raw_k", [P, 2, KL])
        raw_r = m.sb("raw_r", [P, KQ, P])
        raw_v = m.sb("raw_v", [P, 2, KL])
        raw_o = m.sb("raw_o", [P, 2, D])
        wq_hi = m.sb("wq_hi", [P, 2, KQ, KL], F32R)
        wq_lo = m.sb("wq_lo", [P, 2, KQ, KL], F32R)
        wr_hi = m.sb("wr_hi", [P, KQ, P], F32R)
        wr_lo = m.sb("wr_lo", [P, KQ, P], F32R)
        wo_hi = m.sb("wo_hi", [P, 2, D], F32R)
        wo_lo = m.sb("wo_lo", [P, 2, D], F32R)
        q_hi = m.sb("q_hi", [P, S], F32R)
        q_lo = m.sb("q_lo", [P, S], F32R)
        rot = m.sb("qrot", [P, S])
        rot_swapped = m.sb("qrot_swapped", [P, S])
        qr = m.sb("qr_stacked", [P, 2, S], F32R)
        probs = m.sb("probs", [P, 2, sum(SEEN)])
        neg_max = m.sb("neg_max", [P, 2, QB])
        row_sum = m.sb("row_sum", [P, 2, QB])
        row_inv = m.sb("row_inv", [P, 2, QB])
        pt_hi = m.sb("pt_hi", [P, sum(SEEN)], F32R)
        pt_lo = m.sb("pt_lo", [P, sum(SEEN)], F32R)
        mix_hi = m.sb("mix_hi", [P, 2, S], F32R)
        mix_lo = m.sb("mix_lo", [P, 2, S], F32R)
        score = m.banks("score_bank", 3)
        turned = m.banks("prob_bank", 2)
        front = m.psum("front_bank", [P, 512])
        mixed = m.psum("mixed_bank", [P, 512])
        outp = m.psum("out_bank", [P, 512])

        GROUPS = ((3,), (2, 0), (1,))
        NG = len(GROUPS)

        def score_at(q):
            bank, at = {3: (0, 0), 2: (1, 0), 0: (1, 3 * P), 1: (2, 0)}[q]
            return score[bank][:, at:at + SEEN[q]]

        def probs_at(h, q, start, size):
            at = sum(SEEN[:q]) + start
            return probs[:, h, at:at + size]

        def pt_at(x, k):
            at = sum(S - i * P for i in range(k))
            return x[:, at:at + S - k * P]

        def turned_at(k):
            bank, at = {0: (turned[0], 0), 1: (turned[1], 0), 3: (turned[1], 3 * P), 2: (score[2], 2 * P)}[k]
            return bank[:, at:at + S - k * P]

        fold_in = m.sem("fold_in")
        rope_in = m.sem("rope_in")
        outw_in = m.sem("outw_in")
        front_mm = m.sem("front_mm")
        outw_hi = m.sem("outw_hi")
        q_hi_ready = m.sem("q_hi_ready")
        q_ready = m.sem("q_ready")
        wq_ready = m.sem("wq_ready")
        wr_ready = m.sem("wr_ready")
        wo_ready = m.sem("wo_ready")
        rope_read = m.sem("rope_read")
        rope_swapped = m.sem("rope_swapped")
        rope_turned = m.sem("rope_turned")
        rope_hi = m.sem("rope_hi")
        rope_ready = m.sem("rope_ready")
        score_mm = m.sem("score_mm")
        max_ready = m.sem("max_ready")
        exp_done = m.sem("exp_done")
        inv_ready = m.sem("inv_ready")
        probs_ready = m.sem("probs_ready")
        turn_mm = m.sem("pturn_mm")
        turn_hi = m.sem("pturn_hi")
        turn_lo = m.sem("pturn_lo")
        mix_mm = m.sem("mix_mm")
        mix_hi_ready = m.sem("mix_hi_ready")
        mix_ready = m.sem("mix_ready")
        out_mm = m.sem("out_mm")
        out_added = m.sem("out_added")
        split_step = m.sem("split_step")
        block = stack.enter_context(nc.Block())

        FRONT = 16

        def front_uses(s, last):
            uses = [("rope", s // 2 + 1)] if s % 2 and not (last and s == NS - 1) else []
            if not (last and s == NS - 1):
                uses.append(("query", s + 1))
            if s in (1, 2):
                uses.append(("outw", s - 1))
            if s in (6, 7) and not last:
                uses.append(("wq", s - 6))
            return uses

        def front_index(s, last):
            return 4 + sum(len(front_uses(i, False)) for i in range(s))

        PROLOGUE = [("wq", 0), ("rope", 0), ("query", 0), ("wq", 1)]

        @block.sync
        def _(sp):
            wq_n = io["wq_nope"].rearrange("h d c -> d h c")
            wk_n = io["w_kv"][:, 0:NOPE, :].rearrange("h d c -> d h c")
            wv_n = io["w_kv"][:, NOPE:, :].rearrange("h d c -> d h c")
            wo_n = io["w_o_t"].rearrange("(h p) n -> p h n", p=P)
            wr_n = io["wq_rope_t"].rearrange("(k p) n -> p k n", p=P)

            def load_queries(p):
                sp.dma_start(raw_q[:], wq_n[:, bass.ts(p, 2), :]).then_inc(fold_in, 16)
                sp.dma_start(raw_k[:], wk_n[:, bass.ts(p, 2), :]).then_inc(fold_in, 16)
                sp.dma_start(raw_r[:], wr_n[:, :, bass.ts(p, P)]).then_inc(rope_in, 16)

            def load_outputs(p):
                sp.dma_start(raw_v[:], wv_n[:, bass.ts(p, 2), :]).then_inc(outw_in, 16)
                sp.dma_start(raw_o[:], wo_n[:, bass.ts(p, 2), :]).then_inc(outw_in, 16)

            load_queries(0)
            load_outputs(0)
            with sp.Fori(1, NP) as p:
                sp.wait_ge(wq_ready, 2 * p)
                sp.wait_ge(wr_ready, p)
                load_queries(p)
                sp.wait_ge(wo_ready, 2 * p)
                load_outputs(p)

        def over_pairs(engine, pair):
            pair(0, True, False)
            with engine.Fori(1, NP - 1) as p:
                pair(p, False, False)
            pair(NP - 1, False, True)

        @block.tensor
        def _(pe):
            before = [None]

            def front_one(p, kind, a):
                if before[0]:
                    p0, kind0, a0 = before[0]
                    read, count = {"wq": (wq_ready, 2), "outw": (wo_ready, 2), "rope": (rope_read, B),
                                   "query": (q_ready, NS)}[kind0]
                    pe.wait_ge(read, count * p0 + a0 + 1)
                before[0] = (p, kind, a)
                if kind == "wq":
                    pe.wait_ge(fold_in, (p + 1) * 32)
                    for c in range(KQ):
                        last = nc.tensor.matmul(front[:, c * KL:(c + 1) * KL], raw_q[:, a, c * P:(c + 1) * P],
                                                raw_k[:, a, :], start=True, stop=True)
                elif kind == "outw":
                    pe.wait_ge(outw_in, (p + 1) * 32)
                    last = nc.tensor.matmul(front[:], raw_v[:, a, :], raw_o[:, a, :], start=True, stop=True)
                elif kind == "rope":
                    if a % B == 0:
                        pe.wait_ge(wr_ready, p + 1)
                    b = a % B
                    for c in range(KQ):
                        last = split_matmul(nc, front[:], wr_hi[:, c, :], wr_lo[:, c, :],
                                            g.qn_hi[:, c, b * S:(b + 1) * S], g.qn_lo[:, c, b * S:(b + 1) * S],
                                            c == 0, c == KQ - 1)
                else:
                    h, b = a % 2, a // 2
                    if b == 0:
                        pe.wait_ge(wq_ready, 2 * p + h + 1)
                    for c in range(KQ):
                        last = split_matmul(nc, front[:], wq_hi[:, h, c, :], wq_lo[:, h, c, :],
                                            g.qn_hi[:, c, b * S:(b + 1) * S], g.qn_lo[:, c, b * S:(b + 1) * S],
                                            c == 0, c == KQ - 1)
                last.then_inc(front_mm, 1)

            def place(p, kind, a):
                if kind == "wq":
                    return p + 1, kind, a
                if (kind == "rope" and a == B) or (kind == "query" and a == NS):
                    return p + 1, kind, 0
                return p, kind, a

            def scores(p, s):
                b, h = s // 2, s % 2
                pe.wait_ge(q_ready, NS * p + s + 1)
                pe.wait_ge(rope_ready, B * p + b + 1)
                past(pe, exp_done, NG * (NS * p + s))
                for q in [q for group in GROUPS for q in group]:
                    n, tile = SEEN[q], slice(q * P, (q + 1) * P)
                    out = score_at(q)
                    keys = slice(b * S, b * S + n)
                    split_matmul(nc, out, q_hi[:, tile], q_lo[:, tile], g.key_hi[:, keys], g.key_lo[:, keys],
                                 True, False)
                    nc.tensor.matmul(out, qr[:, h, tile], g.kr_hi[:, keys], start=False, stop=False)
                    nc.tensor.matmul(out, qr[:, h, tile], g.kr_lo[:, keys], start=False, stop=False)
                    last = nc.tensor.matmul(out[:, q * P:n], g.ident_b[:], g.mask[:], start=False, stop=True)
                    if q != 2:
                        last.then_inc(score_mm, 1)

            def turn(j, s, parts, scored=0):
                h = s % 2
                if 0 in parts:
                    pe.wait_ge(probs_ready, j + 1)
                    past(pe, turn_lo, 3 * j)
                if 2 in parts:
                    pe.wait_ge(exp_done, scored)
                for k in parts:
                    for q in range(k, QB):
                        last = nc.tensor.transpose(turned_at(k)[:, (q - k) * P:(q - k + 1) * P],
                                                   probs_at(h, q, k * P, P), g.ident[:])
                    if k != 1:
                        last.then_inc(turn_mm, 1)

            def mix(j, s, n_out):
                b = s // 2
                past(pe, mix_ready, j)
                if n_out is not None:
                    pe.wait_ge(out_added, n_out)
                for i, (k, ready) in enumerate(((0, 1), (1, 2), (3, 2), (2, 3))):
                    pe.wait_ge(turn_lo, 3 * j + ready)
                    t = b * QB + k
                    last = split_matmul(nc, mixed[:, k * P:S], g.val_hi[:, t, :], g.val_lo[:, t, :],
                                        pt_at(pt_hi, k), pt_at(pt_lo, k), i == 0, i == QB - 1)
                last.then_inc(mix_mm, 1)

            def project(n, tiles):
                for t in tiles:
                    if t == 0:
                        pe.wait_ge(mix_ready, 2 * n + 2)
                        past(pe, out_added, QB * n)
                    bank = outp if t % 2 == 0 else mixed
                    if t >= 2:
                        pe.wait_ge(out_added, QB * n + t - 1)
                    for h in range(2):
                        last = split_matmul(nc, bank[:], mix_hi[:, h, t * P:(t + 1) * P],
                                            mix_lo[:, h, t * P:(t + 1) * P], wo_hi[:, h, :], wo_lo[:, h, :],
                                            h == 0, h == 1)
                    last.then_inc(out_mm, 1)

            def pair(p, first, last):
                for s in range(NS):
                    j = NS * p + s
                    back = not (first and s == 0)
                    uses = [place(p, *u) for u in front_uses(s, last)]
                    if s == 0:
                        before[0] = (p, "wq", 1)
                    scores(p, s)
                    if s % 2 == 0:
                        if back:
                            turn(j - 1, (s - 1) % NS, (0, 1, 3))
                        front_one(*uses[0])
                        if back:
                            turn(j - 1, (s - 1) % NS, (2,), NG * (j + 1))
                            mix(j - 1, (s - 1) % NS, None)
                        rest = 1
                    else:
                        n = B * p + s // 2 - 1
                        out = not (first and s == 1)
                        rest = 0
                        if uses and uses[0][1] == "rope":
                            front_one(*uses[0])
                            rest = 1
                        turn(j - 1, s - 1, (0, 1, 3))
                        if out:
                            if s == 3:
                                pe.wait_ge(wo_ready, 2 * p + 2)
                            project(n, (0, 1))
                        turn(j - 1, s - 1, (2,), NG * (j + 1))
                        if out:
                            project(n, (2, 3))
                        if len(uses) > rest and uses[rest][1] == "query":
                            front_one(*uses[rest])
                            rest += 1
                        mix(j - 1, s - 1, QB * (n + 1) if out else None)
                    for i in range(rest, len(uses)):
                        front_one(*uses[i])

            for i, (kind, a) in enumerate(PROLOGUE):
                front_one(0, kind, a)
            over_pairs(pe, pair)
            j = NS * NP - 1
            turn(j, NS - 1, (0, 1, 3, 2), NG * (j + 1))
            mix(j, NS - 1, QB * (B * NP - 1))
            project(B * NP - 1, range(QB))

        @block.scalar
        def _(act):
            def front_one(kind, p, a, index):
                if kind == "outw":
                    act.wait_ge(front_mm, index + 1)
                    nc.scalar.activation(wo_hi[:, a, :], front[:], ACT.Copy).then_inc(outw_hi, 1)
                elif kind == "query":
                    act.wait_ge(front_mm, index + 1)
                    nc.scalar.activation(q_hi[:], front[:], ACT.Copy).then_inc(q_hi_ready, 1)
                elif kind == "rope":
                    act.wait_ge(rope_turned, B * p + a + 1)
                    nc.scalar.activation(qr[0:64, 0, :], rot[0:64, :], ACT.Copy)
                    nc.scalar.activation(qr[64:P, 1, :], rot[64:P, :], ACT.Copy).then_inc(rope_hi, 1)

            def softmax(j, h, first_two):
                if not first_two:
                    act.wait_ge(turn_mm, 3 * (j - 1))
                for i, group in enumerate(GROUPS):
                    act.wait_ge(max_ready, NG * j + i + 1)
                    for q in group:
                        last = nc.scalar.activation(probs_at(h, q, 0, SEEN[q]), score_at(q), ACT.Exp,
                                                    bias=neg_max[:, h, q:q + 1], accum_out=row_sum[:, h, q:q + 1])
                    last.then_inc(exp_done, 1)

            def turn(j, parts):
                for i in parts:
                    act.wait_ge(turn_mm, 3 * j + i + 1)
                    for k in ((0,), (1, 3), (2,))[i]:
                        last = nc.scalar.activation(pt_at(pt_hi, k), turned_at(k), ACT.Copy)
                    last.then_inc(turn_hi, 1)

            def mix(j, h):
                act.wait_ge(mix_mm, j + 1)
                nc.scalar.activation(mix_hi[:, h, :], mixed[:], ACT.Copy).then_inc(mix_hi_ready, 1)

            def pair(p, first, last):
                for s in range(NS):
                    j = NS * p + s
                    back = not (first and s == 0)
                    uses = front_uses(s, last)
                    index = FRONT * p + front_index(s, last)
                    softmax(j, s % 2, first and s < 2)
                    if back:
                        turn(j - 1, (0, 1))
                        if s % 2:
                            turn(j - 1, (2,))
                    for i, (kind, a) in enumerate(uses):
                        if kind in ("rope", "query"):
                            front_one(kind, p, a, index + i)
                    if back:
                        if s % 2 == 0:
                            turn(j - 1, (2,))
                        mix(j - 1, (s - 1) % 2)
                    for i, (kind, a) in enumerate(uses):
                        if kind == "outw":
                            front_one(kind, p, a, index + i)

            for i, (kind, a) in enumerate(PROLOGUE):
                front_one(kind, 0, a, i)
            over_pairs(act, pair)
            turn(NS * NP - 1, (0, 1, 2))
            mix(NS * NP - 1, 1)

        @block.vector
        def _(dve):
            def split_columns(hi, lo, src, chain_at, ready):
                for c in range(KQ):
                    last = nc.vector.tensor_scalar(hi[:, c, :], src[:, c, :], g.q_gain[:, c:c + 1], None, ALU.mult)
                last.then_inc(split_step, 1)
                dve.wait_ge(split_step, chain_at)
                for c in range(KQ):
                    last = nc.vector.scalar_tensor_tensor(lo[:, c, :], src[:, c, :], g.q_gain[:, c:c + 1],
                                                          hi[:, c, :].bitcast(F32), ALU.mult, ALU.subtract)
                return last.then_inc(ready, 1)

            def front_one(kind, p, a, index):
                if kind == "wq":
                    dve.wait_ge(front_mm, index + 1)
                    src = front[:, 0:KQ * KL].rearrange("p (c n) -> p c n", c=KQ)
                    split_columns(wq_hi[:, a], wq_lo[:, a], src, 3 * p + (1 if a == 0 else 3), wq_ready)
                    if a == 0:
                        dve.wait_ge(rope_in, 16 * (p + 1))
                        split_columns(wr_hi, wr_lo, raw_r, 3 * p + 2, wr_ready)
                elif kind == "outw":
                    dve.wait_ge(outw_hi, 2 * p + a + 1)
                    nc.vector.tensor_tensor(wo_lo[:, a, :], front[:], wo_hi[:, a, :].bitcast(F32),
                                            ALU.subtract).then_inc(wo_ready, 1)
                elif kind == "rope":
                    dve.wait_ge(front_mm, index + 1)
                    past(dve, rope_ready, B * p + a)
                    nc.vector.tensor_tensor(rot[:], front[:], g.cos[:], ALU.mult)
                    nc.vector.stream_shuffle(rot_swapped[:], front[:], SWAP).then_inc(rope_read, 1)
                else:
                    dve.wait_ge(q_hi_ready, NS * p + a + 1)
                    nc.vector.tensor_tensor(q_lo[:], front[:], q_hi[:].bitcast(F32),
                                            ALU.subtract).then_inc(q_ready, 1)

            def maxima(j, h):
                for i, group in enumerate(GROUPS):
                    dve.wait_ge(score_mm, NG * j + i + 1)
                    for q in group:
                        last = nc.vector.tensor_reduce(neg_max[:, h, q:q + 1], score_at(q), AX_X, ALU.max, negate=True)
                    last.then_inc(max_ready, 1)

            def normalise(j, h):
                dve.wait_ge(exp_done, NG * (j + 1))
                nc.vector.reciprocal(row_inv[:, h, :], row_sum[:, h, :]).then_inc(inv_ready, 1)
                dve.wait_ge(inv_ready, j + 1)
                for q in range(QB):
                    row = probs_at(h, q, 0, SEEN[q])
                    last = nc.vector.tensor_scalar(row, row, row_inv[:, h, q:q + 1], None, ALU.mult)
                last.then_inc(probs_ready, 1)

            def turn(j, parts):
                for i in parts:
                    dve.wait_ge(turn_hi, 3 * j + i + 1)
                    for k in ((0,), (1, 3), (2,))[i]:
                        last = nc.vector.tensor_tensor(pt_at(pt_lo, k), turned_at(k),
                                                       pt_at(pt_hi, k).bitcast(F32), ALU.subtract)
                    last.then_inc(turn_lo, 1)

            def mix(j, h):
                dve.wait_ge(mix_hi_ready, j + 1)
                nc.vector.tensor_tensor(mix_lo[:, h, :], mixed[:], mix_hi[:, h, :].bitcast(F32),
                                        ALU.subtract).then_inc(mix_ready, 1)

            def add(n, b, tiles):
                for t in tiles:
                    bank = outp if t % 2 == 0 else mixed
                    row = g.res[:, b * QB + t, :]
                    dve.wait_ge(out_mm, QB * n + t + 1)
                    nc.vector.tensor_tensor(row, bank[:], row, ALU.add).then_inc(out_added, 1)

            def pair(p, first, last):
                for s in range(NS):
                    j = NS * p + s
                    back = not (first and s == 0)
                    uses = front_uses(s, last)
                    index = FRONT * p + front_index(s, last)

                    def use(kinds):
                        for i, (kind, a) in enumerate(uses):
                            if kind in kinds:
                                if kind == "wq":
                                    front_one(kind, p + 1, a, index + i)
                                else:
                                    front_one(kind, p, a, index + i)

                    maxima(j, s % 2)
                    if s % 2 == 0:
                        if back:
                            turn(j - 1, (0, 1))
                        use(("query",))
                        if back:
                            turn(j - 1, (2,))
                        normalise(j, 0)
                        if back:
                            mix(j - 1, 1)
                    else:
                        n, b = B * p + s // 2 - 1, (s // 2 - 1) % B
                        out = not (first and s == 1)
                        use(("rope",))
                        turn(j - 1, (0, 1))
                        if out:
                            add(n, b, (0, 1))
                        turn(j - 1, (2,))
                        if out:
                            add(n, b, (2, 3))
                        normalise(j, 1)
                        use(("query",))
                        mix(j - 1, 0)
                    use(("outw", "wq"))

            for i, (kind, a) in enumerate(PROLOGUE):
                front_one(kind, 0, a, i)
            over_pairs(dve, pair)
            turn(NS * NP - 1, (0, 1, 2))
            mix(NS * NP - 1, 1)
            add(B * NP - 1, B - 1, range(QB))

        @block.gpsimd
        def _(pool):
            def rope(n):
                pool.wait_ge(rope_read, n + 1)
                nc.gpsimd.tensor_tensor(rot_swapped[:], rot_swapped[:], g.sin[:], ALU.mult).then_inc(rope_swapped, 1)
                pool.wait_ge(rope_swapped, n + 1)
                nc.gpsimd.tensor_tensor(rot[:], rot[:], rot_swapped[:], ALU.add).then_inc(rope_turned, 1)
                pool.wait_ge(rope_hi, n + 1)
                nc.gpsimd.tensor_tensor(qr[64:P, 0, :], rot[0:64, :], qr[0:64, 0, :].bitcast(F32), ALU.subtract)
                nc.gpsimd.tensor_tensor(qr[0:64, 1, :], rot[64:P, :], qr[64:P, 1, :].bitcast(F32),
                                        ALU.subtract).then_inc(rope_ready, 1)

            with pool.Fori(0, B * NP) as n:
                rope(n)


def inverse_root(nc, chain, x, y, t):
    xi, yi = x.bitcast(I32), y.bitcast(I32)
    chain.link(nc.vector.tensor_scalar(yi, xi, 1, None, ALU.logical_shift_right))
    chain.link(nc.vector.tensor_scalar(yi, yi, -1.0, float(0x5F3759DF), ALU.mult, ALU.add))
    for _ in range(3):
        chain.link(nc.vector.scalar_tensor_tensor(t, y, -0.5, y, ALU.mult, ALU.mult))
        chain.link(nc.vector.tensor_tensor(t, t, x, ALU.mult))
        chain.link(nc.vector.scalar_tensor_tensor(y, t, 1.5, y, ALU.add, ALU.mult))


ROOT_LINKS = 11


def norm_rows(nc, chain, space, rows, n):
    stats, mean_var, inv, variance, t0, carry = space
    nc.vector.memset(carry[:, 0:1], 0.0)
    for t in range(n):
        last = nc.vector.bn_stats(stats[:, t, :], rows(t))
    chain.link(last)
    nc.vector.memset(carry[:, 1:2], 0.0)
    for t in range(n):
        last = nc.vector.bn_aggr(mean_var[:, t, :], stats[:, t, :])
    chain.link(last)
    chain.link(nc.vector.tensor_scalar(variance[:], mean_var[:, :, 1], LN_EPS, None, ALU.add))
    inverse_root(nc, chain, variance[:], inv[:], t0[:])
    for t in range(n):
        last = nc.vector.tensor_scalar(rows(t), rows(t), mean_var[:, t, 0:1], inv[:, t:t + 1],
                                       ALU.subtract, ALU.mult)
    return last


def norm_space(m, name):
    return (m.sb(f"{name}_stats", [P, QB, 6]), m.sb(f"{name}_mean_var", [P, QB, 2]), m.sb(f"{name}_inv", [P, QB]),
            m.sb(f"{name}_variance", [P, QB]), m.sb(f"{name}_t", [P, QB]), m.sb(f"{name}_carry", [P, 2]))


def quant_phase(nc, g, io):
    U = 2
    with ExitStack() as stack:
        m = Space(nc, stack)
        both = range(U)
        w1 = [m.sb(f"w1_rows{u}", [P, KD, D]) for u in both]
        w2 = [m.sb(f"w2_rows{u}", [P, KD, INNER]) for u in both]
        hidden = [m.sb(f"hidden{u}", [P, QB, D]) for u in both]
        gated = [m.sb(f"gated{u}", [P, QB, INNER]) for u in both]
        amax = [m.sb(f"amax{u}", [P, 2, D]) for u in both]
        diag = [m.sb(f"diag{u}", [P, 2, KD, P]) for u in both]
        rows = [m.sb(f"s_rows{u}", [P, 2, D]) for u in both]
        quant = [m.sb(f"quantised{u}", [P, 2, QB, D], BF16) for u in both]
        quant_t = [m.sb(f"quantised_t{u}", [P, 2, KD, D], BF16) for u in both]
        wstep = [m.sb(f"w_scale_rows{u}", [P, D]) for u in both]
        top = [m.sb(f"top{u}", [P, 2, KD]) for u in both]
        ratio = [m.sb(f"ratio{u}", [P, KD]) for u in both]
        root = [m.sb(f"root{u}", [P, KD]) for u in both]
        tiny = [m.sb(f"tiny{u}", [P, KD]) for u in both]
        factor = [m.sb(f"factor{u}", [P, 2, KD]) for u in both]
        rowmax = [m.sb(f"rowmax{u}", [P, 2, KD]) for u in both]
        step = [m.sb(f"step{u}", [P, 2, KD]) for u in both]
        per = [m.sb(f"per{u}", [P, 2, KD]) for u in both]
        norm = [norm_space(m, f"norm{u}") for u in both]
        round_bias = m.sb("round_bias", [P, 2])
        bank = [m.banks(f"quant_bank{u}_", 4) for u in both]

        def sems(name):
            return [m.sem(f"{name}{u}") for u in both]

        w_in, amax_ready, top_mm, diag_ready = sems("qw_in"), sems("amax_ready"), sems("top_mm"), sems("diag_ready")
        spread_mm, rows_copied, scaled, per_ready = sems("spread_mm"), sems("rows_copied"), sems("scaled"), sems("per_ready")
        rounded, clamped, quantised = sems("rounded"), sems("clamped"), sems("quantised")
        qturn_mm, qturn_read = sems("qturn_mm"), sems("qturn_read")
        step_mm, step_read, qout_mm, qout_read = sems("step_mm"), sems("step_read"), sems("qout_mm"), sems("qout_read")
        silu_done, gate_done, res_added, batch_done = sems("silu_done"), sems("gate_done"), sems("res_added"), sems("batch_done")
        weights_used = sems("weights_used")
        dve_step = m.sem("quant_dve_step")
        block = stack.enter_context(nc.Block())

        LINEARS = ((0, w1, KD), (1, w2, INNER // P))
        ROUNDS = B // U

        def halves(n):
            return [range(c, min(c + 2, n)) for c in range(0, n, 2)]

        READS = 2 * sum(len(halves(n)) for _, _, n in LINEARS)

        def reads_before(i, side):
            return 2 * len(halves(KD)) * i + side * len(halves(LINEARS[i][2]))

        @block.sync
        def _(sp):
            def load(c):
                for u in both:
                    for w, name in ((w1, "w_gate_up"), (w2, "w_down")):
                        view = io[name].rearrange("b (t p) n -> b p t n", p=P)[bass.ds(c * U + u, 1)]
                        sp.dma_start(w[u][:], view.rearrange("b p t n -> (b p) t n")).then_inc(w_in[u], 16)

            load(0)
            for i, name in enumerate(("w_g", "w_u", "w_d")):
                sp.dma_start(g.raw[i][:], io[name][0].rearrange("(k p) n -> p k n", p=P)).then_inc(g.expert_in[i], 16)
            with sp.Fori(1, ROUNDS) as c:
                for u in both:
                    sp.wait_ge(batch_done[u], c)
                load(c)

        @block.scalar
        def _(act):
            with act.Fori(0, ROUNDS) as c:
                for i, w, n in LINEARS:
                    width = n * P
                    for u in both:
                        for side in range(2):
                            act.wait_ge(spread_mm[u], 2 * (2 * c + i) + side + 1)
                            nc.scalar.activation(rows[u][:, side, 0:width], bank[u][2 + side][:, 0:width],
                                                 ACT.Copy).then_inc(rows_copied[u], 1)
                    for side in range(2):
                        for u in both:
                            data = hidden[u] if side == 0 else w[u]
                            act.wait_ge(per_ready[u], 2 * (2 * c + i) + side + 1)
                            for t in range(QB):
                                row = data[:, t, 0:width]
                                last = nc.scalar.activation(row, row, ACT.Identity, bias=round_bias[:, 0:1],
                                                            scale=per[u][:, side, t:t + 1])
                            last.then_inc(rounded[u], 1)
                        for u in both:
                            data = hidden[u] if side == 0 else w[u]
                            act.wait_ge(clamped[u], 2 * (2 * c + i) + side + 1)
                            nc.scalar.activation(quant[u][:, side, :, 0:width], data[:, :, 0:width], ACT.Identity,
                                                 bias=round_bias[:, 1:2]).then_inc(quantised[u], 1)
                        for u in both:
                            for h, tiles in enumerate(halves(n)):
                                act.wait_ge(qturn_mm[u], READS * c + reads_before(i, side) + h + 1)
                                src = bank[u][2 * side + h][:].bitcast(BF16).rearrange("p (k n) -> p k n", k=2)
                                nc.scalar.activation(quant_t[u][:, side, tiles[0]:tiles[-1] + 1, :],
                                                     src[:, 0:len(tiles), :], ACT.Copy).then_inc(qturn_read[u], 1)
                    for u in both:
                        act.wait_ge(step_mm[u], 2 * c + i + 1)
                        nc.scalar.activation(wstep[u][:], bank[u][0][:], ACT.Copy).then_inc(step_read[u], 1)
                    if i == 0:
                        for u in both:
                            act.wait_ge(qout_read[u], 2 * QB * c + QB)
                            nc.scalar.activation(gated[u][:], hidden[u][:, :, 0:INNER], ACT.Silu).then_inc(silu_done[u], 1)

        @block.vector
        def _(dve):
            start = Chain(dve, dve_step)
            nc.vector.memset(round_bias[:, 0:1], ROUND)
            start.link(nc.vector.memset(round_bias[:, 1:2], -ROUND))
            LINKS = U * (2 * (3 + ROOT_LINKS) + 1 + 2 * (10 + ROOT_LINKS))
            with dve.Fori(0, ROUNDS) as c:
                chain = Chain(dve, dve_step, start.n + c * LINKS)

                def tile(u, t, n=1):
                    return g.res[:, bass.ds((c * U + u) * QB + t, n), :]

                for u in both:
                    chain.link(norm_rows(nc, chain, norm[u], lambda t: tile(u, t), QB))
                for i, w, n in LINEARS:
                    width = n * P

                    def source(u, side):
                        return w[u][:] if side else tile(u, 0, QB) if i == 0 else gated[u][:]

                    for side in (1, 0):
                        for u in both:
                            if side:
                                dve.wait_ge(w_in[u], 32 * (c + 1))
                            elif i == 1:
                                dve.wait_ge(gate_done[u], c + 1)
                            nc.vector.tensor_reduce(amax[u][:, side, 0:width],
                                                    source(u, side).rearrange("p t k -> p k t"), AX_X, ALU.max,
                                                    apply_absolute_value=True).then_inc(amax_ready[u], 1)
                    for u in both:
                        dve.wait_ge(top_mm[u], 2 * (2 * c + i) + 2)
                        for side in range(2):
                            last = nc.vector.tensor_reduce(
                                top[u][:, side, 0:n], bank[u][side][:, 0:width].rearrange("p (k q) -> p k q", k=n),
                                AX_X, ALU.max)
                        chain.link(last)
                        chain.link(nc.vector.tensor_scalar(top[u][:, :, 0:n], top[u][:, :, 0:n], Q_EPS, None, ALU.max))
                        chain.link(nc.vector.reciprocal(tiny[u][:, 0:n], top[u][:, 1, 0:n]))
                        chain.link(nc.vector.tensor_tensor(ratio[u][:, 0:n], top[u][:, 0, 0:n], tiny[u][:, 0:n], ALU.mult))
                        inverse_root(nc, chain, ratio[u][:, 0:n], root[u][:, 0:n], tiny[u][:, 0:n])
                        chain.link(nc.vector.tensor_tensor(tiny[u][:, 0:n], ratio[u][:, 0:n], root[u][:, 0:n], ALU.mult))
                        chain.link(nc.vector.tensor_scalar(factor[u][:, 1, 0:n], tiny[u][:, 0:n], Q_EPS, None, ALU.max))
                        nc.vector.reciprocal(factor[u][:, 0, 0:n], factor[u][:, 1, 0:n]).then_inc(scaled[u], 1)
                        dve.wait_ge(scaled[u], 3 * (2 * c + i) + 1)
                        for side in range(2):
                            for k in range(n):
                                last = nc.vector.tensor_scalar(diag[u][:, side, k, :], g.ident[:],
                                                               factor[u][:, side, k:k + 1], None, ALU.mult)
                            last.then_inc(diag_ready[u], 1)
                    for side in range(2):
                        for u in both:
                            if side == 0:
                                dve.wait_ge(rows_copied[u], 2 * (2 * c + i) + 1)
                                row = rows[u][:, 0, 0:width]
                                last = nc.vector.tensor_tensor(
                                    hidden[u][:, :, 0:width], source(u, 0),
                                    row.unsqueeze(1).to_broadcast([P, QB, width]), ALU.mult)
                                last.then_inc(scaled[u], 1)
                                dve.wait_ge(scaled[u], 3 * (2 * c + i) + 2)
                            else:
                                dve.wait_ge(scaled[u], 3 * (2 * c + i) + 3)
                            data = hidden[u] if side == 0 else w[u]
                            chain.link(nc.vector.tensor_reduce(rowmax[u][:, side, :], data[:, :, 0:width], AX_X, ALU.max,
                                                               apply_absolute_value=True))
                            chain.link(nc.vector.tensor_scalar(step[u][:, side, :], rowmax[u][:, side, :], Q_EPS,
                                                               1.0 / QMAX, ALU.max, ALU.mult))
                            nc.vector.reciprocal(per[u][:, side, :], step[u][:, side, :]).then_inc(per_ready[u], 1)
                        for u in both:
                            data = (hidden[u] if side == 0 else w[u])[:, :, 0:width]
                            dve.wait_ge(rounded[u], 2 * (2 * c + i) + side + 1)
                            nc.vector.tensor_scalar(data, data, ROUND - QMAX, ROUND + QMAX, ALU.max,
                                                    ALU.min).then_inc(clamped[u], 1)
                    for u in both:
                        dve.wait_ge(clamped[u], 2 * (2 * c + i) + 2)
                        for t in range(KD):
                            last = nc.vector.tensor_scalar(diag[u][:, 0, t, :], g.ident[:], step[u][:, 1, t:t + 1],
                                                           None, ALU.mult)
                        last.then_inc(diag_ready[u], 1)
                    for t in range(QB):
                        for u in both:
                            if t == 0:
                                dve.wait_ge(step_read[u], 2 * c + i + 1)
                            dve.wait_ge(qout_mm[u], 2 * QB * c + QB * i + t + 1)
                            nc.vector.scalar_tensor_tensor(hidden[u][:, t, :], bank[u][1 + t % 3][:],
                                                           step[u][:, 0, t:t + 1], wstep[u][:], ALU.mult,
                                                           ALU.mult).then_inc(qout_read[u], 1)
                for u in both:
                    dve.wait_ge(res_added[u], c + 1)
                    last = norm_rows(nc, chain, norm[u], lambda t: tile(u, t), QB)
                    last.then_inc(batch_done[u], 1)
                for u in both:
                    dve.wait_ge(batch_done[u], c + 1)
                assert chain.n == LINKS

        @block.gpsimd
        def _(pool):
            with pool.Fori(0, ROUNDS) as c:
                for i, w, n in LINEARS:
                    width = n * P
                    for u in both:
                        pool.wait_ge(rows_copied[u], 2 * (2 * c + i) + 2)
                        pool.wait_ge(scaled[u], 3 * (2 * c + i) + 2)
                        for t in range(KD):
                            last = nc.gpsimd.tensor_tensor(w[u][:, t, :], w[u][:, t, :], rows[u][:, 1, 0:width], ALU.mult)
                        last.then_inc(scaled[u], 1)
                    for u in both:
                        if i == 0:
                            pool.wait_ge(silu_done[u], c + 1)
                            nc.gpsimd.tensor_tensor(gated[u][:], gated[u][:], hidden[u][:, :, INNER:],
                                                    ALU.mult).then_inc(gate_done[u], 1)
                        else:
                            for t in range(QB):
                                pool.wait_ge(qout_read[u], 2 * QB * c + QB + t + 1)
                                row = g.res[:, bass.ds((c * U + u) * QB + t, 1), :]
                                last = nc.gpsimd.tensor_tensor(row, row, hidden[u][:, t:t + 1, :], ALU.add)
                            last.then_inc(res_added[u], 1)

        @block.tensor
        def _(pe):
            with pe.Fori(0, ROUNDS) as c:
                for i, w, n in LINEARS:
                    width = n * P
                    for u in both:
                        pe.wait_ge(amax_ready[u], 2 * (2 * c + i) + 2)
                        for side in range(2):
                            for k in range(n):
                                last = nc.tensor.transpose(bank[u][side][:, k * P:(k + 1) * P],
                                                           amax[u][:, side, k * P:(k + 1) * P], g.ident[:])
                            last.then_inc(top_mm[u], 1)
                    for u in both:
                        for side in range(2):
                            pe.wait_ge(diag_ready[u], 3 * (2 * c + i) + side + 1)
                            nc.tensor.matmul(bank[u][2 + side][:, 0:width], g.ones[:], diag[u][:, side, 0:n, :],
                                             start=True, stop=True).then_inc(spread_mm[u], 1)
                    for side in range(2):
                        for u in both:
                            pe.wait_ge(quantised[u], 2 * (2 * c + i) + side + 1)
                            for h, tiles in enumerate(halves(n)):
                                out = bank[u][2 * side + h][:].bitcast(BF16)
                                for k in tiles:
                                    for t in range(QB):
                                        at = (k % 2) * D + t * P
                                        last = nc.tensor.transpose(out[:, at:at + P],
                                                                   quant[u][:, side, t, k * P:(k + 1) * P], g.ident_b[:])
                                last.then_inc(qturn_mm[u], 1)
                    for u in both:
                        pe.wait_ge(diag_ready[u], 3 * (2 * c + i) + 3)
                        pe.wait_ge(qturn_read[u], READS * c + reads_before(i, 1) + len(halves(n)))
                        nc.tensor.matmul(bank[u][0][:], g.ones[:], diag[u][:, 0, :, :], start=True,
                                         stop=True).then_inc(step_mm[u], 1)
                    for t in range(QB):
                        for u in both:
                            if t == 3:
                                pe.wait_ge(qout_read[u], 2 * QB * c + QB * i + 1)
                            for k in range(n):
                                last = nc.tensor.matmul(bank[u][1 + t % 3][:], quant_t[u][:, 0, k, t * P:(t + 1) * P],
                                                        quant_t[u][:, 1, k, :], start=k == 0, stop=k == n - 1)
                            last.then_inc(qout_mm[u], 1)


def expert_phase(nc, g, io):
    lower, upper, centre = 0.5 - float(np.log(4.0 / 3.0)), 0.5, 1.0 / float(np.e)
    with ExitStack() as stack:
        m = Space(nc, stack)
        x_hi = m.sb("xt_hi", [P, KD, NT * P], F32R)
        x_lo = m.sb("xt_lo", [P, KD, NT * P], F32R)
        raw = g.raw
        w_hi = [m.sb(f"hi_{k}", [P, KD, FF], F32R) for k in ("gate", "up", "down")]
        w_lo = [m.sb(f"lo_{k}", [P, KD, FF], F32R) for k in ("gate", "up", "down")]
        h_hi = m.sb("h_hi", [P, KF, S], F32R)
        h_lo = m.sb("h_lo", [P, KF, S], F32R)
        silu = m.sb("silu", [P, S])
        h = m.sb("h", [P, S])
        wr = m.sb("router", [P, KD, E])
        wr_hi = m.sb("router_hi", [P, KD, E], F32R)
        wr_lo = m.sb("router_lo", [P, KD, E], F32R)
        temp = m.sb("temperature", [P, 1])
        weight = m.sb("weight", [P, NT, E])
        r = [m.sb(f"route{i}", [P, NT, E]) for i in range(5)]
        rs = [m.sb(f"route_sum{i}", [P, NT]) for i in range(3)]
        norm = norm_space(m, "norm_out")
        gate = m.banks("gate_bank", 2)
        up = m.banks("up_bank", 2)
        down = m.banks("down_bank", QB)

        w_in = g.expert_in
        router_in = m.sem("router_in")
        w_hi_ready = m.sem("w_hi_ready")
        w_ready = m.sem("w_ready")
        xturn_mm = m.sem("xturn_mm")
        xturn_hi = m.sem("xturn_hi")
        xturn_lo = m.sem("xturn_lo")
        logit_mm = m.sem("logit_mm")
        logit_scaled = m.sem("logit_scaled")
        exp_ready = m.sem("exp_ready")
        near_ready = m.sem("near_ready")
        gate_up_mm = m.sem("gate_up_mm")
        silu_ready = m.sem("silu_ready")
        h_ready = m.sem("h_ready")
        h_hi_ready = m.sem("h_hi_ready")
        h_split = m.sem("h_split")
        down_mm = m.sem("down_mm")
        down_added = m.sem("down_added")
        normed = m.sem("normed2")
        out_done = m.sem("out_done")
        dve_step = m.sem("expert_dve_step")
        block = stack.enter_context(nc.Block())
        SPLITS = 2 * KF + 1

        def split_slices():
            for f in range(KF):
                for which in (0, 1):
                    yield which, slice(f * P, (f + 1) * P)
            yield 2, slice(0, D)

        @block.sync
        def _(sp):
            views = [io[k].rearrange("e (k p) n -> e p k n", p=P) for k in ("w_g", "w_u", "w_d")]
            sp.dma_start(wr[:], io["w_router"].rearrange("(k p) e -> p k e", p=P)).then_inc(router_in, 16)
            sp.dma_start(temp[:], io["temperature"].partition_broadcast(P)).then_inc(router_in, 16)
            with sp.Fori(1, E) as e:
                sp.wait_ge(w_ready, SPLITS * e - 1)
                for i in range(2):
                    sp.dma_start(raw[i][:], views[i][bass.ts(e, 1)].rearrange("e p k n -> (e p) k n")).then_inc(w_in[i], 16)
                sp.wait_ge(w_ready, SPLITS * e)
                sp.dma_start(raw[2][:], views[2][bass.ts(e, 1)].rearrange("e p k n -> (e p) k n")).then_inc(w_in[2], 16)
            out = io["out"].rearrange("b (t p) n -> p (b t) n", p=P)
            for b in range(B):
                sp.wait_ge(normed, b + 1)
                sp.dma_start(out[:, b * QB:(b + 1) * QB, :], g.res[:, b * QB:(b + 1) * QB, :]).then_inc(out_done, 16)
            sp.wait_ge(out_done, 16 * B)

        @block.tensor
        def _(pe):
            for t in range(NT):
                bank = down[t % QB]
                if t >= QB:
                    pe.wait_ge(xturn_lo, t - QB + 1)
                for k in range(KD):
                    last = nc.tensor.transpose(bank[:, k * P:(k + 1) * P], g.res[:, t, k * P:(k + 1) * P], g.ident[:])
                last.then_inc(xturn_mm, 1)
            pe.wait_ge(router_in, 32)
            pe.wait_ge(h_ready, 2)
            for t in range(NT):
                pe.wait_ge(xturn_lo, t + 1)
                for k in range(KD):
                    tile = slice(t * P, (t + 1) * P)
                    last = split_matmul(nc, gate[0][:, t * E:(t + 1) * E], x_hi[:, k, tile], x_lo[:, k, tile],
                                        wr_hi[:, k, :], wr_lo[:, k, :], k == 0, k == KD - 1)
            last.then_inc(logit_mm, 1)
            pe.wait_ge(logit_scaled, 1)
            with pe.Fori(0, E) as e:
                for b in range(B):
                    turn = B * e + b
                    tokens = slice(b * S, (b + 1) * S)
                    for f in range(KF):
                        n = KF * turn + f
                        if b == 0:
                            pe.wait_ge(w_ready, SPLITS * e + 2 * f + 2)
                        pe.wait_ge(h_ready, n - 1 + 2)
                        for which, bank in ((0, gate[f % 2]), (1, up[f % 2])):
                            for k in range(KD):
                                cols = slice(f * P, (f + 1) * P)
                                last = split_matmul(nc, bank[:], w_hi[which][:, k, cols], w_lo[which][:, k, cols],
                                                    x_hi[:, k, tokens], x_lo[:, k, tokens], k == 0, k == KD - 1)
                        last.then_inc(gate_up_mm, 1)
                    if b == 0:
                        pe.wait_ge(w_ready, SPLITS * (e + 1))
                    for part in (range(KF - 1), range(KF - 1, KF)):
                        pe.wait_ge(h_split, KF * turn + part[-1] + 1)
                        for t in range(QB):
                            for f in part:
                                last = split_matmul(nc, down[t][:], h_hi[:, f, t * P:(t + 1) * P],
                                                    h_lo[:, f, t * P:(t + 1) * P], w_hi[2][:, f, :], w_lo[2][:, f, :],
                                                    f == 0, f == KF - 1)
                            if part[-1] == KF - 1:
                                last.then_inc(down_mm, 1)

        @block.scalar
        def _(act):
            for t in range(NT):
                act.wait_ge(xturn_mm, t + 1)
                nc.scalar.activation(x_hi[:, :, t * P:(t + 1) * P],
                                     down[t % QB][:].rearrange("p (k n) -> p k n", k=KD), ACT.Copy).then_inc(xturn_hi, 1)
            def split(e, after):
                for i, (which, cols) in enumerate(split_slices()):
                    if i < 2:
                        act.wait_ge(w_in[which], 16 * (e + 1))
                    elif which == 2:
                        act.wait_ge(w_in[2], 16 * (e + 1))
                    if after is not None:
                        if which == 2:
                            act.wait_ge(down_mm, B * QB * e)
                        elif which == 0:
                            act.wait_ge(gate_up_mm, B * KF * e - KF + i // 2 + 1)
                    nc.scalar.activation(w_hi[which][:, :, cols], raw[which][:, :, cols],
                                         ACT.Copy).then_inc(w_hi_ready, 1)

            def silus(e, b):
                for f in range(KF):
                    n = KF * (B * e + b) + f
                    act.wait_ge(gate_up_mm, n + 1)
                    act.wait_ge(h_ready, n + 2)
                    nc.scalar.activation(silu[:], gate[f % 2][:], ACT.Silu).then_inc(silu_ready, 1)
                    act.wait_ge(h_ready, n + 3)
                    nc.scalar.activation(h_hi[:, f, :], h[:], ACT.Copy).then_inc(h_hi_ready, 1)

            split(0, None)
            act.wait_ge(logit_scaled, 1)
            nc.scalar.activation(r[1][:], r[0][:], ACT.Exp, scale=-1.0).then_inc(exp_ready, 1)
            act.wait_ge(near_ready, 1)
            nc.scalar.activation(r[1][:], r[0][:], ACT.Exp, scale=-1.0 / 0.1)
            nc.scalar.activation(r[2][:], r[0][:], ACT.Exp, scale=-1.0 / 0.3).then_inc(exp_ready, 1)

            with act.Fori(0, E - 1) as e:
                for b in range(B):
                    silus(e, b)
                split(e + 1, True)
            for b in range(B):
                silus(E - 1, b)

        @block.vector
        def _(dve):
            chain = Chain(dve, dve_step)
            dve.wait_ge(router_in, 32)
            nc.vector.tensor_copy(wr_hi[:], wr[:]).then_inc(h_ready, 1)
            dve.wait_ge(h_ready, 1)
            nc.vector.tensor_tensor(wr_lo[:], wr[:], wr_hi[:].bitcast(F32), ALU.subtract).then_inc(h_ready, 1)
            chain.link(nc.vector.reciprocal(temp[:], temp[:]))
            for t in range(NT):
                dve.wait_ge(xturn_hi, t + 1)
                tile = slice(t * P, (t + 1) * P)
                nc.vector.tensor_tensor(x_lo[:, :, tile], down[t % QB][:].rearrange("p (k n) -> p k n", k=KD),
                                        x_hi[:, :, tile].bitcast(F32), ALU.subtract).then_inc(xturn_lo, 1)

            dve.wait_ge(logit_mm, 1)
            nc.vector.tensor_scalar(r[0][:], gate[0][:, 0:NT * E].rearrange("p (t e) -> p t e", e=E), temp[:, 0:1],
                                    None, ALU.mult).then_inc(logit_scaled, 1)
            dve.wait_ge(exp_ready, 1)
            chain.link(nc.vector.tensor_scalar(r[1][:], r[1][:], 1.0, None, ALU.add))
            chain.link(nc.vector.reciprocal(r[2][:], r[1][:]))
            inside, zone, near = r[2], r[3], r[0]
            chain.link(nc.vector.tensor_scalar(zone[:], inside[:], lower, None, ALU.is_ge))
            chain.link(nc.vector.scalar_tensor_tensor(zone[:], inside[:], upper, zone[:], ALU.is_le, ALU.mult))
            chain.link(nc.vector.tensor_scalar(r[4][:], inside[:], centre, None, ALU.subtract))
            nc.vector.scalar_tensor_tensor(near[:], r[4][:], -1.0, r[4][:], ALU.mult, ALU.max).then_inc(near_ready, 1)
            dve.wait_ge(exp_ready, 2)
            wide, fallback = r[1], r[2]
            chain.link(nc.vector.tensor_tensor(weight[:], wide[:], zone[:], ALU.mult))
            rank, ahead = r[3], r[4]
            chain.link(nc.vector.memset(rank[:], 0.0))
            for i in range(E):
                one = fallback[:, :, i:i + 1]
                if i:
                    nc.vector.tensor_tensor(ahead[:, :, 0:i], one.to_broadcast([P, NT, i]), fallback[:, :, 0:i], ALU.is_gt)
                chain.link(nc.vector.tensor_tensor(ahead[:, :, i:E], one.to_broadcast([P, NT, E - i]),
                                                   fallback[:, :, i:E], ALU.is_ge))
                chain.link(nc.vector.tensor_tensor(rank[:], rank[:], ahead[:], ALU.add))
            chain.link(nc.vector.tensor_scalar(rank[:], rank[:], 2.5, None, ALU.is_le))
            chain.link(nc.vector.tensor_tensor(fallback[:], fallback[:], rank[:], ALU.mult))

            def row_scale(values, total):
                chain.link(nc.vector.tensor_scalar(rs[1][:], total[:], 1e-8, None, ALU.max))
                chain.link(nc.vector.reciprocal(rs[1][:], rs[1][:]))
                chain.link(nc.vector.tensor_tensor(values[:], values[:],
                                                   rs[1][:].unsqueeze(2).to_broadcast([P, NT, E]), ALU.mult))

            chain.link(nc.vector.tensor_reduce(rs[0][:], fallback[:], AX_X, ALU.add))
            row_scale(fallback, rs[0])
            chain.link(nc.vector.tensor_reduce(rs[0][:], weight[:], AX_X, ALU.add))
            none = rs[2]
            chain.link(nc.vector.tensor_scalar(none[:], rs[0][:], 1e-8, None, ALU.is_lt))
            chain.link(nc.vector.tensor_tensor(fallback[:], fallback[:], none[:].unsqueeze(2).to_broadcast([P, NT, E]),
                                               ALU.mult))
            chain.link(nc.vector.tensor_scalar(none[:], none[:], -1.0, 1.0, ALU.mult, ALU.add))
            chain.link(nc.vector.tensor_tensor(weight[:], weight[:], none[:].unsqueeze(2).to_broadcast([P, NT, E]),
                                               ALU.mult))
            chain.link(nc.vector.tensor_tensor(weight[:], weight[:], fallback[:], ALU.add))
            chain.link(nc.vector.tensor_reduce(rs[0][:], weight[:], AX_X, ALU.add))
            row_scale(weight, rs[0])

            def batches(e, last_expert):
                for b in range(B):
                    turn = B * e + b
                    for f in range(KF):
                        n = KF * turn + f
                        dve.wait_ge(silu_ready, n + 1)
                        nc.vector.tensor_tensor(h[:], up[f % 2][:], silu[:], ALU.mult).then_inc(h_ready, 1)
                        dve.wait_ge(h_hi_ready, n + 1)
                        nc.vector.tensor_tensor(h_lo[:, f, :], h[:], h_hi[:, f, :].bitcast(F32),
                                                ALU.subtract).then_inc(h_split, 1)
                        dve.wait_ge(h_split, n + 1)
                    for t in range(QB):
                        tile = b * QB + t
                        dve.wait_ge(down_mm, QB * turn + t + 1)
                        row = g.res[:, tile, :]
                        nc.vector.scalar_tensor_tensor(row, down[t][:], weight[:, tile, bass.ds(e, 1)], row,
                                                       ALU.mult, ALU.add).then_inc(down_added, 1)

                    if last_expert:
                        dve.wait_ge(down_added, QB * (turn + 1))
                        last = norm_rows(nc, chain, norm, lambda t: g.res[:, b * QB + t, :], QB)
                        last.then_inc(normed, 1)
                        dve.wait_ge(normed, b + 1)

            with dve.Fori(0, E - 1) as e:
                batches(e, False)
            batches(E - 1, True)

        @block.gpsimd
        def _(pool):
            def split(e):
                for i, (which, cols) in enumerate(split_slices()):
                    for k in range(KD):
                        pool.wait_ge(w_hi_ready, SPLITS * e + i + 1)
                        last = nc.gpsimd.tensor_tensor(w_lo[which][:, k, cols], raw[which][:, k, cols],
                                                       w_hi[which][:, k, cols].bitcast(F32), ALU.subtract)
                    last.then_inc(w_ready, 1)

            with pool.Fori(0, E) as e:
                split(e)


def build(nc, io):
    with ExitStack() as stack:
        m = Space(nc, stack)

        class g:
            res = m.sb("res", [P, NT, D])
            ident = m.sb("ident", [P, P])
            ident_b = m.sb("ident_b", [P, P], BF16)
            mask = m.sb("mask", [P, P], BF16)
            ones = m.sb("ones", [P, P])

        with ExitStack() as inner:
            a = Space(nc, inner)
            g.cos = a.sb("cos", [P, S])
            g.sin = a.sb("sin", [P, S])
            g.q_gain = a.sb("q_gain", [P, KQ])
            g.qn_hi = a.sb("qn_hi", [P, KQ, B * S], F32R)
            g.qn_lo = a.sb("qn_lo", [P, KQ, B * S], F32R)
            g.key_hi = a.sb("key_hi", [P, B * S], F32R)
            g.key_lo = a.sb("key_lo", [P, B * S], F32R)
            g.kr_hi = a.sb("kr_hi", [P, B * S], F32R)
            g.kr_lo = a.sb("kr_lo", [P, B * S], F32R)
            g.val_hi = a.sb("val_hi", [P, NT, KL], F32R)
            g.val_lo = a.sb("val_lo", [P, NT, KL], F32R)
            latent_phase(nc, g, io)
            attention_phase(nc, g, io)
        g.raw = [m.sb(f"raw_{k}", [P, KD, FF]) for k in ("gate", "up", "down")]
        g.expert_in = [m.sem(f"{k}_in") for k in ("gate", "up", "down")]
        quant_phase(nc, g, io)
        expert_phase(nc, g, io)


def rotary_order():
    half = ROPE // 2
    return np.concatenate([np.r_[q * 16:q * 16 + 16, half + q * 16:half + q * 16 + 16] for q in range(2)])


def shape_constants():
    order = rotary_order()
    inv_freq = (1.0 / np.float32(10000.0) ** (np.arange(0, ROPE, 2, dtype=np.float32) / np.float32(ROPE)))
    angle = np.outer(np.arange(S, dtype=np.float32), inv_freq.astype(np.float32)).astype(np.float32)
    angle = np.concatenate([angle, angle], -1)[:, order].T
    sign = np.where(order < ROPE // 2, -1.0, 1.0).astype(np.float32)[:, None]
    cos, sin = np.cos(angle), np.sin(angle) * sign
    mask = np.where(np.tril(np.ones((P, P), bool)), 0.0, MASKED)
    return {
        "cos": np.concatenate([cos, cos], 0).astype(np.float32),
        "sin": np.concatenate([sin, sin], 0).astype(np.float32),
        "mask": mask.astype(np.float32),
        "ident": np.eye(P, dtype=np.float32),
        "ones": np.ones((P, P), np.float32),
    }


def lay_out(inputs):
    a = {k: np.asarray(v) for k, v in inputs.items()}
    order = rotary_order()
    x = a["x"]
    wq = a["L0_attn_q_b_w"].reshape(H, NOPE + ROPE, QL)
    wkva = a["L0_attn_kv_a_w"]
    w_kr = wkva[KL:][order].T
    arrays = {
        "x": x,
        "x_t": x.transpose(0, 2, 1),
        "w_a": np.concatenate([a["L0_attn_q_a_w"], wkva[:KL]], 0).T,
        "w_kr": np.concatenate([w_kr, w_kr], 1),
        "q_ln": a["L0_attn_q_a_ln_w"].reshape(KQ, P).T,
        "kv_ln": a["L0_attn_kv_a_ln_w"],
        "wq_nope": wq[:, :NOPE],
        "wq_rope_t": wq[:, NOPE:][:, order].reshape(H * ROPE, QL).T,
        "w_kv": a["L0_attn_kv_b_w"].reshape(H, NOPE + VD, KL),
        "w_o_t": a["L0_attn_o_w"].T,
        "w_gate_up": a["fside_BxS2xS2_0"],
        "w_down": a["ctx_1024"],
        "w_g": a["L0_ffn_Wg"],
        "w_u": a["L0_ffn_Wu"],
        "w_d": a["L0_ffn_Wd"],
        "w_router": a["L0_ffn_Wr"],
        "temperature": a["L0_ffn_temperature"],
    }
    return {k: np.ascontiguousarray(v) for k, v in {**arrays, **shape_constants()}.items()}


def kernel(**inputs):
    import concourse.bacc as bacc
    from concourse.bass_utils import run_bass_kernel_spmd

    nc = bacc.Bacc("TRN2", target_bir_lowering=False, num_devices=1)
    arrays = lay_out(inputs)
    io = {k: nc.dram_tensor(f"in_{k}", v.shape, mybir.dt.from_np(v.dtype), kind="ExternalInput").ap()
          for k, v in arrays.items()}
    io["out"] = nc.dram_tensor("out_y", (B, S, D), F32, kind="ExternalOutput").ap()
    build(nc, io)
    result = run_bass_kernel_spmd(nc, [{f"in_{k}": v for k, v in arrays.items()}], core_ids=[0])
    return result.results[0]["out_y"]
```

```python
from contextlib import ExitStack

import numpy as np

import concourse.bass as bass
from concourse import mybir

F32 = mybir.dt.float32
F32R = mybir.dt.float32r
BF16 = mybir.dt.bfloat16
I32 = mybir.dt.int32
ALU = mybir.AluOpType
ACT = mybir.ActivationFunctionType
AX_X = mybir.AxisListType.X

P = 128
B, S, D = 4, 512, 512
H, NOPE, ROPE, VD = 16, 128, 64, 128
QL, KL = 384, 128
QB = S // P
NT = B * QB
KD = D // P
KQ = QL // P
NP = H // 2
E, FF = 8, 512
KF = FF // P
INNER = 256
RMS_EPS, LN_EPS, Q_EPS, QMAX = 1e-6, 1e-5, 1e-6, 127.0
SCALE = float(NOPE + ROPE) ** -0.5
MASKED = -1e30
ROUND = 1.5 * 2.0 ** 23
SWAP = [(i + 16) % 32 for i in range(32)]
SEEN = [(q + 1) * P for q in range(QB)]


def past(engine, semaphore, count):
    if not (isinstance(count, int) and count == 0):
        engine.wait_ge(semaphore, count)


class Chain:

    def __init__(self, engine, semaphore, base=0):
        self.engine, self.semaphore, self.base, self.n = engine, semaphore, base, 0

    def link(self, instruction):
        self.n += 1
        instruction.then_inc(self.semaphore, 1)
        self.engine.wait_ge(self.semaphore, self.base + self.n)


class Space:

    def __init__(self, nc, stack):
        self.nc, self.stack = nc, stack

    def sb(self, name, shape, dtype=F32):
        return self.stack.enter_context(self.nc.sbuf_tensor(name, shape, dtype))

    def psum(self, name, shape, dtype=F32):
        return self.stack.enter_context(self.nc.psum_tensor(name, shape, dtype))

    def sem(self, name):
        return self.stack.enter_context(self.nc.semaphore(name))

    def banks(self, name, n):
        return [self.psum(f"{name}{i}", [P, 512]) for i in range(n)]


def split_matmul(nc, out, w_hi, w_lo, x_hi, x_lo, start, stop):
    nc.tensor.matmul(out, w_hi, x_hi, start=start, stop=False)
    nc.tensor.matmul(out, w_hi, x_lo, start=False, stop=False)
    return nc.tensor.matmul(out, w_lo, x_hi, start=False, stop=stop)


def load_queries(sp, g, io, p):
    wq_n = io["wq_nope"].rearrange("h d c -> d h c")
    wk_n = io["w_kv"][:, 0:NOPE, :].rearrange("h d c -> d h c")
    wr_n = io["wq_rope_t"].rearrange("(k p) n -> p k n", p=P)
    sp.dma_start(g.raw_r[:], wr_n[:, :, bass.ts(p, P)]).then_inc(g.rope_in, 16)
    sp.dma_start(g.raw_q[:], wq_n[:, bass.ts(p, 2), :]).then_inc(g.fold_in, 16)
    sp.dma_start(g.raw_k[:], wk_n[:, bass.ts(p, 2), :]).then_inc(g.fold_in, 16)


def latent_phase(nc, g, io):
    with ExitStack() as stack:
        m = Space(nc, stack)
        x_t = m.sb("x_t", [P, KD, S])
        x_hi = m.sb("x_hi", [P, KD, S], F32R)
        x_lo = m.sb("x_lo", [P, KD, S], F32R)
        wa = m.sb("wa", [P, KD, QL + KL])
        wa_hi = m.sb("wa_hi", [P, KD, QL + KL], F32R)
        wa_lo = m.sb("wa_lo", [P, KD, QL + KL], F32R)
        wr = m.sb("wkr", [P, KD, P])
        wr_hi = m.sb("wkr_hi", [P, KD, P], F32R)
        wr_lo = m.sb("wkr_lo", [P, KD, P], F32R)
        junk = m.sb("square_junk", [P, 2, QL + KL], BF16)
        latent = m.sb("latent", [P, QB, QL + KL])
        ms = m.sb("ms", [P, QB, 2])
        rms = m.sb("rms", [P, QB, 2])
        rstd = m.sb("rstd", [P, QB, 2])
        nt = m.sb("newton", [P, QB, 2])
        eps = m.sb("rms_eps", [P, 1])
        kv_gain = m.sb("kv_gain", [P, KL])
        rot = m.sb("krot", [P, S])
        rot_swapped = m.sb("krot_swapped", [P, S])
        product = m.banks("latent_bank", QB)
        rotary = m.psum("rotary_bank", [P, 512])
        turned = m.banks("turned_bank", 3)

        wr_in = m.sem("wr_in")
        wa_in = [m.sem(f"wa_in{k}") for k in range(KD)]
        x0_in = [m.sem(f"x0_in{k}") for k in range(KD)]
        x_in = m.sem("x_in")
        res_in = m.sem("res_in")
        consts_in = m.sem("consts_in")
        mask_in = m.sem("mask_in")
        wr_split, wa_hi_ready, wa_split = m.sem("wr_split"), m.sem("wa_hi_ready"), m.sem("wa_split")
        x_hi_ready = m.sem("x_hi_ready")
        x_split = m.sem("x_split")
        lat_mm = m.sem("lat_mm")
        rot_mm = m.sem("rot_mm")
        squared = m.sem("squared")
        root_ready = m.sem("root_ready")
        normed = m.sem("normed")
        turn_mm = m.sem("turn_mm")
        turn_hi = m.sem("turn_hi")
        turn_lo = m.sem("turn_lo")
        value_hi = m.sem("value_hi")
        value_lo = m.sem("value_lo")
        rot_read = m.sem("rot_read")
        rot_ready = m.sem("rot_ready")
        rot_hi_ready = m.sem("rot_hi_ready")
        rot_split = m.sem("rot_split")
        pool_step = m.sem("lat_pool_step")
        dve_step = m.sem("lat_dve_step")
        block = stack.enter_context(nc.Block())
        CONSTS = 5

        @block.sync
        def _(sp):
            xt_view = io["x_t"].rearrange("b (k p) n -> b p k n", p=P)
            wa_view = io["w_a"].rearrange("(k p) n -> p k n", p=P)
            res_view = io["x"].rearrange("b (t p) n -> b p t n", p=P)
            sp.dma_start(wr[:], io["w_kr"].rearrange("(k p) n -> p k n", p=P)).then_inc(wr_in, 16)
            for k in range(KD):
                sp.dma_start(x_t[:, k, :], xt_view[0][:, k, :]).then_inc(x0_in[k], 16)
            for k in range(KD):
                sp.dma_start(wa[:, k, :], wa_view[:, k, :]).then_inc(wa_in[k], 16)
            sp.dma_start(kv_gain[:], io["kv_ln"].partition_broadcast(P)).then_inc(consts_in, 16)
            sp.dma_start(g.q_gain[:], io["q_ln"]).then_inc(consts_in, 16)
            for dst, name in ((g.cos, "cos"), (g.sin, "sin"), (g.ident, "ident")):
                sp.dma_start(dst[:], io[name]).then_inc(consts_in, 16)
            with sp.Fori(1, B) as b:
                sp.wait_ge(x_split, KD * b)
                sp.dma_start(x_t[:], xt_view[bass.ds(b, 1)].rearrange("b p k n -> (b p) k n")).then_inc(x_in, 16)
                sp.dma_start(g.res[:, bass.ds(b * QB - QB, QB), :],
                             res_view[bass.ds(b - 1, 1)].rearrange("b p t n -> (b p) t n")).then_inc(res_in, 16)
            sp.dma_start(g.res[:, (B - 1) * QB:, :], res_view[B - 1]).then_inc(res_in, 16)
            load_queries(sp, g, io, 0)
            sp.wait_ge(x_split, KD * B)
            sp.dma_start(x_t[:, 0, 0:P], io["mask"]).then_inc(mask_in, 16)
            sp.wait_ge(res_in, 16 * B)

        def chunk(x_parts, key_parts, b, c):
            return [q[:, c, bass.ts(b, S)] if c < KQ else key[:, bass.ts(b, S)] for q, key in zip(x_parts, key_parts)]

        @block.scalar
        def _(act):
            def square(b, t):
                act.wait_ge(lat_mm, QB * b + t + 1)
                nc.scalar.activation(junk[:, t % 2, 0:QL], product[t][:, 0:QL], ACT.Square, scale=float(QL) ** -0.5,
                                     accum_out=ms[:, t, 0:1])
                nc.scalar.activation(junk[:, t % 2, QL:], product[t][:, QL:QL + KL], ACT.Square, scale=float(KL) ** -0.5,
                                     accum_out=ms[:, t, 1:2]).then_inc(squared, 1)

            def roots(b, half):
                act.wait_ge(squared, QB * b + 2 * half + 2)
                pair = slice(2 * half, 2 * half + 2)
                nc.scalar.activation(rms[:, pair, :], ms[:, pair, :], ACT.Sqrt, bias=eps[:]).then_inc(root_ready, 1)

            def turns(b):
                act.wait_ge(normed, QB * (b + 1))
                nc.scalar.activation(g.val_hi[:, bass.ts(b, QB), :], latent[:, :, QL:], ACT.Copy).then_inc(value_hi, 1)
                for c in range(KQ + 1):
                    act.wait_ge(turn_mm, (KQ + 1) * b + c + 1)
                    nc.scalar.activation(*chunk([g.qn_hi], [g.key_hi], b, c), turned[c % 3][:],
                                         ACT.Copy).then_inc(turn_hi, 1)

            def batch(b, first=False):
                if not first:
                    act.wait_ge(x_in, 16 * b)
                    act.wait_ge(lat_mm, QB * b)
                for k in range(KD):
                    if first:
                        act.wait_ge(x0_in[k], 16)
                    nc.scalar.activation(x_hi[:, k, :], x_t[:, k, :], ACT.Copy).then_inc(x_hi_ready, 1)
                if first:
                    for k in range(KD):
                        act.wait_ge(wa_in[k], 16)
                        nc.scalar.activation(wa_hi[:, k, :], wa[:, k, :], ACT.Copy).then_inc(wa_hi_ready, 1)
                else:
                    square(b - 1, 3)
                    roots(b - 1, 1)
                square(b, 0)
                square(b, 1)
                roots(b, 0)
                act.wait_ge(rot_ready, b + 1)
                nc.scalar.activation(g.kr_hi[:, bass.ts(b, S)], rot[:], ACT.Copy).then_inc(rot_hi_ready, 1)
                if not first:
                    turns(b - 1)
                square(b, 2)

            act.wait_ge(wr_in, 16)
            nc.scalar.activation(wr_hi[:], wr[:], ACT.Copy).then_inc(wr_split, 1)
            batch(0, first=True)
            with act.Fori(1, B) as b:
                batch(b)
            square(B - 1, 3)
            roots(B - 1, 1)
            turns(B - 1)

        @block.vector
        def _(dve):
            start = Chain(dve, dve_step)
            LINKS = 4

            def norm_pair(b, half, base):
                chain = Chain(dve, dve_step, base)
                dve.wait_ge(root_ready, 2 * b + half + 1)
                pair = slice(2 * half, 2 * half + 2)
                r, n, mean = rstd[:, pair, :], nt[:, pair, :], ms[:, pair, :]
                chain.link(nc.vector.reciprocal(r, rms[:, pair, :]))
                chain.link(nc.vector.scalar_tensor_tensor(n, r, -0.5, r, ALU.mult, ALU.mult))
                chain.link(nc.vector.scalar_tensor_tensor(n, mean, RMS_EPS, n, ALU.add, ALU.mult))
                chain.link(nc.vector.scalar_tensor_tensor(r, n, 1.5, r, ALU.add, ALU.mult))
                for t in range(2 * half, 2 * half + 2):
                    nc.vector.tensor_scalar(latent[:, t, 0:QL], product[t][:, 0:QL], rstd[:, t, 0:1],
                                            None, ALU.mult)
                    nc.vector.scalar_tensor_tensor(latent[:, t, QL:], product[t][:, QL:], rstd[:, t, 1:2],
                                                   kv_gain[:], ALU.mult, ALU.mult).then_inc(normed, 1)

            def turns(b):
                for c in range(KQ + 1):
                    dve.wait_ge(turn_hi, (KQ + 1) * b + c + 1)
                    hi, lo = chunk([g.qn_hi, g.qn_lo], [g.key_hi, g.key_lo], b, c)
                    nc.vector.tensor_tensor(lo, turned[c % 3][:], hi.bitcast(F32), ALU.subtract).then_inc(turn_lo, 1)

            def batch(b, base, first=False):
                for k in range(KD):
                    dve.wait_ge(x_hi_ready, KD * b + k + 1)
                    nc.vector.tensor_tensor(x_lo[:, k, :], x_t[:, k, :], x_hi[:, k, :].bitcast(F32),
                                            ALU.subtract).then_inc(x_split, 1)
                if first:
                    for k in range(KD):
                        dve.wait_ge(wa_hi_ready, k + 1)
                        nc.vector.tensor_tensor(wa_lo[:, k, :], wa[:, k, :], wa_hi[:, k, :].bitcast(F32),
                                                ALU.subtract).then_inc(wa_split, 1)
                    dve.wait_ge(consts_in, 16 * CONSTS)
                dve.wait_ge(rot_mm, b + 1)
                nc.vector.tensor_tensor(rot[:], rotary[:], g.cos[:], ALU.mult)
                nc.vector.stream_shuffle(rot_swapped[:], rotary[:], SWAP).then_inc(rot_read, 1)
                if not first:
                    norm_pair(b - 1, 1, base)
                    turns(b - 1)
                dve.wait_ge(rot_hi_ready, b + 1)
                nc.vector.tensor_tensor(g.kr_lo[:, bass.ts(b, S)], rot[:], g.kr_hi[:, bass.ts(b, S)].bitcast(F32),
                                        ALU.subtract).then_inc(rot_split, 1)
                if not first:
                    dve.wait_ge(value_lo, b)
                norm_pair(b, 0, base if first else base + LINKS)
                dve.wait_ge(rot_split, b + 1)

            nc.vector.memset(eps[:], RMS_EPS)
            dve.wait_ge(wr_split, 1)
            nc.vector.tensor_tensor(wr_lo[:], wr[:], wr_hi[:].bitcast(F32), ALU.subtract).then_inc(wr_split, 1)
            batch(0, 0, first=True)
            with dve.Fori(1, B) as b:
                batch(b, LINKS * (2 * b - 1))
            norm_pair(B - 1, 1, LINKS * (2 * B - 1))
            turns(B - 1)
            nc.vector.tensor_copy(g.ident_b[:], g.ident[:])
            dve.wait_ge(mask_in, 16)
            nc.vector.tensor_copy(g.mask[:], x_t[:, 0, 0:P])
            nc.vector.tensor_scalar(g.q_gain[:], g.q_gain[:], SCALE, None, ALU.mult)

        @block.gpsimd
        def _(pool):
            def rotate(b):
                pool.wait_ge(rot_read, b + 1)
                nc.gpsimd.tensor_tensor(rot_swapped[:], rot_swapped[:], g.sin[:], ALU.mult).then_inc(pool_step, 1)
                pool.wait_ge(pool_step, b + 1)
                nc.gpsimd.tensor_tensor(rot[:], rot[:], rot_swapped[:], ALU.add).then_inc(rot_ready, 1)

            def values(b):
                pool.wait_ge(value_hi, b + 1)
                nc.gpsimd.tensor_tensor(g.val_lo[:, bass.ts(b, QB), :], latent[:, :, QL:],
                                        g.val_hi[:, bass.ts(b, QB), :].bitcast(F32), ALU.subtract).then_inc(value_lo, 1)

            pool.wait_ge(consts_in, 16 * CONSTS)
            rotate(0)
            with pool.Fori(1, B) as b:
                rotate(b)
                values(b - 1)
            values(B - 1)

        @block.tensor
        def _(pe):
            def turns(b):
                pe.wait_ge(normed, QB * (b + 1))
                for c in range(KQ + 1):
                    if c == 3:
                        pe.wait_ge(turn_lo, (KQ + 1) * b + 1)
                    for t in range(QB):
                        last = nc.tensor.transpose(turned[c % 3][:, t * P:(t + 1) * P],
                                                   latent[:, t, c * P:(c + 1) * P], g.ident[:])
                    last.then_inc(turn_mm, 1)

            def batch(b, first=False):
                for k in range(KD):
                    pe.wait_ge(x_split, KD * b + k + 1)
                    last = split_matmul(nc, rotary[:], wr_hi[:, k, :], wr_lo[:, k, :], x_hi[:, k, :],
                                        x_lo[:, k, :], k == 0, k == KD - 1)
                last.then_inc(rot_mm, 1)
                for t in range(QB):
                    if t == 2 and not first:
                        turns(b - 1)
                    for k in range(KD):
                        if first and t == 0:
                            pe.wait_ge(wa_split, k + 1)
                        last = split_matmul(nc, product[t][:], x_hi[:, k, t * P:(t + 1) * P],
                                            x_lo[:, k, t * P:(t + 1) * P], wa_hi[:, k, :], wa_lo[:, k, :],
                                            k == 0, k == KD - 1)
                    last.then_inc(lat_mm, 1)

            pe.wait_ge(wr_split, 2)
            batch(0, first=True)
            with pe.Fori(1, B) as b:
                batch(b)
            turns(B - 1)


def attention_phase(nc, g, io):
    NS = 2 * B
    with ExitStack() as stack:
        m = Space(nc, stack)
        raw_q, raw_k, raw_r = g.raw_q, g.raw_k, g.raw_r
        raw_v = m.sb("raw_v", [P, 2, KL])
        raw_o = m.sb("raw_o", [P, 2, D])
        wq_hi = m.sb("wq_hi", [P, 2, KQ, KL], F32R)
        wq_lo = m.sb("wq_lo", [P, 2, KQ, KL], F32R)
        wr_hi = m.sb("wr_hi", [P, KQ, P], F32R)
        wr_lo = m.sb("wr_lo", [P, KQ, P], F32R)
        wo_hi = m.sb("wo_hi", [P, 2, D], F32R)
        wo_lo = m.sb("wo_lo", [P, 2, D], F32R)
        q_hi = m.sb("q_hi", [P, S], F32R)
        q_lo = m.sb("q_lo", [P, S], F32R)
        rot = m.sb("qrot", [P, S])
        rot_swapped = m.sb("qrot_swapped", [P, S])
        qr = m.sb("qr_stacked", [P, 2, S], F32R)
        probs = m.sb("probs", [P, 2, sum(SEEN)])
        neg_max = m.sb("neg_max", [P, 2, QB])
        row_sum = m.sb("row_sum", [P, 2, QB])
        row_inv = m.sb("row_inv", [P, 2, QB])
        pt_hi = m.sb("pt_hi", [P, sum(SEEN)], F32R)
        pt_lo = m.sb("pt_lo", [P, sum(SEEN)], F32R)
        mix_hi = m.sb("mix_hi", [P, 2, S], F32R)
        mix_lo = m.sb("mix_lo", [P, 2, S], F32R)
        score = m.banks("score_bank", 3)
        turned = m.banks("prob_bank", 2)
        front = m.psum("front_bank", [P, 512])
        mixed = m.psum("mixed_bank", [P, 512])
        outp = m.psum("out_bank", [P, 512])

        GROUPS = ((3,), (2, 0), (1,))
        NG = len(GROUPS)
        DIAGONALS = (slice(3 * P, S), slice(2 * P, S), slice(P, 2 * P))

        def score_at(q):
            bank, at = {3: (0, 0), 2: (1, 0), 0: (1, 3 * P), 1: (2, 0)}[q]
            return score[bank][:, at:at + SEEN[q]]

        def probs_at(h, q, start, size):
            at = sum(SEEN[:q]) + start
            return probs[:, h, at:at + size]

        def pt_at(x, k):
            at = sum(S - i * P for i in range(k))
            return x[:, at:at + S - k * P]

        def turned_at(k):
            bank, at = {0: (turned[0], 0), 1: (turned[1], 0), 3: (turned[1], 3 * P), 2: (score[2], 2 * P)}[k]
            return bank[:, at:at + S - k * P]

        fold_in, rope_in = g.fold_in, g.rope_in
        outw_in = m.sem("outw_in")
        front_mm = m.sem("front_mm")
        outw_hi = m.sem("outw_hi")
        q_hi_ready = m.sem("q_hi_ready")
        q_ready = m.sem("q_ready")
        wq_ready = m.sem("wq_ready")
        wr_ready = m.sem("wr_ready")
        wo_ready = m.sem("wo_ready")
        rope_read = m.sem("rope_read")
        rope_swapped = m.sem("rope_swapped")
        rope_turned = m.sem("rope_turned")
        rope_hi = m.sem("rope_hi")
        rope_ready = m.sem("rope_ready")
        score_mm = m.sem("score_mm")
        masked = m.sem("masked")
        max_ready = m.sem("max_ready")
        exp_done = m.sem("exp_done")
        inv_ready = m.sem("inv_ready")
        probs_ready = m.sem("probs_ready")
        turn_mm = m.sem("pturn_mm")
        turn_hi = m.sem("pturn_hi")
        turn_lo = m.sem("pturn_lo")
        mix_mm = m.sem("mix_mm")
        mix_hi_ready = m.sem("mix_hi_ready")
        mix_ready = m.sem("mix_ready")
        out_mm = m.sem("out_mm")
        out_added = m.sem("out_added")
        split_step = m.sem("split_step")
        block = stack.enter_context(nc.Block())

        FRONT = 16

        def front_uses(s, last):
            uses = [("rope", s // 2 + 1)] if s % 2 and not (last and s == NS - 1) else []
            if not (last and s == NS - 1):
                uses.append(("query", s + 1))
            if s in (1, 2):
                uses.append(("outw", s - 1))
            if s in (6, 7) and not last:
                uses.append(("wq", s - 6))
            return uses

        def front_index(s, last):
            return 4 + sum(len(front_uses(i, False)) for i in range(s))

        PROLOGUE = [("wq", 0, mixed), ("wq", 1, turned[0]), ("rope", 0, front), ("query", 0, outp)]
        READ_PROLOGUE = [(i, *PROLOGUE[i]) for i in (0, 2, 3, 1)]

        @block.sync
        def _(sp):
            wv_n = io["w_kv"][:, NOPE:, :].rearrange("h d c -> d h c")
            wo_n = io["w_o_t"].rearrange("(h p) n -> p h n", p=P)

            def load_outputs(p):
                sp.dma_start(raw_v[:], wv_n[:, bass.ts(p, 2), :]).then_inc(outw_in, 16)
                sp.dma_start(raw_o[:], wo_n[:, bass.ts(p, 2), :]).then_inc(outw_in, 16)

            load_outputs(0)
            with sp.Fori(1, NP) as p:
                sp.wait_ge(wq_ready, 2 * p)
                sp.wait_ge(wr_ready, p)
                load_queries(sp, g, io, p)
                sp.wait_ge(wo_ready, 2 * p)
                load_outputs(p)

        def over_pairs(engine, pair):
            pair(0, True, False)
            with engine.Fori(1, NP - 1) as p:
                pair(p, False, False)
            pair(NP - 1, False, True)

        @block.tensor
        def _(pe):
            before = [None]

            def front_one(p, kind, a, front=front):
                if before[0]:
                    p0, kind0, a0 = before[0]
                    read, count = {"wq": (wq_ready, 2), "outw": (wo_ready, 2), "rope": (rope_read, B),
                                   "query": (q_ready, NS)}[kind0]
                    pe.wait_ge(read, count * p0 + a0 + 1)
                    before[0] = (p, kind, a)
                if kind == "wq":
                    pe.wait_ge(fold_in, (p + 1) * 32)
                    for c in range(KQ):
                        last = nc.tensor.matmul(front[:, c * KL:(c + 1) * KL], raw_q[:, a, c * P:(c + 1) * P],
                                                raw_k[:, a, :], start=True, stop=True)
                elif kind == "outw":
                    pe.wait_ge(outw_in, (p + 1) * 32)
                    last = nc.tensor.matmul(front[:], raw_v[:, a, :], raw_o[:, a, :], start=True, stop=True)
                elif kind == "rope":
                    if a % B == 0:
                        pe.wait_ge(wr_ready, p + 1)
                    b = a % B
                    for c in range(KQ):
                        last = split_matmul(nc, front[:], wr_hi[:, c, :], wr_lo[:, c, :],
                                            g.qn_hi[:, c, b * S:(b + 1) * S], g.qn_lo[:, c, b * S:(b + 1) * S],
                                            c == 0, c == KQ - 1)
                else:
                    h, b = a % 2, a // 2
                    if b == 0:
                        pe.wait_ge(wq_ready, 2 * p + h + 1)
                    for c in range(KQ):
                        last = split_matmul(nc, front[:], wq_hi[:, h, c, :], wq_lo[:, h, c, :],
                                            g.qn_hi[:, c, b * S:(b + 1) * S], g.qn_lo[:, c, b * S:(b + 1) * S],
                                            c == 0, c == KQ - 1)
                last.then_inc(front_mm, 1)

            def place(p, kind, a):
                if kind == "wq":
                    return p + 1, kind, a
                if (kind == "rope" and a == B) or (kind == "query" and a == NS):
                    return p + 1, kind, 0
                return p, kind, a

            def scores(p, s):
                b, h = s // 2, s % 2
                pe.wait_ge(q_ready, NS * p + s + 1)
                pe.wait_ge(rope_ready, B * p + b + 1)
                past(pe, exp_done, NG * (NS * p + s))
                for q in [q for group in GROUPS for q in group]:
                    n, tile = SEEN[q], slice(q * P, (q + 1) * P)
                    out = score_at(q)
                    keys = slice(b * S, b * S + n)
                    split_matmul(nc, out, q_hi[:, tile], q_lo[:, tile], g.key_hi[:, keys], g.key_lo[:, keys],
                                 True, False)
                    nc.tensor.matmul(out, qr[:, h, tile], g.kr_hi[:, keys], start=False, stop=False)
                    last = nc.tensor.matmul(out, qr[:, h, tile], g.kr_lo[:, keys], start=False, stop=h == 1)
                    if h == 0:
                        last = nc.tensor.matmul(out[:, q * P:n], g.ident_b[:], g.mask[:], start=False, stop=True)
                    if q != 2:
                        last.then_inc(score_mm, 1)

            def turn(j, s, parts, scored=0):
                h = s % 2
                if 0 in parts:
                    pe.wait_ge(probs_ready, j + 1)
                    past(pe, turn_lo, 3 * j)
                if 2 in parts:
                    pe.wait_ge(exp_done, scored)
                for k in parts:
                    for q in range(k, QB):
                        last = nc.tensor.transpose(turned_at(k)[:, (q - k) * P:(q - k + 1) * P],
                                                   probs_at(h, q, k * P, P), g.ident[:])
                    if k != 1:
                        last.then_inc(turn_mm, 1)

            def mix(j, s, n_out):
                b = s // 2
                past(pe, mix_ready, j)
                if n_out is not None:
                    pe.wait_ge(out_added, n_out)
                for i, (k, ready) in enumerate(((0, 1), (1, 2), (3, 2), (2, 3))):
                    pe.wait_ge(turn_lo, 3 * j + ready)
                    t = b * QB + k
                    last = split_matmul(nc, mixed[:, k * P:S], g.val_hi[:, t, :], g.val_lo[:, t, :],
                                        pt_at(pt_hi, k), pt_at(pt_lo, k), i == 0, i == QB - 1)
                last.then_inc(mix_mm, 1)

            def project(n, tiles):
                for t in tiles:
                    if t == 0:
                        pe.wait_ge(mix_ready, 2 * n + 2)
                        past(pe, out_added, QB * n)
                    bank = outp if t % 2 == 0 else mixed
                    if t >= 2:
                        pe.wait_ge(out_added, QB * n + t - 1)
                    for h in range(2):
                        last = split_matmul(nc, bank[:], mix_hi[:, h, t * P:(t + 1) * P],
                                            mix_lo[:, h, t * P:(t + 1) * P], wo_hi[:, h, :], wo_lo[:, h, :],
                                            h == 0, h == 1)
                    last.then_inc(out_mm, 1)

            def pair(p, first, last):
                for s in range(NS):
                    j = NS * p + s
                    back = not (first and s == 0)
                    uses = [place(p, *u) for u in front_uses(s, last)]
                    if s == 0:
                        before[0] = (p, "wq", 1)
                    scores(p, s)
                    if s % 2 == 0:
                        if back:
                            turn(j - 1, (s - 1) % NS, (0, 1, 3))
                        front_one(*uses[0])
                        if back:
                            turn(j - 1, (s - 1) % NS, (2,), NG * (j + 1))
                            mix(j - 1, (s - 1) % NS, None)
                        rest = 1
                    else:
                        n = B * p + s // 2 - 1
                        out = not (first and s == 1)
                        rest = 0
                        if uses and uses[0][1] == "rope":
                            front_one(*uses[0])
                            rest = 1
                        turn(j - 1, s - 1, (0, 1, 3))
                        if out:
                            if s == 3:
                                pe.wait_ge(wo_ready, 2 * p + 2)
                            project(n, (0, 1))
                        turn(j - 1, s - 1, (2,), NG * (j + 1))
                        if out:
                            project(n, (2, 3))
                        if len(uses) > rest and uses[rest][1] == "query":
                            front_one(*uses[rest])
                            rest += 1
                        mix(j - 1, s - 1, QB * (n + 1) if out else None)
                    for i in range(rest, len(uses)):
                        front_one(*uses[i])

            for kind, a, bank in PROLOGUE:
                front_one(0, kind, a, bank)
            over_pairs(pe, pair)
            j = NS * NP - 1
            turn(j, NS - 1, (0, 1, 3, 2), NG * (j + 1))
            mix(j, NS - 1, QB * (B * NP - 1))
            project(B * NP - 1, range(QB))

        @block.scalar
        def _(act):
            def front_one(kind, p, a, index, front=front):
                if kind == "outw":
                    act.wait_ge(front_mm, index + 1)
                    nc.scalar.activation(wo_hi[:, a, :], front[:], ACT.Copy).then_inc(outw_hi, 1)
                elif kind == "query":
                    act.wait_ge(front_mm, index + 1)
                    nc.scalar.activation(q_hi[:], front[:], ACT.Copy).then_inc(q_hi_ready, 1)
                elif kind == "rope":
                    act.wait_ge(rope_turned, B * p + a + 1)
                    nc.scalar.activation(qr[0:64, 0, :], rot[0:64, :], ACT.Copy)
                    nc.scalar.activation(qr[64:P, 1, :], rot[64:P, :], ACT.Copy).then_inc(rope_hi, 1)

            def softmax(j, h, first_two):
                if not first_two:
                    act.wait_ge(turn_mm, 3 * (j - 1))
                for i, group in enumerate(GROUPS):
                    act.wait_ge(max_ready, NG * j + i + 1)
                    for q in group:
                        last = nc.scalar.activation(probs_at(h, q, 0, SEEN[q]), score_at(q), ACT.Exp,
                                                    bias=neg_max[:, h, q:q + 1], accum_out=row_sum[:, h, q:q + 1])
                    last.then_inc(exp_done, 1)

            def turn(j, parts):
                for i in parts:
                    act.wait_ge(turn_mm, 3 * j + i + 1)
                    for k in ((0,), (1, 3), (2,))[i]:
                        last = nc.scalar.activation(pt_at(pt_hi, k), turned_at(k), ACT.Copy)
                    last.then_inc(turn_hi, 1)

            def mix(j, h):
                act.wait_ge(mix_mm, j + 1)
                nc.scalar.activation(mix_hi[:, h, :], mixed[:], ACT.Copy).then_inc(mix_hi_ready, 1)

            def pair(p, first, last):
                for s in range(NS):
                    j = NS * p + s
                    back = not (first and s == 0)
                    uses = front_uses(s, last)
                    index = FRONT * p + front_index(s, last)
                    softmax(j, s % 2, first and s < 2)
                    if back:
                        turn(j - 1, (0, 1, 2))
                    for i, (kind, a) in enumerate(uses):
                        if kind in ("rope", "query"):
                            front_one(kind, p, a, index + i)
                    if back:
                        mix(j - 1, (s - 1) % 2)
                    for i, (kind, a) in enumerate(uses):
                        if kind == "outw":
                            front_one(kind, p, a, index + i)

            for i, kind, a, bank in READ_PROLOGUE:
                front_one(kind, 0, a, i, bank)
            over_pairs(act, pair)
            turn(NS * NP - 1, (0, 1, 2))
            mix(NS * NP - 1, 1)

        @block.vector
        def _(dve):
            def split_columns(hi, lo, src, chain_at, ready):
                for c in range(KQ):
                    last = nc.vector.tensor_scalar(hi[:, c, :], src[:, c, :], g.q_gain[:, c:c + 1], None, ALU.mult)
                last.then_inc(split_step, 1)
                dve.wait_ge(split_step, chain_at)
                for c in range(KQ):
                    last = nc.vector.scalar_tensor_tensor(lo[:, c, :], src[:, c, :], g.q_gain[:, c:c + 1],
                                                          hi[:, c, :].bitcast(F32), ALU.mult, ALU.subtract)
                return last.then_inc(ready, 1)

            def split_rotary(p):
                dve.wait_ge(rope_in, 16 * (p + 1))
                split_columns(wr_hi, wr_lo, raw_r, 3 * p + 1, wr_ready)

            def front_one(kind, p, a, index, front=front):
                if kind == "wq":
                    dve.wait_ge(front_mm, index + 1)
                    src = front[:, 0:KQ * KL].rearrange("p (c n) -> p c n", c=KQ)
                    split_columns(wq_hi[:, a], wq_lo[:, a], src, 3 * p + a + 2, wq_ready)
                elif kind == "outw":
                    dve.wait_ge(outw_hi, 2 * p + a + 1)
                    nc.vector.tensor_tensor(wo_lo[:, a, :], front[:], wo_hi[:, a, :].bitcast(F32),
                                            ALU.subtract).then_inc(wo_ready, 1)
                elif kind == "rope":
                    dve.wait_ge(front_mm, index + 1)
                    past(dve, rope_ready, B * p + a)
                    nc.vector.tensor_tensor(rot[:], front[:], g.cos[:], ALU.mult)
                    nc.vector.stream_shuffle(rot_swapped[:], front[:], SWAP).then_inc(rope_read, 1)
                else:
                    dve.wait_ge(q_hi_ready, NS * p + a + 1)
                    nc.vector.tensor_tensor(q_lo[:], front[:], q_hi[:].bitcast(F32),
                                            ALU.subtract).then_inc(q_ready, 1)

            def maxima(j, h, pairs_before):
                for i, group in enumerate(GROUPS):
                    dve.wait_ge(score_mm, NG * j + i + 1)
                    if h:
                        diagonal = score[i][:, DIAGONALS[i]].rearrange("p (q k) -> p q k", k=P)
                        nc.vector.tensor_tensor(diagonal, diagonal,
                                                g.mask[:].unsqueeze(1).to_broadcast([P, len(group), P]),
                                                ALU.add).then_inc(masked, 1)
                        dve.wait_ge(masked, NG * pairs_before + i + 1)
                    for q in group:
                        last = nc.vector.tensor_reduce(neg_max[:, h, q:q + 1], score_at(q), AX_X, ALU.max, negate=True)
                    last.then_inc(max_ready, 1)

            def normalise(j, h):
                dve.wait_ge(exp_done, NG * (j + 1))
                nc.vector.reciprocal(row_inv[:, h, :], row_sum[:, h, :]).then_inc(inv_ready, 1)
                dve.wait_ge(inv_ready, j + 1)
                for q in range(QB):
                    row = probs_at(h, q, 0, SEEN[q])
                    last = nc.vector.tensor_scalar(row, row, row_inv[:, h, q:q + 1], None, ALU.mult)
                last.then_inc(probs_ready, 1)

            def turn(j, parts):
                for i in parts:
                    dve.wait_ge(turn_hi, 3 * j + i + 1)
                    for k in ((0,), (1, 3), (2,))[i]:
                        last = nc.vector.tensor_tensor(pt_at(pt_lo, k), turned_at(k),
                                                       pt_at(pt_hi, k).bitcast(F32), ALU.subtract)
                    last.then_inc(turn_lo, 1)

            def mix(j, h):
                dve.wait_ge(mix_hi_ready, j + 1)
                nc.vector.tensor_tensor(mix_lo[:, h, :], mixed[:], mix_hi[:, h, :].bitcast(F32),
                                        ALU.subtract).then_inc(mix_ready, 1)

            def add(n, b, tiles, complete=False):
                for t in tiles:
                    bank = outp if t % 2 == 0 else mixed
                    row = g.res[:, b * QB + t, :]
                    dve.wait_ge(out_mm, QB * n + t + 1)
                    nc.vector.tensor_tensor(row, bank[:], row, ALU.add).then_inc(out_added, 1)
                if complete:
                    for t in tiles:
                        dve.wait_ge(out_added, QB * n + t + 1)
                        nc.vector.bn_stats(g.stats[:, b * QB + t, :], g.res[:, b * QB + t, :])

            def pair(p, first, last):
                for s in range(NS):
                    j = NS * p + s
                    back = not (first and s == 0)
                    uses = front_uses(s, last)
                    index = FRONT * p + front_index(s, last)

                    def use(kinds):
                        for i, (kind, a) in enumerate(uses):
                            if kind in kinds:
                                if kind == "wq":
                                    front_one(kind, p + 1, a, index + i)
                                else:
                                    front_one(kind, p, a, index + i)

                    maxima(j, s % 2, B * p + s // 2)
                    if s % 2 == 0:
                        if back:
                            turn(j - 1, (0, 1))
                        if back:
                            turn(j - 1, (2,))
                        use(("query",))
                        normalise(j, 0)
                        if back:
                            mix(j - 1, 1)
                    else:
                        n, b = B * p + s // 2 - 1, (s // 2 - 1) % B
                        out = not (first and s == 1)
                        use(("rope",))
                        turn(j - 1, (0, 1))
                        if out:
                            add(n, b, (0, 1), last and s > 1)
                        turn(j - 1, (2,))
                        if out:
                            add(n, b, (2, 3), last and s > 1)
                        normalise(j, 1)
                        use(("query",))
                        mix(j - 1, 0)
                        if s == 5 and not last:
                            split_rotary(p + 1)
                    use(("outw", "wq"))

            split_rotary(0)
            for i, kind, a, bank in READ_PROLOGUE:
                front_one(kind, 0, a, i, bank)
            over_pairs(dve, pair)
            turn(NS * NP - 1, (0, 1, 2))
            mix(NS * NP - 1, 1)
            for t in range(QB):
                add(B * NP - 1, B - 1, (t,), True)

        @block.gpsimd
        def _(pool):
            def rope(n):
                pool.wait_ge(rope_read, n + 1)
                nc.gpsimd.tensor_tensor(rot_swapped[:], rot_swapped[:], g.sin[:], ALU.mult).then_inc(rope_swapped, 1)
                pool.wait_ge(rope_swapped, n + 1)
                nc.gpsimd.tensor_tensor(rot[:], rot[:], rot_swapped[:], ALU.add).then_inc(rope_turned, 1)
                pool.wait_ge(rope_hi, n + 1)
                nc.gpsimd.tensor_tensor(qr[64:P, 0, :], rot[0:64, :], qr[0:64, 0, :].bitcast(F32), ALU.subtract)
                nc.gpsimd.tensor_tensor(qr[0:64, 1, :], rot[64:P, :], qr[64:P, 1, :].bitcast(F32),
                                        ALU.subtract).then_inc(rope_ready, 1)

            with pool.Fori(0, B * NP) as n:
                rope(n)


def inverse_root(nc, chain, x, y, t):
    xi, yi = x.bitcast(I32), y.bitcast(I32)
    chain.link(nc.vector.tensor_scalar(yi, xi, 1, None, ALU.logical_shift_right))
    chain.link(nc.vector.tensor_scalar(yi, yi, -1.0, float(0x5F3759DF), ALU.mult, ALU.add))
    for _ in range(3):
        chain.link(nc.vector.scalar_tensor_tensor(t, y, -0.5, y, ALU.mult, ALU.mult))
        chain.link(nc.vector.tensor_tensor(t, t, x, ALU.mult))
        chain.link(nc.vector.scalar_tensor_tensor(y, t, 1.5, y, ALU.add, ALU.mult))


ROOT_LINKS = 11


def norm_stats(nc, chain, space, rows, n):
    stats, *_, carry = space
    nc.vector.memset(carry[:, 0:1], 0.0)
    for t in range(n):
        last = nc.vector.bn_stats(stats[:, t, :], rows(t))
    chain.link(last)


def norm_factors(nc, chain, space, n):
    stats, mean_var, inv, variance, t0, carry = space
    nc.vector.memset(carry[:, 1:2], 0.0)
    for t in range(n):
        last = nc.vector.bn_aggr(mean_var[:, t, :], stats[:, t, :])
    chain.link(last)
    chain.link(nc.vector.tensor_scalar(variance[:], mean_var[:, :, 1], LN_EPS, None, ALU.add))
    inverse_root(nc, chain, variance[:], inv[:], t0[:])


def norm_apply(nc, space, rows, tiles):
    _, mean_var, inv, *_ = space
    for t in tiles:
        last = nc.vector.tensor_scalar(rows(t), rows(t), mean_var[:, t, 0:1], inv[:, t:t + 1],
                                       ALU.subtract, ALU.mult)
    return last


def norm_space(m, name, n, stats=None):
    return (stats or m.sb(f"{name}_stats", [P, n, 6]), m.sb(f"{name}_mean_var", [P, n, 2]), m.sb(f"{name}_inv", [P, n]),
            m.sb(f"{name}_variance", [P, n]), m.sb(f"{name}_t", [P, n]), m.sb(f"{name}_carry", [P, 2]))


def quant_phase(nc, g, io):
    U = 2
    with ExitStack() as stack:
        m = Space(nc, stack)
        both = range(U)
        w1 = m.sb("w1_rows", [P, U, KD, D])
        w2 = m.sb("w2_rows", [P, U, KD, INNER])
        hidden = m.sb("hidden", [P, U, QB, D])
        gated = m.sb("gated", [P, U, QB, INNER])
        amax = m.sb("amax", [P, U, 2, D])
        w_row = m.sb("w_s_row", [P, U, D])
        quant_t = m.sb("quantised_t", [P, U, 2, KD, D], BF16)
        top = m.sb("top", [P, U, 2, KD])
        ratio = m.sb("ratio", [P, U, KD])
        root = m.sb("root", [P, U, KD])
        tiny = m.sb("tiny", [P, U, KD])
        factor = m.sb("factor", [P, U, 2, KD])
        rowmax = m.sb("rowmax", [P, U, 2, KD])
        step = m.sb("step", [P, U, 2, KD])
        per = m.sb("per", [P, U, 2, KD])
        norm = norm_space(m, "norm", NT, g.stats)
        shift = m.sb("norm_shift", [P, NT])
        round_bias = m.sb("round_bias", [P, 2])
        bank = [m.banks(f"quant_bank{u}_", 4) for u in both]

        def sems(name):
            return [m.sem(f"{name}{u}") for u in both]

        w1_in, w2_in, amax_ready, top_mm = sems("w1_in"), sems("w2_in"), sems("amax_ready"), sems("top_mm")
        spread_mm, row_copied, w_scaled = sems("spread_mm"), sems("row_copied"), sems("w_scaled")
        per_ready, x_rounded, w_rounded, clamped = sems("per_ready"), sems("x_rounded"), sems("w_rounded"), sems("clamped")
        qturn_mm, turn_read = sems("qturn_mm"), (sems("x_turn_read"), sems("w_turn_read"))
        step_mm, step_read, qout_mm, qout_read = sems("step_mm"), sems("step_read"), sems("qout_mm"), sems("qout_read")
        silu_done, gate_done, res_added = sems("silu_done"), sems("gate_done"), sems("res_added")
        factor_ready = m.sem("factor_ready")
        factors_ready, normed_act = m.sem("norm_factors_ready"), m.sem("normed_act")
        res_added_dve = m.sem("res_added_dve")
        dve_step = m.sem("quant_dve_step")
        block = stack.enter_context(nc.Block())

        LINEARS = ((0, w1, KD), (1, w2, INNER // P))
        ROUNDS = B // U
        TURNS = 2 * sum(n for *_, n in LINEARS)

        def turns_before(c, i, side):
            return TURNS * c + 2 * KD * i + side * LINEARS[i][2]

        def reads_before(c, i):
            return TURNS // 2 * c + KD * i

        @block.sync
        def _(sp):
            def load(c, w, sem, name, u):
                view = io[name].rearrange("b (t p) n -> b p t n", p=P)[bass.ds(c * U + u, 1)]
                sp.dma_start(w[:, u], view.rearrange("b p t n -> (b p) t n")).then_inc(sem[u], 16)

            for w, sem, name in ((w1, w1_in, "w_gate_up"), (w2, w2_in, "w_down")):
                for u in both:
                    load(0, w, sem, name, u)
            for i, name in enumerate(("w_g", "w_u", "w_d")):
                sp.dma_start(g.raw[i][:], io[name][0].rearrange("(k p) n -> p k n", p=P)).then_inc(g.expert_in[i], 16)
            with sp.Fori(1, ROUNDS) as c:
                for u in both:
                    sp.wait_ge(qturn_mm[u], turns_before(c - 1, 1, 0))
                    load(c, w1, w1_in, "w_gate_up", u)
                for u in both:
                    sp.wait_ge(qturn_mm[u], turns_before(c, 0, 0))
                    load(c, w2, w2_in, "w_down", u)

        @block.scalar
        def _(act):
            def normalise(count, first):
                act.wait_ge(factors_ready, count)
                for t in range(first, NT):
                    row = g.res[:, t, :]
                    last = nc.scalar.activation(row, row, ACT.Identity, bias=shift[:, t:t + 1],
                                                scale=norm[2][:, t:t + 1])
                    if (t + 1) % QB == 0:
                        last.then_inc(normed_act, 1)

            normalise(1, QB)
            with act.Fori(0, ROUNDS) as c:
                for i, w, n in LINEARS:
                    width = n * P

                    def round_x(u):
                        act.wait_ge(per_ready[u], 2 * (2 * c + i) + 1)
                        for t in range(QB):
                            row = hidden[:, u, t, 0:width]
                            last = nc.scalar.activation(row, row, ACT.Identity, bias=round_bias[:, 0:1],
                                                        scale=per[:, u, 0, t:t + 1])
                        last.then_inc(x_rounded[u], 1)

                    def read_turns(u, side):
                        for k in range(n):
                            act.wait_ge(qturn_mm[u], turns_before(c, i, side) + k + 1)
                            nc.scalar.activation(quant_t[:, u, side, k, :], bank[u][k][:], ACT.Identity,
                                                 bias=round_bias[:, 1:2]).then_inc(turn_read[side][u], 1)

                    for u in both:
                        act.wait_ge(spread_mm[u], 2 * (2 * c + i) + 2)
                        nc.scalar.activation(w_row[:, u, 0:width], bank[u][3][:, 0:width],
                                             ACT.Copy).then_inc(row_copied[u], 1)
                    round_x(0)
                    round_x(1)
                    read_turns(0, 0)
                    read_turns(1, 0)
                    read_turns(0, 1)
                    read_turns(1, 1)
                    for u in both:
                        act.wait_ge(step_mm[u], 2 * c + i + 1)
                        nc.scalar.activation(w_row[:, u, :], bank[u][0][:], ACT.Copy).then_inc(step_read[u], 1)
                    if i == 0:
                        for u in both:
                            act.wait_ge(qout_read[u], 2 * QB * c + QB)
                            nc.scalar.activation(gated[:, u], hidden[:, u, :, 0:INNER], ACT.Silu).then_inc(silu_done[u], 1)
            normalise(2, NT // 2)

        @block.vector
        def _(dve):
            start = Chain(dve, dve_step)
            nc.vector.memset(round_bias[:, 0:1], ROUND)
            start.link(nc.vector.memset(round_bias[:, 1:2], -ROUND))

            def normalise(n_first):
                norm_factors(nc, start, norm, NT)
                nc.vector.scalar_tensor_tensor(shift[:], norm[1][:, :, 0], -1.0, norm[2][:], ALU.mult,
                                               ALU.mult).then_inc(factors_ready, 1)
                return norm_apply(nc, norm, lambda t: g.res[:, t, :], range(n_first))

            start.link(normalise(QB))
            LINKS = 2 * (6 + ROOT_LINKS + U * 5)
            with dve.Fori(0, ROUNDS) as c:
                chain = Chain(dve, dve_step, start.n + c * LINKS)

                def tile(t, n=1):
                    return g.res[:, bass.ds(c * U * QB + t, n), :]

                def source(u, i):
                    return gated[:, u] if i else tile(u * QB, QB)

                def largest(w, u, width):
                    dve.wait_ge((w2_in if w is w2 else w1_in)[u], 16 * (c + 1))
                    nc.vector.tensor_reduce(amax[:, u, 1, 0:width], w[:, u].rearrange("p t k -> p k t"), AX_X,
                                            ALU.max, apply_absolute_value=True).then_inc(amax_ready[u], 1)

                for u in both:
                    largest(w1, u, D)
                for i, w, n in LINEARS:
                    width = n * P

                    for u in both:
                        if i == 1:
                            dve.wait_ge(silu_done[u], c + 1)
                            nc.vector.tensor_tensor(gated[:, u], gated[:, u], hidden[:, u, :, INNER:],
                                                    ALU.mult).then_inc(gate_done[u], 1)
                            dve.wait_ge(gate_done[u], c + 1)
                        elif u == 0:
                            dve.wait_ge(normed_act, 2 * c + 1)
                            nc.vector.memset(norm[5][:, 0:1], 0.0)
                        nc.vector.tensor_reduce(amax[:, u, 0, 0:width], source(u, i).rearrange("p t k -> p k t"), AX_X,
                                                ALU.max, apply_absolute_value=True).then_inc(amax_ready[u], 1)
                    for u in both:
                        dve.wait_ge(top_mm[u], 2 * (2 * c + i) + 2)
                        for side in range(2):
                            last = nc.vector.tensor_reduce(
                                top[:, u, side, 0:n], bank[u][side][:, 0:width].rearrange("p (k q) -> p k q", k=n),
                                AX_X, ALU.max)
                    chain.link(last)
                    tops, small = top[:, :, :, 0:n], tiny[:, :, 0:n]
                    ratios, roots = ratio[:, :, 0:n], root[:, :, 0:n]
                    chain.link(nc.vector.tensor_scalar(tops, tops, Q_EPS, None, ALU.max))
                    chain.link(nc.vector.reciprocal(small, top[:, :, 1, 0:n]))
                    chain.link(nc.vector.tensor_tensor(ratios, top[:, :, 0, 0:n], small, ALU.mult))
                    inverse_root(nc, chain, ratios, roots, small)
                    chain.link(nc.vector.tensor_tensor(small, ratios, roots, ALU.mult))
                    chain.link(nc.vector.tensor_scalar(factor[:, :, 1, 0:n], small, Q_EPS, None, ALU.max))
                    nc.vector.reciprocal(factor[:, :, 0, 0:n], factor[:, :, 1, 0:n]).then_inc(factor_ready, 1)

                    def steps(u, side):
                        data = w if side else hidden
                        chain.link(nc.vector.tensor_reduce(rowmax[:, u, side, :], data[:, u, :, 0:width], AX_X, ALU.max,
                                                           apply_absolute_value=True))
                        chain.link(nc.vector.tensor_scalar(step[:, u, side, :], rowmax[:, u, side, :], Q_EPS,
                                                           1.0 / QMAX, ALU.max, ALU.mult))
                        nc.vector.reciprocal(per[:, u, side, :], step[:, u, side, :]).then_inc(per_ready[u], 1)

                    def clamp(u, side):
                        data = quant_t[:, u, side, 0:n, :]
                        dve.wait_ge(turn_read[side][u], reads_before(c, i) + n)
                        nc.vector.tensor_scalar(data, data, -QMAX, QMAX, ALU.max, ALU.min).then_inc(clamped[u], 1)

                    for u in both:
                        dve.wait_ge(spread_mm[u], 2 * (2 * c + i) + 1)
                        row = bank[u][2][:, 0:width]
                        chain.link(nc.vector.tensor_tensor(hidden[:, u, :, 0:width], source(u, i),
                                                           row.unsqueeze(1).to_broadcast([P, QB, width]), ALU.mult))
                        steps(u, 0)
                    for u in both:
                        dve.wait_ge(w_scaled[u], 2 * c + i + 1)
                        steps(u, 1)
                        dve.wait_ge(per_ready[u], 2 * (2 * c + i) + 2)
                        for t in range(QB):
                            row = w[:, u, t, 0:width]
                            last = nc.vector.tensor_scalar(row, row, per[:, u, 1, t:t + 1], ROUND, ALU.mult, ALU.add)
                        last.then_inc(w_rounded[u], 1)
                    for u in both:
                        clamp(u, 0)
                        if i == 0:
                            largest(w2, u, INNER)
                    clamp(0, 1)
                    clamp(1, 1)
                    for u in both:
                        for t in range(QB):
                            if t == 0:
                                dve.wait_ge(step_read[u], 2 * c + i + 1)
                            dve.wait_ge(qout_mm[u], 2 * QB * c + QB * i + t + 1)
                            nc.vector.scalar_tensor_tensor(hidden[:, u, t, :], bank[u][1 + t % 3][:],
                                                           step[:, u, 0, t:t + 1], w_row[:, u, :], ALU.mult,
                                                           ALU.mult).then_inc(qout_read[u], 1)
                for u in both:
                    dve.wait_ge(qout_read[u], 2 * QB * (c + 1))
                    rows = tile(u * QB + QB // 2, QB // 2)
                    last = nc.vector.tensor_tensor(rows, rows, hidden[:, u, QB // 2:, :], ALU.add)
                last.then_inc(res_added_dve, 1)
                dve.wait_ge(res_added_dve, c + 1)
                for u in both:
                    dve.wait_ge(res_added[u], c + 1)
                assert chain.n == LINKS, chain.n
            start.base = ROUNDS * LINKS
            norm_stats(nc, start, norm, lambda t: g.res[:, t, :], NT)
            normalise(NT // 2)

        @block.gpsimd
        def _(pool):
            with pool.Fori(0, ROUNDS) as c:
                for i, w, n in LINEARS:
                    width = n * P
                    for u in both:
                        pool.wait_ge(row_copied[u], 2 * c + i + 1)
                        for t in range(KD):
                            last = nc.gpsimd.tensor_tensor(w[:, u, t, :], w[:, u, t, :], w_row[:, u, 0:width], ALU.mult)
                        last.then_inc(w_scaled[u], 1)
                for u in both:
                    for t in range(QB // 2):
                        pool.wait_ge(qout_read[u], 2 * QB * c + QB + t + 1)
                        row = g.res[:, bass.ds((c * U + u) * QB + t, 1), :]
                        last = nc.gpsimd.tensor_tensor(row, row, hidden[:, u, t:t + 1, :], ALU.add)
                    last.then_inc(res_added[u], 1)

        @block.tensor
        def _(pe):
            def spread(out, column, n):
                for k in range(n):
                    last = nc.tensor.transpose(out[:, k * P:(k + 1) * P], column[:, k:k + 1].to_broadcast([P, P]),
                                               g.ident[:])
                return last

            with pe.Fori(0, ROUNDS) as c:
                for i, w, n in LINEARS:
                    width = n * P
                    for u in both:
                        pe.wait_ge(amax_ready[u], 2 * (2 * c + i) + 2)
                        for side in range(2):
                            for k in range(n):
                                last = nc.tensor.transpose(bank[u][side][:, k * P:(k + 1) * P],
                                                           amax[:, u, side, k * P:(k + 1) * P], g.ident[:])
                            last.then_inc(top_mm[u], 1)
                    pe.wait_ge(factor_ready, 2 * c + i + 1)
                    for side in range(2):
                        for u in both:
                            spread(bank[u][2 + side], factor[:, u, side], n).then_inc(spread_mm[u], 1)
                    for side in range(2):
                        data = w if side else hidden
                        for u in both:
                            pe.wait_ge((w_rounded if side else x_rounded)[u], 2 * c + i + 1)
                            for k in range(n):
                                if side:
                                    pe.wait_ge(turn_read[0][u], reads_before(c, i) + k + 1)
                                for t in range(QB):
                                    last = nc.tensor.transpose(bank[u][k][:, t * P:(t + 1) * P],
                                                               data[:, u, t, k * P:(k + 1) * P], g.ident[:])
                                last.then_inc(qturn_mm[u], 1)
                    for u in both:
                        pe.wait_ge(per_ready[u], 2 * (2 * c + i) + 2)
                        pe.wait_ge(turn_read[1][u], reads_before(c, i) + 1)
                        spread(bank[u][0], step[:, u, 1], KD).then_inc(step_mm[u], 1)
                    for u in both:
                        for t in range(QB):
                            if t == 0:
                                pe.wait_ge(clamped[u], 2 * (2 * c + i) + 2)
                            if t == 3:
                                pe.wait_ge(qout_read[u], 2 * QB * c + QB * i + 1)
                            for k in range(n):
                                last = nc.tensor.matmul(bank[u][1 + t % 3][:], quant_t[:, u, 0, k, t * P:(t + 1) * P],
                                                        quant_t[:, u, 1, k, :], start=k == 0, stop=k == n - 1)
                            last.then_inc(qout_mm[u], 1)


def expert_phase(nc, g, io):
    lower, upper, centre = 0.5 - float(np.log(4.0 / 3.0)), 0.5, 1.0 / float(np.e)
    with ExitStack() as stack:
        m = Space(nc, stack)
        x_hi = m.sb("xt_hi", [P, KD, NT * P], F32R)
        x_lo = m.sb("xt_lo", [P, KD, NT * P], F32R)
        raw = g.raw
        w_hi = [m.sb(f"hi_{k}", [P, KD, FF], F32R) for k in ("gate", "up", "down")]
        w_lo = [m.sb(f"lo_{k}", [P, KD, FF], F32R) for k in ("gate", "up", "down")]
        h_hi = m.sb("h_hi", [P, KF, S], F32R)
        h_lo = m.sb("h_lo", [P, KF, S], F32R)
        silu = m.sb("silu", [P, S])
        h = m.sb("h", [P, S])
        wr = m.sb("router", [P, KD, E])
        wr_parts = m.sb("router_parts", [P, KD, 2 * E], F32R)
        logits = m.sb("logits", [2 * E, NT * P])
        scaled = m.sb("scaled_logits", [P, NT, 2 * E])
        temp = m.sb("temperature", [P, 1])
        weight = m.sb("weight", [P, NT, E])
        r = [m.sb(f"route{i}", [P, NT, E]) for i in range(5)]
        ahead = m.sb("ahead", [P, NT, E, E])
        rs = [m.sb(f"route_sum{i}", [P, NT]) for i in range(3)]
        norm = norm_space(m, "norm_out", QB)
        gate = m.banks("gate_bank", 2)
        up = m.banks("up_bank", 2)
        down = m.banks("down_bank", QB)
        logit_banks = gate + up

        w_in = g.expert_in
        router_in = m.sem("router_in")
        w_hi_ready = m.sem("w_hi_ready")
        w_ready = m.sem("w_ready")
        xturn_mm = m.sem("xturn_mm")
        xturn_hi = m.sem("xturn_hi")
        xturn_lo = m.sem("xturn_lo")
        logit_mm = m.sem("logit_mm")
        logits_out = m.sem("logits_out")
        logit_turned = m.sem("logit_turned")
        logit_scaled = m.sem("logit_scaled")
        exp_ready = m.sem("exp_ready")
        near_ready = m.sem("near_ready")
        gate_up_mm = m.sem("gate_up_mm")
        silu_ready = m.sem("silu_ready")
        h_ready = m.sem("h_ready")
        h_hi_ready = m.sem("h_hi_ready")
        h_split = m.sem("h_split")
        down_mm = m.sem("down_mm")
        down_added = m.sem("down_added")
        normed = m.sem("normed2")
        out_done = m.sem("out_done")
        dve_step = m.sem("expert_dve_step")
        block = stack.enter_context(nc.Block())
        SPLITS = 2 * KF + 1

        def split_slices():
            for f in range(KF):
                for which in (0, 1):
                    yield which, slice(f * P, (f + 1) * P)
            yield 2, slice(0, D)

        @block.sync
        def _(sp):
            views = [io[k].rearrange("e (k p) n -> e p k n", p=P) for k in ("w_g", "w_u", "w_d")]
            sp.dma_start(wr[:], io["w_router"].rearrange("(k p) e -> p k e", p=P)).then_inc(router_in, 16)
            sp.dma_start(temp[:], io["temperature"].partition_broadcast(P)).then_inc(router_in, 16)
            with sp.Fori(1, E) as e:
                sp.wait_ge(w_ready, SPLITS * e - 1)
                for i in range(2):
                    sp.dma_start(raw[i][:], views[i][bass.ts(e, 1)].rearrange("e p k n -> (e p) k n")).then_inc(w_in[i], 16)
                sp.wait_ge(w_ready, SPLITS * e)
                sp.dma_start(raw[2][:], views[2][bass.ts(e, 1)].rearrange("e p k n -> (e p) k n")).then_inc(w_in[2], 16)
            out = io["out"].rearrange("b (t p) n -> p (b t) n", p=P)
            for n in range(NT // 2):
                sp.wait_ge(normed, n + 1)
                pair = slice(2 * n, 2 * n + 2)
                sp.dma_start(out[:, pair, :], g.res[:, pair, :]).then_inc(out_done, 16)
            sp.wait_ge(out_done, 16 * NT // 2)

        @block.tensor
        def _(pe):
            def turn_tiles(b):
                for t in range(b * QB, (b + 1) * QB):
                    bank = down[t % QB]
                    if t >= QB:
                        pe.wait_ge(xturn_lo, t - QB + 1)
                    for k in range(KD):
                        last = nc.tensor.transpose(bank[:, k * P:(k + 1) * P], g.res[:, t, k * P:(k + 1) * P], g.ident[:])
                    last.then_inc(xturn_mm, 1)

            turn_tiles(0)
            pe.wait_ge(h_ready, 2)
            for b in range(B):
                if b + 1 < B:
                    turn_tiles(b + 1)
                pe.wait_ge(xturn_lo, QB * (b + 1))
                tokens = slice(b * S, (b + 1) * S)
                for k in range(KD):
                    for x in (x_hi, x_lo):
                        last = nc.tensor.matmul(logit_banks[b][0:2 * E, :], wr_parts[:, k, :], x[:, k, tokens],
                                                start=k == 0 and x is x_hi, stop=k == KD - 1 and x is x_lo)
                last.then_inc(logit_mm, 1)
            pe.wait_ge(logits_out, B)
            for t in range(NT):
                last = nc.tensor.transpose(down[0][:, t * S // NT:t * S // NT + 2 * E], logits[:, t * P:(t + 1) * P],
                                           g.ident[0:2 * E, 0:2 * E])
            last.then_inc(logit_turned, 1)
            with pe.Fori(0, E) as e:
                for b in range(B):
                    turn = B * e + b
                    tokens = slice(b * S, (b + 1) * S)
                    for f in range(KF):
                        n = KF * turn + f
                        if b == 0:
                            pe.wait_ge(w_ready, SPLITS * e + 2 * f + 2)
                        pe.wait_ge(h_ready, n - 1 + 2)
                        for which, bank in ((0, gate[f % 2]), (1, up[f % 2])):
                            for k in range(KD):
                                cols = slice(f * P, (f + 1) * P)
                                last = split_matmul(nc, bank[:], w_hi[which][:, k, cols], w_lo[which][:, k, cols],
                                                    x_hi[:, k, tokens], x_lo[:, k, tokens], k == 0, k == KD - 1)
                        last.then_inc(gate_up_mm, 1)
                    if b == 0:
                        pe.wait_ge(w_ready, SPLITS * (e + 1))
                    for part in (range(KF - 1), range(KF - 1, KF)):
                        pe.wait_ge(h_split, KF * turn + part[-1] + 1)
                        for t in range(QB):
                            for f in part:
                                last = split_matmul(nc, down[t][:], h_hi[:, f, t * P:(t + 1) * P],
                                                    h_lo[:, f, t * P:(t + 1) * P], w_hi[2][:, f, :], w_lo[2][:, f, :],
                                                    f == 0, f == KF - 1)
                            if part[-1] == KF - 1:
                                last.then_inc(down_mm, 1)

        @block.scalar
        def _(act):
            for t in range(NT):
                act.wait_ge(xturn_mm, t + 1)
                nc.scalar.activation(x_hi[:, :, t * P:(t + 1) * P],
                                     down[t % QB][:].rearrange("p (k n) -> p k n", k=KD), ACT.Copy).then_inc(xturn_hi, 1)
            def split(e, after, slices=range(SPLITS)):
                for i, (which, cols) in enumerate(split_slices()):
                    if i not in slices:
                        continue
                    if i < 2:
                        act.wait_ge(w_in[which], 16 * (e + 1))
                    elif which == 2:
                        act.wait_ge(w_in[2], 16 * (e + 1))
                    if after is not None:
                        if which == 2:
                            act.wait_ge(down_mm, B * QB * e)
                        elif which == 0:
                            act.wait_ge(gate_up_mm, B * KF * e - KF + i // 2 + 1)
                    nc.scalar.activation(w_hi[which][:, :, cols], raw[which][:, :, cols],
                                         ACT.Copy).then_inc(w_hi_ready, 1)

            def silus(e, b):
                for f in range(KF):
                    n = KF * (B * e + b) + f
                    act.wait_ge(gate_up_mm, n + 1)
                    act.wait_ge(h_ready, n + 2)
                    nc.scalar.activation(silu[:], gate[f % 2][:], ACT.Silu).then_inc(silu_ready, 1)
                    act.wait_ge(h_ready, n + 3)
                    nc.scalar.activation(h_hi[:, f, :], h[:], ACT.Copy).then_inc(h_hi_ready, 1)

            split(0, None, range(2))
            for b in range(B):
                act.wait_ge(logit_mm, b + 1)
                nc.scalar.activation(logits[:, b * S:(b + 1) * S], logit_banks[b][0:2 * E, :], ACT.Copy).then_inc(logits_out, 1)
            split(0, None, range(2, 6))
            act.wait_ge(logit_scaled, 1)
            nc.scalar.activation(r[1][:], r[0][:], ACT.Exp, scale=-1.0).then_inc(exp_ready, 1)
            act.wait_ge(near_ready, 1)
            nc.scalar.activation(r[1][:], r[0][:], ACT.Exp, scale=-1.0 / 0.1)
            nc.scalar.activation(r[2][:], r[0][:], ACT.Exp, scale=-1.0 / 0.3).then_inc(exp_ready, 1)
            split(0, None, range(6, SPLITS))

            with act.Fori(0, E - 1) as e:
                for b in range(B):
                    silus(e, b)
                split(e + 1, True)
            for b in range(B):
                silus(E - 1, b)

        @block.vector
        def _(dve):
            chain = Chain(dve, dve_step)
            dve.wait_ge(router_in, 32)
            nc.vector.tensor_copy(wr_parts[:, :, 0:E], wr[:]).then_inc(h_ready, 1)
            dve.wait_ge(h_ready, 1)
            nc.vector.tensor_tensor(wr_parts[:, :, E:], wr[:], wr_parts[:, :, 0:E].bitcast(F32),
                                    ALU.subtract).then_inc(h_ready, 1)
            chain.link(nc.vector.reciprocal(temp[:], temp[:]))
            for t in range(NT):
                dve.wait_ge(xturn_hi, t + 1)
                tile = slice(t * P, (t + 1) * P)
                nc.vector.tensor_tensor(x_lo[:, :, tile], down[t % QB][:].rearrange("p (k n) -> p k n", k=KD),
                                        x_hi[:, :, tile].bitcast(F32), ALU.subtract).then_inc(xturn_lo, 1)

            dve.wait_ge(logit_turned, 1)
            chain.link(nc.vector.tensor_scalar(scaled[:], down[0][:].rearrange("p (t e) -> p t e", t=NT)[:, :, 0:2 * E],
                                               temp[:, 0:1], None, ALU.mult))
            nc.vector.tensor_tensor(r[0][:], scaled[:, :, 0:E], scaled[:, :, E:], ALU.add).then_inc(logit_scaled, 1)
            dve.wait_ge(exp_ready, 1)
            chain.link(nc.vector.tensor_scalar(r[1][:], r[1][:], 1.0, None, ALU.add))
            chain.link(nc.vector.reciprocal(r[2][:], r[1][:]))
            inside, zone, near = r[2], r[3], r[0]
            chain.link(nc.vector.tensor_scalar(zone[:], inside[:], lower, None, ALU.is_ge))
            chain.link(nc.vector.scalar_tensor_tensor(zone[:], inside[:], upper, zone[:], ALU.is_le, ALU.mult))
            chain.link(nc.vector.tensor_scalar(r[4][:], inside[:], centre, None, ALU.subtract))
            nc.vector.scalar_tensor_tensor(near[:], r[4][:], -1.0, r[4][:], ALU.mult, ALU.max).then_inc(near_ready, 1)
            wide, fallback, rank, none = r[1], r[2], r[3], rs[2]

            def row_scale(values, total):
                chain.link(nc.vector.tensor_scalar(rs[1][:], total[:], 1e-8, None, ALU.max))
                chain.link(nc.vector.reciprocal(rs[1][:], rs[1][:]))
                chain.link(nc.vector.tensor_tensor(values[:], values[:],
                                                   rs[1][:].unsqueeze(2).to_broadcast([P, NT, E]), ALU.mult))

            def rank_experts():
                dve.wait_ge(exp_ready, 2)
                nc.vector.tensor_tensor(weight[:], wide[:], zone[:], ALU.mult)
                one = lambda e, n: fallback[:, :, e:e + 1].to_broadcast([P, NT, n])
                for e in range(E):
                    nc.vector.tensor_tensor(ahead[:, :, e, e:], fallback[:, :, e:], one(e, E - e), ALU.is_gt)
                    if e:
                        nc.vector.tensor_tensor(ahead[:, :, e, 0:e], fallback[:, :, 0:e], one(e, e), ALU.is_ge)
                chain.link(nc.vector.memset(rs[0][:], 0.0))
                chain.link(nc.vector.tensor_reduce(rank[:], ahead[:], AX_X, ALU.add))
                chain.link(nc.vector.tensor_scalar(rank[:], rank[:], 1.5, None, ALU.is_le))

            def weigh_fallback():
                chain.link(nc.vector.tensor_tensor(fallback[:], fallback[:], rank[:], ALU.mult))
                chain.link(nc.vector.tensor_reduce(rs[0][:], fallback[:], AX_X, ALU.add))
                row_scale(fallback, rs[0])

            def choose_weights():
                chain.link(nc.vector.tensor_reduce(rs[0][:], weight[:], AX_X, ALU.add))
                chain.link(nc.vector.tensor_scalar(none[:], rs[0][:], 1e-8, None, ALU.is_lt))
                chain.link(nc.vector.tensor_tensor(fallback[:], fallback[:],
                                                   none[:].unsqueeze(2).to_broadcast([P, NT, E]), ALU.mult))
                chain.link(nc.vector.tensor_scalar(none[:], none[:], -1.0, 1.0, ALU.mult, ALU.add))
                chain.link(nc.vector.tensor_tensor(weight[:], weight[:],
                                                   none[:].unsqueeze(2).to_broadcast([P, NT, E]), ALU.mult))
                chain.link(nc.vector.tensor_tensor(weight[:], weight[:], fallback[:], ALU.add))
                chain.link(nc.vector.tensor_reduce(rs[0][:], weight[:], AX_X, ALU.add))
                row_scale(weight, rs[0])

            router_steps = (rank_experts, weigh_fallback, choose_weights)

            def batches(e, first_expert=False, last_expert=False):
                for b in range(B):
                    turn = B * e + b
                    for f in range(KF):
                        n = KF * turn + f
                        dve.wait_ge(silu_ready, n + 1)
                        nc.vector.tensor_tensor(h[:], up[f % 2][:], silu[:], ALU.mult).then_inc(h_ready, 1)
                        dve.wait_ge(h_hi_ready, n + 1)
                        nc.vector.tensor_tensor(h_lo[:, f, :], h[:], h_hi[:, f, :].bitcast(F32),
                                                ALU.subtract).then_inc(h_split, 1)
                        dve.wait_ge(h_split, n + 1)
                        if first_expert and b == 0 and f < len(router_steps):
                            router_steps[f]()
                    for t in range(QB):
                        tile = b * QB + t
                        dve.wait_ge(down_mm, QB * turn + t + 1)
                        row = g.res[:, tile, :]
                        nc.vector.scalar_tensor_tensor(row, down[t][:], weight[:, tile, bass.ds(e, 1)], row,
                                                       ALU.mult, ALU.add).then_inc(down_added, 1)
                        if last_expert:
                            dve.wait_ge(down_added, QB * turn + t + 1)
                            last = nc.vector.bn_stats(norm[0][:, t, :], g.res[:, tile, :])
                    if last_expert:
                        chain.link(last)
                        rows = lambda t: g.res[:, b * QB + t, :]
                        norm_factors(nc, chain, norm, QB)
                        for half in range(2):
                            norm_apply(nc, norm, rows, range(2 * half, 2 * half + 2)).then_inc(normed, 1)
                        dve.wait_ge(normed, 2 * (b + 1))

            batches(0, first_expert=True)
            with dve.Fori(1, E - 1) as e:
                batches(e)
            batches(E - 1, last_expert=True)

        @block.gpsimd
        def _(pool):
            def split(e):
                for i, (which, cols) in enumerate(split_slices()):
                    for k in range(KD):
                        pool.wait_ge(w_hi_ready, SPLITS * e + i + 1)
                        last = nc.gpsimd.tensor_tensor(w_lo[which][:, k, cols], raw[which][:, k, cols],
                                                       w_hi[which][:, k, cols].bitcast(F32), ALU.subtract)
                    last.then_inc(w_ready, 1)

            with pool.Fori(0, E) as e:
                split(e)


def build(nc, io):
    with ExitStack() as stack:
        m = Space(nc, stack)

        class g:
            res = m.sb("res", [P, NT, D])
            ident = m.sb("ident", [P, P])
            ident_b = m.sb("ident_b", [P, P], BF16)
            mask = m.sb("mask", [P, P], BF16)
            stats = m.sb("res_stats", [P, NT, 6])

        with ExitStack() as inner:
            a = Space(nc, inner)
            g.cos = a.sb("cos", [P, S])
            g.sin = a.sb("sin", [P, S])
            g.q_gain = a.sb("q_gain", [P, KQ])
            g.raw_q = a.sb("raw_q", [P, 2, QL])
            g.raw_k = a.sb("raw_k", [P, 2, KL])
            g.raw_r = a.sb("raw_r", [P, KQ, P])
            g.fold_in, g.rope_in = a.sem("fold_in"), a.sem("rope_in")
            g.qn_hi = a.sb("qn_hi", [P, KQ, B * S], F32R)
            g.qn_lo = a.sb("qn_lo", [P, KQ, B * S], F32R)
            g.key_hi = a.sb("key_hi", [P, B * S], F32R)
            g.key_lo = a.sb("key_lo", [P, B * S], F32R)
            g.kr_hi = a.sb("kr_hi", [P, B * S], F32R)
            g.kr_lo = a.sb("kr_lo", [P, B * S], F32R)
            g.val_hi = a.sb("val_hi", [P, NT, KL], F32R)
            g.val_lo = a.sb("val_lo", [P, NT, KL], F32R)
            latent_phase(nc, g, io)
            attention_phase(nc, g, io)
        g.raw = [m.sb(f"raw_{k}", [P, KD, FF]) for k in ("gate", "up", "down")]
        g.expert_in = [m.sem(f"{k}_in") for k in ("gate", "up", "down")]
        quant_phase(nc, g, io)
        expert_phase(nc, g, io)


def rotary_order():
    half = ROPE // 2
    return np.concatenate([np.r_[q * 16:q * 16 + 16, half + q * 16:half + q * 16 + 16] for q in range(2)])


def shape_constants():
    order = rotary_order()
    inv_freq = (1.0 / np.float32(10000.0) ** (np.arange(0, ROPE, 2, dtype=np.float32) / np.float32(ROPE)))
    angle = np.outer(np.arange(S, dtype=np.float32), inv_freq.astype(np.float32)).astype(np.float32)
    angle = np.concatenate([angle, angle], -1)[:, order].T
    sign = np.where(order < ROPE // 2, -1.0, 1.0).astype(np.float32)[:, None]
    cos, sin = np.cos(angle), np.sin(angle) * sign
    mask = np.where(np.tril(np.ones((P, P), bool)), 0.0, MASKED)
    return {
        "cos": np.concatenate([cos, cos], 0).astype(np.float32),
        "sin": np.concatenate([sin, sin], 0).astype(np.float32),
        "mask": mask.astype(np.float32),
        "ident": np.eye(P, dtype=np.float32),
    }


def lay_out(inputs):
    a = {k: np.asarray(v) for k, v in inputs.items()}
    order = rotary_order()
    x = a["x"]
    wq = a["L0_attn_q_b_w"].reshape(H, NOPE + ROPE, QL)
    wkva = a["L0_attn_kv_a_w"]
    w_kr = wkva[KL:][order].T
    arrays = {
        "x": x,
        "x_t": x.transpose(0, 2, 1),
        "w_a": np.concatenate([a["L0_attn_q_a_w"], wkva[:KL]], 0).T,
        "w_kr": np.concatenate([w_kr, w_kr], 1),
        "q_ln": a["L0_attn_q_a_ln_w"].reshape(KQ, P).T,
        "kv_ln": a["L0_attn_kv_a_ln_w"],
        "wq_nope": wq[:, :NOPE],
        "wq_rope_t": wq[:, NOPE:][:, order].reshape(H * ROPE, QL).T,
        "w_kv": a["L0_attn_kv_b_w"].reshape(H, NOPE + VD, KL),
        "w_o_t": a["L0_attn_o_w"].T,
        "w_gate_up": a["fside_BxS2xS2_0"],
        "w_down": a["ctx_1024"],
        "w_g": a["L0_ffn_Wg"],
        "w_u": a["L0_ffn_Wu"],
        "w_d": a["L0_ffn_Wd"],
        "w_router": a["L0_ffn_Wr"],
        "temperature": a["L0_ffn_temperature"],
    }
    return {k: np.ascontiguousarray(v) for k, v in {**arrays, **shape_constants()}.items()}


def kernel(**inputs):
    import concourse.bacc as bacc
    from concourse.bass_utils import run_bass_kernel_spmd

    nc = bacc.Bacc("TRN2", target_bir_lowering=False, num_devices=1)
    arrays = lay_out(inputs)
    io = {k: nc.dram_tensor(f"in_{k}", v.shape, mybir.dt.from_np(v.dtype), kind="ExternalInput").ap()
          for k, v in arrays.items()}
    io["out"] = nc.dram_tensor("out_y", (B, S, D), F32, kind="ExternalOutput").ap()
    build(nc, io)
    result = run_bass_kernel_spmd(nc, [{f"in_{k}": v for k, v in arrays.items()}], core_ids=[0])
    return result.results[0]["out_y"]
```
